# Optimizing a Trainium2 kernel written in Bass

```python
import numpy as np
import jax
import jax.numpy as jnp

def _softmax(x, axis=-1):
    return jax.nn.softmax(x, axis=axis)

def _gelu(x):
    return jax.nn.gelu(x, approximate=True)

def _silu(x):
    return jax.nn.silu(x)

def _sigmoid(x):
    return jax.nn.sigmoid(x)

def _layernorm(x, axis=-1, eps=1e-05):
    m = jnp.mean(x, axis=axis, keepdims=True)
    v = jnp.var(x, axis=axis, keepdims=True)
    return (x - m) / jnp.sqrt(v + eps)

def _scatter_add(tgt, idx, src, axis=0):
    return tgt.at[idx].add(src)

def _segment_sum(src, seg, n):
    return jax.ops.segment_sum(src, seg, n)
kernel_name = 'mk_decoder_postln_d2_seqx_r8_9ed643'

def setup_inputs(seed: int=0):
    np.random.seed(seed)
    _w = jnp.asarray

    def _rec_inputs():
        import jax
        import jax.numpy as jnp
        _rk = jax.random.key(seed)
        x = 7.22e-05 + 1 * jax.random.normal(jax.random.fold_in(_rk, 1), (4, 512, 128), jnp.float32)
        _lenS = 512 - jax.random.randint(jax.random.fold_in(_rk, 7), (4,), 0, max(1, 512 // 4) + 1, jnp.int32)
        _lenS2 = 77 - jax.random.randint(jax.random.fold_in(_rk, 8), (4,), 0, max(1, 77 // 4) + 1, jnp.int32)
        _ctx_1024P = jax.random.normal(jax.random.fold_in(_rk, 11), (4, 16, 128), jnp.float32)
        _ctx_1024c = jax.random.dirichlet(jax.random.fold_in(_rk, 511), 0.3 * jnp.ones((16,), jnp.float32), (4, 77))
        _ctx_1024t = jnp.einsum('bsk,bkd->bsd', _ctx_1024c, _ctx_1024P)
        _ctx_1024t = _ctx_1024t * jax.lax.rsqrt(jnp.mean(jnp.square(_ctx_1024t)) + 1e-12) * 0.953939
        ctx_1024 = 4.13588e-05 + 0.999923 * (_ctx_1024t + 0.3 * jax.random.normal(jax.random.fold_in(_rk, 611), (4, 77, 128), jnp.float32))
        _validS = jnp.arange(512)[None, :] < _lenS[:, None]
        _validS2 = jnp.arange(77)[None, :] < _lenS2[:, None]
        _causal = jnp.tril(jnp.ones((512, 512), dtype=bool))
        mask_BxSxS2_ik1 = jnp.where(jnp.broadcast_to(_validS2[:, None, :], (4, 512, 77)), 1, 0).astype(jnp.int32)
        return (x, ctx_1024, mask_BxSxS2_ik1)
    x, ctx_1024, mask_BxSxS2_ik1 = _rec_inputs()

    def _L0_attn_setup():
        import jax, jax.numpy as jnp
        import numpy as np
        D = 128
        FW = 64
        DEPTH = 2
        E = D * (DEPTH + 1)
        B, L = (2, 512)

        def _fftconv(x_bdl, h, bias_d):
            Lq = x_bdl.shape[-1]
            n = 2 * Lq
            Xf = jnp.fft.rfft(x_bdl, n=n)
            Hf = jnp.fft.rfft(h, n=n) / n
            y = jnp.fft.irfft(Xf * Hf, n=n, norm='forward')[..., :Lq]
            return y + x_bdl * bias_d[:, None]
        key = jax.random.key(seed)
        ks = jax.random.split(key, 12)
        s = lambda k, shape, scale: jax.random.normal(k, shape, dtype=jnp.float32) * scale
        return {'x': jax.random.normal(ks[0], (B, L, D), dtype=jnp.float32), 'w_in': s(ks[1], (D, E), 0.02), 'b_in': jnp.zeros((E,), jnp.float32), 'w_conv': s(ks[2], (E, 1, 3), 0.5), 'b_conv': jnp.zeros((E,), jnp.float32), 'w1': s(ks[3], (3, FW), 0.5), 'b1': jnp.zeros((FW,), jnp.float32), 'w2': s(ks[4], (FW, FW), 0.1), 'b2': jnp.zeros((FW,), jnp.float32), 'w3': s(ks[5], (FW, D), 0.1), 'filt_bias': jax.random.normal(ks[6], (D,), dtype=jnp.float32), 'w_out': s(ks[7], (D, D), 0.02), 'b_out': jnp.zeros((D,), jnp.float32)}
    _L0_attn_all = _L0_attn_setup()
    _L0_attn_in = {k: v for k, v in _L0_attn_all.items() if k in ('w_in', 'b_in', 'w_conv', 'b_conv', 'w1', 'b1', 'w2', 'b2', 'w3', 'filt_bias', 'w_out', 'b_out')}
    del _L0_attn_all

    def _L0_xattn_setup():
        import jax, jax.numpy as jnp
        import numpy as np
        NEG = -9000000000000000.0
        EPS = 1e-05
        key = jax.random.key(seed)
        k1, k2, k3, k4 = jax.random.split(key, 4)
        B, S, D = (4, 256, 128)
        q = jax.random.normal(k1, (B, S, D), dtype=jnp.float32)
        k = jax.random.normal(k2, (B, S, D), dtype=jnp.float32)
        v = jax.random.normal(k3, (B, S, D), dtype=jnp.float32)
        mask = jax.random.randint(k4, (B, S, S), 0, 2, dtype=jnp.int32)
        gamma = jnp.ones((D,), dtype=jnp.float32)
        beta = jnp.zeros((D,), dtype=jnp.float32)
        return {'q': q, 'k': k, 'v': v, 'mask': mask, 'gamma': gamma, 'beta': beta}
    _L0_xattn_all = _L0_xattn_setup()
    _L0_xattn_in = {k: v for k, v in _L0_xattn_all.items() if k in ('gamma', 'beta')}
    del _L0_xattn_all

    def _L0_ffn_setup():
        import jax, jax.numpy as jnp
        import numpy as np
        EPS = 1e-05

        def rmsnorm(x):
            var = jnp.mean(jnp.square(x), axis=-1, keepdims=True)
            return x * jax.lax.rsqrt(var + 1e-06)

        def activation_quant(x):
            scale = 127.0 / jnp.clip(jnp.max(jnp.abs(x), axis=-1, keepdims=True), EPS, None)
            return jnp.clip(jnp.round(x * scale), -128, 127) / scale

        def weight_quant(w):
            scale = 1.0 / jnp.clip(jnp.mean(jnp.abs(w)), EPS, None)
            return jnp.clip(jnp.round(w * scale), -1, 1) / scale

        def bitlinear(x, w, b):
            xn = rmsnorm(x)
            xq = xn + jax.lax.stop_gradient(activation_quant(xn) - xn)
            wq = w + jax.lax.stop_gradient(weight_quant(w) - w)
            return jnp.einsum('bsi,oi->bso', xq, wq) + b
        key = jax.random.key(seed)
        k1, k2, k3 = jax.random.split(key, 3)
        B, S, D, H = (4, 256, 128, 512)
        x = jax.random.normal(k1, (B, S, D), dtype=jnp.float32)
        w1 = jax.random.normal(k2, (H, D), dtype=jnp.float32) * D ** (-0.5)
        b1 = jnp.zeros((H,), dtype=jnp.float32)
        w2 = jax.random.normal(k3, (D, H), dtype=jnp.float32) * H ** (-0.5)
        b2 = jnp.zeros((D,), dtype=jnp.float32)
        return {'x': x, 'w1': w1, 'b1': b1, 'w2': w2, 'b2': b2}
    _L0_ffn_all = _L0_ffn_setup()
    _L0_ffn_in = {k: v for k, v in _L0_ffn_all.items() if k in ('w1', 'b1', 'w2', 'b2')}
    del _L0_ffn_all

    def _L1_attn_setup():
        import jax, jax.numpy as jnp
        import numpy as np
        key = jax.random.key(seed)
        B, L, d_model, d_state, expand = (2, 256, 128, 16, 2)
        d_inner = expand * d_model
        ks = jax.random.split(key, 8)
        s = lambda k, shape, scale: jax.random.normal(k, shape, dtype=jnp.float32) * scale
        x = s(ks[0], (B, L, d_model), 1.0)
        W_in = s(ks[1], (d_model, 2 * d_inner), 0.02)
        W_delta = s(ks[2], (d_inner, d_inner), 0.02)
        b_delta = s(ks[3], (d_inner,), 0.02)
        W_B = s(ks[4], (d_inner, d_state), 0.02)
        W_C = s(ks[5], (d_inner, d_state), 0.02)
        A_log = jnp.log(jnp.broadcast_to(jnp.arange(1, d_state + 1, dtype=jnp.float32), (d_inner, d_state)))
        D_param = jnp.ones((d_inner,), dtype=jnp.float32)
        W_out = s(ks[6], (d_inner, d_model), 0.02)
        return dict(x=x, W_in=W_in, W_delta=W_delta, b_delta=b_delta, W_B=W_B, W_C=W_C, A_log=A_log, D_param=D_param, W_out=W_out)
    _L1_attn_all = _L1_attn_setup()
    _L1_attn_in = {k: v for k, v in _L1_attn_all.items() if k in ('W_in', 'W_delta', 'b_delta', 'W_B', 'W_C', 'A_log', 'D_param', 'W_out')}
    del _L1_attn_all

    def _L1_xattn_setup():
        import jax, jax.numpy as jnp
        import numpy as np
        EPS = 1e-06

        def _rmsnorm(x, scale):
            var = jnp.mean(jnp.square(x), axis=-1, keepdims=True)
            return x * jax.lax.rsqrt(var + EPS) * scale
        key = jax.random.key(seed)
        ks = jax.random.split(key, 6)
        B, S, D, H, Hd = (2, 256, 128, 16, 64)
        sc = 1.0 / np.sqrt(D)
        return {'inputs_q': jax.random.normal(ks[0], (B, S, D), jnp.float32), 'inputs_kv': jax.random.normal(ks[1], (B, S, D), jnp.float32), 'Wq': jax.random.normal(ks[2], (D, H, Hd), jnp.float32) * sc, 'Wk': jax.random.normal(ks[3], (D, H, Hd), jnp.float32) * sc, 'Wv': jax.random.normal(ks[4], (D, H, Hd), jnp.float32) * sc, 'Wo': jax.random.normal(ks[5], (H, Hd, D), jnp.float32) * (1.0 / np.sqrt(D)), 'bo': jnp.zeros((D,), jnp.float32), 'gq': jnp.ones((Hd,), jnp.float32), 'gk': jnp.ones((Hd,), jnp.float32)}
    _L1_xattn_all = _L1_xattn_setup()
    _L1_xattn_in = {k: v for k, v in _L1_xattn_all.items() if k in ('Wq', 'Wk', 'Wv', 'Wo', 'bo', 'gq', 'gk')}
    del _L1_xattn_all

    def _L1_ffn_setup():
        import jax, jax.numpy as jnp
        import numpy as np
        B, T, D = (2, 128, 128)
        H, DK, K = (8, 128, 8)
        NKEYS = 32
        NEXP = NKEYS * NKEYS

        def _rmsnorm(x, w, eps=1e-06):
            inv = jax.lax.rsqrt(jnp.mean(x * x, axis=-1, keepdims=True) + eps)
            return x * inv * w
        key = jax.random.key(seed)
        ks = jax.random.split(key, 5)
        return {'x': jax.random.normal(ks[0], (B, T, D), jnp.float32), 'w_q': jax.random.normal(ks[1], (H * 2 * DK, D), jnp.float32) * 0.02, 'keys': jax.random.normal(ks[2], (H, NKEYS, 2, DK), jnp.float32) * 0.02, 'expert_down': jax.random.normal(ks[3], (NEXP, D), jnp.float32) * 0.02, 'expert_up': jax.random.normal(ks[4], (NEXP, D), jnp.float32) * 0.02, 'norm_w': jnp.ones((D,), jnp.float32)}
    _L1_ffn_all = _L1_ffn_setup()
    _L1_ffn_in = {k: v for k, v in _L1_ffn_all.items() if k in ('w_q', 'keys', 'expert_down', 'expert_up', 'norm_w')}
    del _L1_ffn_all
    return {'x': x, 'ctx_1024': ctx_1024, 'mask_BxSxS2_ik1': mask_BxSxS2_ik1, 'L0_attn_w_in': _L0_attn_in['w_in'], 'L0_attn_b_in': _L0_attn_in['b_in'], 'L0_attn_w_conv': _L0_attn_in['w_conv'], 'L0_attn_b_conv': _L0_attn_in['b_conv'], 'L0_attn_w1': _L0_attn_in['w1'], 'L0_attn_b1': _L0_attn_in['b1'], 'L0_attn_w2': _L0_attn_in['w2'], 'L0_attn_b2': _L0_attn_in['b2'], 'L0_attn_w3': _L0_attn_in['w3'], 'L0_attn_filt_bias': _L0_attn_in['filt_bias'], 'L0_attn_w_out': _L0_attn_in['w_out'], 'L0_attn_b_out': _L0_attn_in['b_out'], 'L0_xattn_gamma': _L0_xattn_in['gamma'], 'L0_xattn_beta': _L0_xattn_in['beta'], 'L0_ffn_w1': _L0_ffn_in['w1'], 'L0_ffn_b1': _L0_ffn_in['b1'], 'L0_ffn_w2': _L0_ffn_in['w2'], 'L0_ffn_b2': _L0_ffn_in['b2'], 'L1_attn_W_in': _L1_attn_in['W_in'], 'L1_attn_W_delta': _L1_attn_in['W_delta'], 'L1_attn_b_delta': _L1_attn_in['b_delta'], 'L1_attn_W_B': _L1_attn_in['W_B'], 'L1_attn_W_C': _L1_attn_in['W_C'], 'L1_attn_A_log': _L1_attn_in['A_log'], 'L1_attn_D_param': _L1_attn_in['D_param'], 'L1_attn_W_out': _L1_attn_in['W_out'], 'L1_xattn_Wq': _L1_xattn_in['Wq'], 'L1_xattn_Wk': _L1_xattn_in['Wk'], 'L1_xattn_Wv': _L1_xattn_in['Wv'], 'L1_xattn_Wo': _L1_xattn_in['Wo'], 'L1_xattn_bo': _L1_xattn_in['bo'], 'L1_xattn_gq': _L1_xattn_in['gq'], 'L1_xattn_gk': _L1_xattn_in['gk'], 'L1_ffn_w_q': _L1_ffn_in['w_q'], 'L1_ffn_keys': _L1_ffn_in['keys'], 'L1_ffn_expert_down': _L1_ffn_in['expert_down'], 'L1_ffn_expert_up': _L1_ffn_in['expert_up'], 'L1_ffn_norm_w': _L1_ffn_in['norm_w']}

def reference(x, ctx_1024, mask_BxSxS2_ik1, L0_attn_w_in, L0_attn_b_in, L0_attn_w_conv, L0_attn_b_conv, L0_attn_w1, L0_attn_b1, L0_attn_w2, L0_attn_b2, L0_attn_w3, L0_attn_filt_bias, L0_attn_w_out, L0_attn_b_out, L0_xattn_gamma, L0_xattn_beta, L0_ffn_w1, L0_ffn_b1, L0_ffn_w2, L0_ffn_b2, L1_attn_W_in, L1_attn_W_delta, L1_attn_b_delta, L1_attn_W_B, L1_attn_W_C, L1_attn_A_log, L1_attn_D_param, L1_attn_W_out, L1_xattn_Wq, L1_xattn_Wk, L1_xattn_Wv, L1_xattn_Wo, L1_xattn_bo, L1_xattn_gq, L1_xattn_gk, L1_ffn_w_q, L1_ffn_keys, L1_ffn_expert_down, L1_ffn_expert_up, L1_ffn_norm_w):
    import jax
    import jax.numpy as jnp

    def _L0_attn_ref(x, w_in, b_in, w_conv, b_conv, w1, b1, w2, b2, w3, filt_bias, w_out, b_out):
        import jax, jax.numpy as jnp
        import numpy as np
        D = 128
        FW = 64
        DEPTH = 2
        E = D * (DEPTH + 1)
        B, L = (2, 512)

        def _fftconv(x_bdl, h, bias_d):
            Lq = x_bdl.shape[-1]
            n = 2 * Lq
            Xf = jnp.fft.rfft(x_bdl, n=n)
            Hf = jnp.fft.rfft(h, n=n) / n
            y = jnp.fft.irfft(Xf * Hf, n=n, norm='forward')[..., :Lq]
            return y + x_bdl * bias_d[:, None]
        _, Lx, Dm = x.shape
        u = (x @ w_in + b_in).transpose(0, 2, 1)
        u = jax.lax.conv_general_dilated(u, w_conv, window_strides=(1,), padding=[(2, 2)], feature_group_count=u.shape[1], dimension_numbers=('NCH', 'OIH', 'NCH'))
        u = (u + b_conv[None, :, None])[..., :Lx]
        streams = [u[:, i * Dm:(i + 1) * Dm, :] for i in range(DEPTH + 1)]
        t = jnp.linspace(0.0, 1.0, Lx)
        pos = jnp.tile(t[:, None], (1, 3))
        hmlp = jax.nn.silu(pos @ w1 + b1)
        hmlp = jax.nn.silu(hmlp @ w2 + b2)
        filters = hmlp @ w3 * jnp.exp(-t[:, None] * jnp.abs(filt_bias)[None, :])
        v = streams[-1]
        for i in range(DEPTH - 1):
            v = v * streams[i]
            v = _fftconv(v, filters[i], filt_bias)
        out = (v * streams[0]).transpose(0, 2, 1) @ w_out + b_out
        return out

    def _L0_xattn_ref(q, k, v, mask, gamma, beta):
        import jax, jax.numpy as jnp
        import numpy as np
        NEG = -9000000000000000.0
        EPS = 1e-05
        d_k = q.shape[-1]
        logits = jnp.einsum('bsd,btd->bst', q, k) / jnp.sqrt(jnp.asarray(d_k, q.dtype))
        logits = jnp.where(mask == 0, jnp.asarray(NEG, logits.dtype), logits)
        attn = jax.nn.softmax(logits, axis=-1)
        x = jnp.einsum('bst,btd->bsd', attn, v)
        mu = jnp.mean(x, axis=-1, keepdims=True)
        var = jnp.mean(jnp.square(x - mu), axis=-1, keepdims=True)
        xhat = (x - mu) * jax.lax.rsqrt(var + EPS)
        return xhat * gamma + beta

    def _L0_ffn_ref(x, w1, b1, w2, b2):
        import jax, jax.numpy as jnp
        import numpy as np
        EPS = 1e-05

        def rmsnorm(x):
            var = jnp.mean(jnp.square(x), axis=-1, keepdims=True)
            return x * jax.lax.rsqrt(var + 1e-06)

        def activation_quant(x):
            scale = 127.0 / jnp.clip(jnp.max(jnp.abs(x), axis=-1, keepdims=True), EPS, None)
            return jnp.clip(jnp.round(x * scale), -128, 127) / scale

        def weight_quant(w):
            scale = 1.0 / jnp.clip(jnp.mean(jnp.abs(w)), EPS, None)
            return jnp.clip(jnp.round(w * scale), -1, 1) / scale

        def bitlinear(x, w, b):
            xn = rmsnorm(x)
            xq = xn + jax.lax.stop_gradient(activation_quant(xn) - xn)
            wq = w + jax.lax.stop_gradient(weight_quant(w) - w)
            return jnp.einsum('bsi,oi->bso', xq, wq) + b
        h = bitlinear(x, w1, b1)
        h = jax.nn.gelu(h, approximate=False)
        return bitlinear(h, w2, b2)

    def _L1_attn_ref(x, W_in, W_delta, b_delta, W_B, W_C, A_log, D_param, W_out):
        import jax, jax.numpy as jnp
        import numpy as np
        d_inner = W_delta.shape[0]
        x_and_res = x @ W_in
        u, res = (x_and_res[..., :d_inner], x_and_res[..., d_inner:])
        u = jax.nn.silu(u)
        delta = jax.nn.softplus(u @ W_delta + b_delta)
        Bm = u @ W_B
        Cm = u @ W_C
        A = -jnp.exp(A_log)

        def step(h, inp):
            d_t, B_t, C_t, u_t = inp
            dA = jnp.exp(d_t[..., None] * A)
            h = dA * h + d_t[..., None] * B_t[:, None, :] * u_t[..., None]
            y_t = jnp.einsum('bdn,bn->bd', h, C_t)
            return (h, y_t)
        Bsz = x.shape[0]
        h0 = jnp.zeros((Bsz, d_inner, A.shape[1]), dtype=x.dtype)
        xs = (jnp.swapaxes(delta, 0, 1), jnp.swapaxes(Bm, 0, 1), jnp.swapaxes(Cm, 0, 1), jnp.swapaxes(u, 0, 1))
        _, ys = jax.lax.scan(step, h0, xs)
        y = jnp.swapaxes(ys, 0, 1) + u * D_param
        y = y * jax.nn.silu(res)
        return y @ W_out

    def _L1_xattn_ref(inputs_q, inputs_kv, Wq, Wk, Wv, Wo, bo, gq, gk):
        import jax, jax.numpy as jnp
        import numpy as np
        EPS = 1e-06

        def _rmsnorm(x, scale):
            var = jnp.mean(jnp.square(x), axis=-1, keepdims=True)
            return x * jax.lax.rsqrt(var + EPS) * scale
        q = jnp.einsum('bsd,dhe->bshe', inputs_q, Wq)
        k = jnp.einsum('bsd,dhe->bshe', inputs_kv, Wk)
        v = jnp.einsum('bsd,dhe->bshe', inputs_kv, Wv)
        q = _rmsnorm(q, gq)
        k = _rmsnorm(k, gk)
        head_dim = q.shape[-1]
        scores = jnp.einsum('bqhe,bkhe->bhqk', q, k) / jnp.sqrt(jnp.asarray(head_dim, q.dtype))
        attn = jax.nn.softmax(scores, axis=-1)
        x = jnp.einsum('bhqk,bkhe->bqhe', attn, v)
        out = jnp.einsum('bqhe,hed->bqd', x, Wo) + bo
        return out

    def _L1_ffn_ref(x, w_q, keys, expert_down, expert_up, norm_w):
        import jax, jax.numpy as jnp
        import numpy as np
        B, T, D = (2, 128, 128)
        H, DK, K = (8, 128, 8)
        NKEYS = 32
        NEXP = NKEYS * NKEYS

        def _rmsnorm(x, w, eps=1e-06):
            inv = jax.lax.rsqrt(jnp.mean(x * x, axis=-1, keepdims=True) + eps)
            return x * inv * w
        b, t, d = x.shape
        xn = _rmsnorm(x, norm_w)
        q = (xn @ w_q.T).reshape(b, t, H, 2, DK)
        sim1 = jnp.einsum('bthd,hkd->bthk', q[..., 0, :], keys[:, :, 0, :])
        sim2 = jnp.einsum('bthd,hkd->bthk', q[..., 1, :], keys[:, :, 1, :])
        s1, i1 = jax.lax.top_k(sim1, K)
        s2, i2 = jax.lax.top_k(sim2, K)
        all_idx = (i1[..., :, None] * NKEYS + i2[..., None, :]).reshape(b, t, H, K * K)
        all_sc = (s1[..., :, None] + s2[..., None, :]).reshape(b, t, H, K * K)
        fs, pk = jax.lax.top_k(all_sc, K)
        fi = jnp.take_along_axis(all_idx, pk, axis=-1)
        wd = expert_down[fi]
        wu = expert_up[fi]
        hidden = jax.nn.gelu(jnp.einsum('btd,bthkd->bthk', xn, wd), approximate=False)
        hidden = hidden * jax.nn.relu(fs)
        return jnp.einsum('bthk,bthkd->btd', hidden, wu)
    x = _layernorm(x + _L0_attn_ref(x, L0_attn_w_in, L0_attn_b_in, L0_attn_w_conv, L0_attn_b_conv, L0_attn_w1, L0_attn_b1, L0_attn_w2, L0_attn_b2, L0_attn_w3, L0_attn_filt_bias, L0_attn_w_out, L0_attn_b_out), axis=-1)
    x = _layernorm(x + _L0_xattn_ref(x, ctx_1024, ctx_1024, mask_BxSxS2_ik1, L0_xattn_gamma, L0_xattn_beta), axis=-1)
    x = _layernorm(x + _L0_ffn_ref(x, L0_ffn_w1, L0_ffn_b1, L0_ffn_w2, L0_ffn_b2), axis=-1)
    x = _layernorm(x + _L1_attn_ref(x, L1_attn_W_in, L1_attn_W_delta, L1_attn_b_delta, L1_attn_W_B, L1_attn_W_C, L1_attn_A_log, L1_attn_D_param, L1_attn_W_out), axis=-1)
    x = _layernorm(x + _L1_xattn_ref(x, ctx_1024, L1_xattn_Wq, L1_xattn_Wk, L1_xattn_Wv, L1_xattn_Wo, L1_xattn_bo, L1_xattn_gq, L1_xattn_gk), axis=-1)
    x = _layernorm(x + _L1_ffn_ref(x, L1_ffn_w_q, L1_ffn_keys, L1_ffn_expert_down, L1_ffn_expert_up, L1_ffn_norm_w), axis=-1)
    return x

_drawn_inputs = setup_inputs


def setup_inputs(seed=0):
    import zlib

    import numpy as np

    out = dict(_drawn_inputs(seed))
    spreads = {'L0_attn_b_in': (0.0, 0.8),
     'L0_attn_b_conv': (0.0, 0.8),
     'L0_attn_b1': (0.0, 0.8),
     'L0_attn_b2': (0.0, 0.8),
     'L0_attn_b_out': (0.0, 0.1),
     'L0_xattn_gamma': (1.0, 0.2),
     'L0_xattn_beta': (0.0, 0.1),
     'L0_ffn_b1': (0.0, 0.1),
     'L0_ffn_b2': (0.0, 0.1),
     'L1_attn_D_param': (1.0, 0.6),
     'L1_xattn_bo': (0.0, 0.1),
     'L1_xattn_gq': (1.0, 0.2),
     'L1_xattn_gk': (1.0, 0.2),
     'L1_ffn_norm_w': (1.0, 0.6)}
    factors = {'L0_attn_w_in': 8.0,
     'L0_attn_w_conv': 8.0,
     'L0_attn_w2': 8.0,
     'L0_attn_w3': 8.0,
     'L0_attn_filt_bias': 8.0,
     'L0_attn_w_out': 8.0,
     'L1_attn_W_in': 8.0,
     'L1_attn_W_delta': 8.0,
     'L1_attn_b_delta': 8.0,
     'L1_attn_W_B': 8.0,
     'L1_attn_W_C': 8.0,
     'L1_attn_A_log': 8.0,
     'L1_attn_W_out': 8.0,
     'L1_ffn_w_q': 8.0,
     'L1_ffn_keys': 8.0,
     'L1_ffn_expert_down': 8.0,
     'L1_ffn_expert_up': 8.0}
    for name, (base, spread) in spreads.items():
        noise = np.random.default_rng([zlib.crc32(name.encode()), seed]).standard_normal(out[name].shape)
        drawn = base * np.exp(spread * noise) if base else spread * noise
        out[name] = jnp.asarray(drawn.astype(out[name].dtype))
    for name, factor in factors.items():
        out[name] = (out[name] * factor).astype(out[name].dtype)
    return out
```

```python
from contextlib import ExitStack

import numpy as np

import concourse.bass as bass
from concourse import mybir

ALU = mybir.AluOpType
ACT = mybir.ActivationFunctionType
AX = mybir.AxisListType
F32 = mybir.dt.float32
BF16 = mybir.dt.bfloat16
I32 = mybir.dt.int32

P = 128
MASKED = -9000000000000000.0
ROUND = 12582912.0


def spread(ap, axis, n):
    dims = [list(d) for d in ap.ap]
    dims.insert(axis, [0, n])
    return bass.AP(ap.tensor, ap.offset, dims)


class Signals:

    def __init__(self, eng, step=None):
        self.eng, self.step, self.steps, self.seen = eng, step, 0, {}

    def next(self, sem, n=1):
        key = sem.name if hasattr(sem, "name") else str(sem)
        self.seen[key] = self.seen.get(key, 0) + n
        self.eng.wait_ge(sem, self.seen[key])

    def link(self, instruction):
        self.steps += 1
        instruction.then_inc(self.step, 1)
        self.eng.wait_ge(self.step, self.steps)


def decoder(nc, x, ctx_1024, mask_BxSxS2_ik1, L0_attn_w_in, L0_attn_b_in, L0_attn_w_conv,
            L0_attn_b_conv, L0_attn_w1, L0_attn_b1, L0_attn_w2, L0_attn_b2, L0_attn_w3,
            L0_attn_filt_bias, L0_attn_w_out, L0_attn_b_out, L0_xattn_gamma, L0_xattn_beta,
            L0_ffn_w1, L0_ffn_b1, L0_ffn_w2, L0_ffn_b2, L1_attn_W_in, L1_attn_W_delta,
            L1_attn_b_delta, L1_attn_W_B, L1_attn_W_C, L1_attn_A_log, L1_attn_D_param,
            L1_attn_W_out, L1_xattn_Wq, L1_xattn_Wk, L1_xattn_Wv, L1_xattn_Wo, L1_xattn_bo,
            L1_xattn_gq, L1_xattn_gk, L1_ffn_w_q, L1_ffn_keys, L1_ffn_expert_down,
            L1_ffn_expert_up, L1_ffn_norm_w, out):
    B, S, D = x.shape
    C = ctx_1024.shape[1]
    NB = S // P
    FW = L0_attn_w2.shape[0]
    F = L0_ffn_w1.shape[0]
    FK = F // P
    DI = L1_attn_W_delta.shape[0]
    DJ = DI // P
    NS = L1_attn_W_B.shape[1]
    H, E = L1_xattn_Wq.shape[1:]
    HP = H * E // P
    PH, NK = L1_ffn_keys.shape[:2]
    NE = L1_ffn_expert_down.shape[0]
    EB = NE // P
    TOP = 8
    HG = 4
    NG = H // (2 * HG)
    LANES = 2
    WB = 4
    assert D == P and DJ == 2 and NE == NK * NK and 3 * 2 * NS <= P and F <= 512

    h_pad = nc.dram_tensor("h_pad", (3 * P,), F32, kind="Internal").ap()

    with ExitStack() as ctx:
        def sb(name, shape, dt=F32):
            return ctx.enter_context(nc.sbuf_tensor(name, shape, dt))

        def sem(name):
            return ctx.enter_context(nc.semaphore(name))

        def lanes(make, name, *a):
            return [make(f"{name}{s}", *a) for s in range(LANES)]

        PS = [ctx.enter_context(nc.psum_tensor(f"ps{s}", [P, 4, 512], F32)) for s in range(LANES)]

        ident = sb("ident", [P, P])
        ident_bf = sb("ident_bf", [P, P], BF16)
        ones = sb("ones", [P, P])
        pair_ones = sb("pair_ones", [P, 2])
        minus_half = sb("minus_half", [P, 64])
        row_pick = sb("row_pick", [96, 2 * NS, P], BF16)

        w_in = sb("w_in", [P, 2, P])
        conv_w = sb("conv_w", [P, 3, 3])
        conv_b = sb("conv_b", [P, 3])
        in_b = sb("in_b", [P, 3])
        f_w1 = sb("f_w1", [3, FW])
        f_b1 = sb("f_b1", [FW, 1])
        f_w2 = sb("f_w2", [FW, FW])
        f_b2 = sb("f_b2", [FW, 1])
        f_w3 = sb("f_w3", [FW, P])
        f_t = sb("f_t", [3, 1])
        f_z = sb("f_z", [FW, 1])
        f_e = sb("f_e", [FW, 1])
        f_h1 = sb("f_h1", [FW, 1])
        f_h2 = sb("f_h2", [FW, 1])
        f_decay = sb("f_decay", [1, P])
        f_row = sb("f_row", [1, 3 * P])
        fb_row = sb("fb_row", [1, P])
        filt_b = sb("filt_b", [P, 1])
        toe = sb("toe", [P, 2 * P])
        w_out = sb("w_out", [P, P])
        b_out = sb("b_out", [P, P])
        gamma = sb("gamma", [P, P])
        beta = sb("beta", [P, P])
        q_abs = sb("q_abs", [P, 2])
        q_clip = sb("q_clip", [P, 2])
        q_scale = sb("q_scale", [P, 2])
        q_deq = sb("q_deq", [P, 2])
        q1T = sb("q1T", [P, F], BF16)
        q2T = sb("q2T", [P, FK, P], BF16)
        b1 = sb("b1", [P, F])
        b2 = sb("b2", [P, P])
        m_in = sb("m_in", [P, 2 * DI])
        m_delta = sb("m_delta", [P, DJ, DI])
        m_bdelta = sb("m_bdelta", [P, DJ])
        m_bc = sb("m_bc", [P, DJ, 2 * NS])
        m_alog = sb("m_alog", [P, DJ, NS])
        m_aexp = sb("m_aexp", [P, DJ, NS])
        m_A = sb("m_A", [P, DJ, NS])
        m_D = sb("m_D", [P, DJ])
        m_out = sb("m_out", [P, DJ, P])
        a_q = sb("a_q", [P, H * E])
        a_k = sb("a_k", [P, H * E])
        a_v = sb("a_v", [P, H * E])
        a_o = sb("a_o", [P, HP, P])
        a_bo = sb("a_bo", [P, P])
        a_gq = sb("a_gq", [P, 1])
        a_gk = sb("a_gk", [P, 1])
        a_g = sb("a_g", [P, 1])
        p_m = sb("p_m", [P, 2 * PH * NK])
        p_downT = sb("p_downT", [P, NE])
        p_up = sb("p_up", [P, EB, P])
        p_norm = sb("p_norm", [P, 1])

        X = lanes(sb, "x", [P, NB, P])
        R = lanes(sb, "r", [P, NB, P])
        R2 = lanes(sb, "r2", [P, NB, P])
        XT = lanes(sb, "xT", [P, S])
        CT = lanes(sb, "c", [C, P])
        CTT = lanes(sb, "cT", [P, C])
        MK = lanes(sb, "mask", [P, NB, C], I32)
        BNS = lanes(sb, "bns", [P, NB, 6])
        MV = lanes(sb, "mv", [P, NB, 2])
        VE = lanes(sb, "ve", [P, 64])
        RS = lanes(sb, "rs", [P, 64])
        ST = lanes(sb, "st", [P, 6, NB])
        VV = lanes(sb, "vv", [C, H, E + 1])

        WORDS = 12 * 1024
        mem = lanes(sb, "mem", [P, WORDS])

        def carve(arena, sizes):
            at, pieces = 0, {}
            for name, (rows, shape, dt) in sizes.items():
                n = int(np.prod(shape))
                words = n if dt is not BF16 else n // 2
                piece = arena[0:rows, at:at + words]
                if dt is BF16:
                    piece = piece.bitcast(BF16)
                if len(shape) > 1:
                    axes = "abcd"[:len(shape)]
                    piece = piece.rearrange(f"p ({' '.join(axes)}) -> p {' '.join(axes)}",
                                            **dict(zip(axes[1:], shape[1:])))
                pieces[name] = piece
                at += words
            assert at <= arena.shape[1], (at, arena.shape)
            return pieces

        def per_lane(**sizes):
            made = [carve(mem[s], sizes) for s in range(LANES)]
            return [[m[name] for m in made] for name in sizes]

        U, CV, V1, V2, V3, VT, PEN = per_lane(
            u=(P, (2, S), F32), cv=(P, (2, S), F32), v1=(P, (S,), F32), v2=(P, (S,), F32),
            v3=(P, (S,), F32), vt=(P, (NB, P), F32), pen=(P, (NB, C), F32))
        pen_at = 8 * S
        _, LG, LE, PT = per_lane(
            hyena=(P, (pen_at + NB * C,), F32), lg=(P, (NB, C), F32), le=(P, (NB, C), F32), pt=(C, (S,), F32))
        BIG1, BIG2, QF, QB, QT, HQ, HT = per_lane(
            pre=(P, (NB, F), F32), act=(P, (NB, F), F32), qf=(P, (NB, P), F32), qb=(P, (NB, P), BF16),
            qt=(P, (S,), BF16), hq=(P, (NB, F), BF16), ht=(P, (NB, FK, P), BF16))
        TU, TR, UU, SPA, SPE, DL, DU, BCS, BC1, BCM, dBu, HS, HC = per_lane(
            tu=(P, (DJ, S), F32), tr=(P, (DJ, S), F32), uu=(P, (DJ, S), F32), spa=(P, (DJ, S), F32),
            spe=(P, (DJ, S), F32), dl=(P, (DJ, S), F32), du=(P, (DJ, S), F32), bcs=(96, (S,), BF16),
            bc1=(2 * NS, (S,), F32), bcm=(2 * NS, (S,), BF16), dbu=(P, (DJ, S), F32), hs=(P, (DJ, S), F32),
            hc=(P, (2, DJ, S), F32))
        ON, AQ, KN, KT, SC, AT, MX, RD = per_lane(
            on=(P, (NB, H * E), F32), aq=(P, (HP, S), F32), kn=(C, (H, E), F32), kt=(P, (HP, C), F32),
            sc=(P, (2, 2, HG, C), F32), at=(C, (2, HG, P), F32), mx=(P, (2, HG), F32), rd=(P, (HG,), F32))
        QSQ, = per_lane(qsq=(P, (HP, S), F32))
        _, KQ = per_lane(front=(P, (NB * H * E + HP * S + H * E + HP * C,), F32), kq=(C, (H, E), F32))
        SIM, OS, A64, T8, TT, TH, SV, WH, HW, HWT = per_lane(
            sim=(P, (NB, 2 * PH * NK), F32), os=(P, (NB, P), F32), a64=(P, (PH, TOP, TOP), F32),
            t8=(P, (2, PH, TOP), F32), tt=(P, (PH, TOP), F32), th=(P, (PH,), F32), sv=(P, (NE,), F32),
            wh=(P, (WB, NE), F32), hw=(P, (NE,), F32), hwT=(P, (EB, P), F32))

        dA = sb("dA", [P, 2, DJ, S])
        OT = sb("oT", [P, 2, 4, P])

        prep = carve(mem[0], dict(q1_w=(P, (FK, P), F32), q2_w=(P, (F,), F32), q_t=(P, (F,), F32),
                                  p_q=(P, (2 * PH, P), F32), p_keys=(P, (2, 2, P), F32),
                                  p_keysT=(P, (4, P), F32), p_down=(P, (EB, P), F32),
                                  q1_n=(P, (FK, P), BF16), q2_n=(P, (F,), BF16),
                                  taps=(P, (2 * P,), F32)))
        q1_w, q2_w, q_t, p_q, p_keys, p_keysT, p_down, q1_n, q2_n, taps = prep.values()

        p_load = sem("p_load")
        p_const = sem("p_const")
        p_step_dve, p_step_act, p_step_pool = sem("p_step_dve"), sem("p_step_act"), sem("p_step_pool")
        p_pe = sem("p_pe")
        p_act = sem("p_act")
        p_dve = sem("p_dve")
        p_hrow = sem("p_hrow")
        p_hout = sem("p_hout")
        p_toe = sem("p_toe")

        names = """x_loaded ctx_loaded mask_loaded stored x_ready turned xT_ready u_ready u_sb
            conv0 v1_ready v_tm y_ready v3_ready o_ready var_ready rstd_ready ctx_turned ctxT_ready
            s_ready l_ready p_ready pT_ready q_ready qT_ready h_ready hpre_ready g_ready silu_u
            silu_r d_ready bc_ready ln_ready delta_ready bcs_ready B_ready C_ready dA_ready
            dbu_done scan_done hc_done y_acc yg_ready k_ready ksq_ready kn_ready kT_ready v_ready
            v_sb qsq_ready ssq_ready s_drained o_drained xr_ready sim_ready sim_sb wh_ready wh_used
            w_drained z_ready g_sb hw_ready hwT_ready""".split()
        sg = {n: [sem(f"{n}{s}") for s in range(LANES)] for n in names}
        dve_step, act_step = sem("dve_step"), sem("act_step")
        lane_sems = [q for n in names for q in sg[n]] + [dve_step, act_step]

        def column(ap):
            return ap.rearrange("(p o) -> p o", o=1)

        def row(ap):
            return ap.rearrange("(o p) -> o p", o=1)

        def down(ap, n=P):
            return bass.AP(ap.tensor, ap.offset, [[0, n], *[list(d) for d in ap.ap]])

        loads = [
            (f_w1[:], L0_attn_w1), (f_b1[:], column(L0_attn_b1)), (f_w2[:], L0_attn_w2),
            (f_b2[:], column(L0_attn_b2)), (f_w3[:], L0_attn_w3), (fb_row[:], row(L0_attn_filt_bias)),
            (filt_b[:], column(L0_attn_filt_bias)),
            (w_in[:, 0, :], L0_attn_w_in[:, 0:P]), (w_in[:, 1, :], L0_attn_w_in[:, 2 * P:3 * P]),
            (conv_w[:], L0_attn_w_conv.rearrange("(c p) o k -> p c (o k)", p=P)),
            (conv_b[:], L0_attn_b_conv.rearrange("(c p) -> p c", p=P)),
            (in_b[:], L0_attn_b_in.rearrange("(c p) -> p c", p=P)),
            (w_out[:], L0_attn_w_out), (b_out[:], down(L0_attn_b_out)),
            (gamma[:], down(L0_xattn_gamma)), (beta[:], down(L0_xattn_beta)),
            (q1_w[:], L0_ffn_w1.rearrange("(k p) d -> p k d", p=P)), (q2_w[:], L0_ffn_w2),
            (b1[:], down(L0_ffn_b1)), (b2[:], down(L0_ffn_b2)),
            (m_in[:], L1_attn_W_in), (m_delta[:], L1_attn_W_delta.rearrange("(k p) m -> p k m", p=P)),
            (m_bdelta[:], L1_attn_b_delta.rearrange("(k p) -> p k", p=P)),
            (m_bc[:, :, 0:NS], L1_attn_W_B.rearrange("(k p) n -> p k n", p=P)),
            (m_bc[:, :, NS:2 * NS], L1_attn_W_C.rearrange("(k p) n -> p k n", p=P)),
            (m_alog[:], L1_attn_A_log.rearrange("(k p) n -> p k n", p=P)),
            (m_D[:], L1_attn_D_param.rearrange("(k p) -> p k", p=P)),
            (m_out[:], L1_attn_W_out.rearrange("(k p) m -> p k m", p=P)),
            (a_q[:], L1_xattn_Wq.rearrange("d h e -> d (h e)")),
            (a_k[:], L1_xattn_Wk.rearrange("d h e -> d (h e)")),
            (a_v[:], L1_xattn_Wv.rearrange("d h e -> d (h e)")),
            (a_o[:], L1_xattn_Wo.rearrange("(j t) e d -> (t e) j d", t=2)),
            (a_bo[:], down(L1_xattn_bo)),
            (a_gq[0:E, :], column(L1_xattn_gq)), (a_gq[E:2 * E, :], column(L1_xattn_gq)),
            (a_gk[0:E, :], column(L1_xattn_gk)), (a_gk[E:2 * E, :], column(L1_xattn_gk)),
            (p_q[:], L1_ffn_w_q.rearrange("(j e) d -> e j d", e=P)),
            (p_keys[:], L1_ffn_keys.rearrange("(t h) k j e -> (h k) t j e", t=2)),
            (p_down[:], L1_ffn_expert_down.rearrange("(b p) d -> p b d", p=P)),
            (p_up[:], L1_ffn_expert_up.rearrange("(b p) d -> p b d", p=P)),
            (p_norm[:], column(L1_ffn_norm_w)),
        ]
        ALL_LOADED = 16 * len(loads)

        with nc.Block() as block:
            @block.sync
            def _(sp):
                with nc.allow_non_contiguous_dma("small vectors down the partitions"):
                    for to, of in loads:
                        sp.dma_start(to, of).then_inc(p_load, 16)
                sp.wait_ge(p_hrow, 1)
                sp.dma_start(row(h_pad), f_row[:]).then_inc(p_hout, 16)
                sp.wait_ge(p_hout, 16)
                sp.dma_start(taps[:], bass.AP(h_pad.tensor, 0, [[1, P], [1, 2 * P]])).then_inc(p_toe, 16)

            @block.gpsimd
            def _(pool):
                w = Signals(pool, p_step_pool)
                w.link(nc.gpsimd.memset(minus_half[:], -0.5))
                w.link(nc.gpsimd.memset(ones[:], 1.0))
                w.link(nc.gpsimd.memset(ident[:], 0.0))
                w.link(nc.gpsimd.affine_select(out=ident[:], in_=ident[:], compare_op=ALU.not_equal,
                                               fill=1.0, base=0, pattern=[[-1, P]], channel_multiplier=1))
                w.link(nc.gpsimd.memset(row_pick[:], 0.0))
                for g in range(3):
                    w.link(nc.gpsimd.affine_select(
                        out=row_pick[:], in_=row_pick[:], compare_op=ALU.not_equal, fill=1.0,
                        base=-2 * NS * g, pattern=[[-1, 2 * NS], [0, P]], channel_multiplier=1))
                w.link(nc.gpsimd.memset(pair_ones[:], 0.0))
                w.link(nc.gpsimd.memset(pair_ones[0:E, 0:1], 1.0))
                w.link(nc.gpsimd.memset(pair_ones[E:2 * E, 1:2], 1.0))
                w.link(nc.gpsimd.memset(f_t[:], 0.0))
                w.link(nc.gpsimd.memset(dA[:], 0.0))
                for s in range(LANES):
                    w.link(nc.gpsimd.memset(VE[s][:], 1.0))
                    w.link(nc.gpsimd.memset(VV[s][:, :, E:E + 1], 1.0))
                nc.gpsimd.memset(f_row[:], 0.0).then_inc(p_const, 1)

            @block.tensor
            def _(pe):
                w = Signals(pe)
                pe.wait_ge(p_load, ALL_LOADED)
                pe.wait_ge(p_const, 1)
                pe.matmul(PS[0][0:FW, 0, 0:1], f_w1[:], f_t[:], start=True, stop=True).then_inc(p_pe, 1)
                pe.wait_ge(p_dve, 1)
                pe.matmul(PS[0][0:FW, 0, 1:2], f_w2[:], f_h1[:], start=True, stop=True).then_inc(p_pe, 1)
                pe.wait_ge(p_dve, 2)
                pe.matmul(PS[0][0:1, 0, 128:256], f_h2[:], f_w3[:, :], start=True, stop=True).then_inc(p_pe, 1)
                pe.wait_ge(p_dve, 3)
                pe.matmul(PS[0][:, 1, 0:2], ones[:], q_abs[:], start=True, stop=True).then_inc(p_pe, 1)
                for n in range(4):
                    mm = pe.transpose(PS[0][:, 2, n * P:(n + 1) * P], p_keys[:, n // 2, n % 2, :], ident[:])
                mm.then_inc(p_pe, 1)
                for n in range(EB):
                    mm = pe.transpose(PS[1][:, n // 4, (n % 4) * P:(n % 4 + 1) * P], p_down[:, n, :], ident[:])
                mm.then_inc(p_pe, 1)
                pe.wait_ge(p_act, 5)
                for j in range(2):
                    for h in range(PH):
                        c = (j * PH + h) * NK
                        n = (h // 4) * 2 + j
                        mm = pe.matmul(PS[0][:, 3, c:c + NK], p_q[:, 2 * h + j, :],
                                       p_keysT[:, n, (h % 4) * NK:(h % 4 + 1) * NK], start=True, stop=True)
                mm.then_inc(p_pe, 1)
                pe.wait_ge(p_dve, 4)
                for k in range(FK):
                    pe.transpose(PS[1][:, 2, :].bitcast(BF16)[:, k * P:(k + 1) * P], q1_n[:, k, :], ident_bf[:])
                for k in range(FK):
                    mm = pe.transpose(PS[1][:, 3, :].bitcast(BF16)[:, k * P:(k + 1) * P],
                                      q2_n[:, k * P:(k + 1) * P], ident_bf[:])
                mm.then_inc(p_pe, 1)

            @block.scalar
            def _(act):
                w = Signals(act, p_step_act)
                act.wait_ge(p_load, ALL_LOADED)
                act.wait_ge(p_const, 1)
                for n in range(2):
                    act.wait_ge(p_step_dve, n + 1)
                    nc.scalar.activation(f_e[:], f_z[:], ACT.Tanh, scale=0.5).then_inc(p_act, 1)
                w.link(nc.scalar.activation(f_decay[:], fb_row[:], ACT.Abs))
                nc.scalar.activation(f_decay[:], f_decay[:], ACT.Exp, scale=-0.0).then_inc(p_act, 1)
                nc.scalar.activation(m_aexp[:], m_alog[:], ACT.Exp).then_inc(p_act, 1)
                act.wait_ge(p_pe, 5)
                nc.scalar.activation(p_keysT[:].rearrange("p a b -> p (a b)"), PS[0][:, 2, :], ACT.Copy)\
                    .then_inc(p_act, 1)
                act.wait_ge(p_pe, 6)
                nc.scalar.activation(p_downT[:].rearrange("p (a b) -> p a b", a=2), PS[1][:, 0:2, :], ACT.Copy)
                act.wait_ge(p_pe, 7)
                nc.scalar.activation(p_m[:], PS[0][:, 3, :], ACT.Copy)
                act.wait_ge(p_pe, 8)
                nc.scalar.activation(q1T[:], PS[1][:, 2, :].bitcast(BF16)[:, 0:F], ACT.Copy)
                nc.scalar.activation(q2T[:].rearrange("p a b -> p (a b)"),
                                     PS[1][:, 3, :].bitcast(BF16)[:, 0:F], ACT.Copy)

            @block.vector
            def _(dve):
                w = Signals(dve, p_step_dve)
                dve.wait_ge(p_load, ALL_LOADED)
                dve.wait_ge(p_const, 1)
                for n, (b, h) in enumerate([(f_b1, f_h1), (f_b2, f_h2)]):
                    dve.wait_ge(p_pe, n + 1)
                    w.link(nc.vector.tensor_tensor(f_z[:], PS[0][0:FW, 0, n:n + 1], b[:], ALU.add))
                    dve.wait_ge(p_act, n + 1)
                    w.steps += 0
                    nc.vector.scalar_tensor_tensor(out=h[:], in0=f_e[:], scalar=1.0, in1=f_z[:],
                                                   op0=ALU.add, op1=ALU.mult)
                    dve.drain()
                    nc.vector.tensor_scalar(h[:], h[:], 0.5, None, ALU.mult).then_inc(p_dve, 1)
                nc.vector.tensor_copy(ident_bf[:], ident[:])
                nc.vector.tensor_reduce(q_abs[:, 0:1], q1_w[:].rearrange("p a b -> p (a b)"), AX.X, ALU.add,
                                        apply_absolute_value=True)
                nc.vector.tensor_reduce(q_abs[:, 1:2], q2_w[:], AX.X, ALU.add,
                                        apply_absolute_value=True).then_inc(p_dve, 1)
                dve.wait_ge(p_pe, 3)
                dve.wait_ge(p_act, 3)
                nc.vector.tensor_tensor(f_row[:, P:2 * P], PS[0][0:1, 0, 128:256][:, ::-1],
                                        f_decay[:, ::-1], ALU.mult).then_inc(p_hrow, 1)
                dve.wait_ge(p_pe, 4)
                w.link(nc.vector.tensor_scalar(q_clip[:], PS[0][:, 1, 0:2], 1.0 / (F * D), 1e-5,
                                               ALU.mult, ALU.max))
                w.link(nc.vector.reciprocal(q_scale[:], q_clip[:]))
                nc.vector.tensor_scalar(q_deq[:], q_clip[:], 1.0 / 127.0, None, ALU.mult)
                for k, (of, to) in enumerate([(q1_w[:].rearrange("p a b -> p (a b)"),
                                               q1_n[:].rearrange("p a b -> p (a b)")), (q2_w[:], q2_n[:])]):
                    w.link(nc.vector.tensor_scalar(q_t[:], of, q_scale[:, k:k + 1], ROUND, ALU.mult, ALU.add))
                    w.link(nc.vector.tensor_scalar(q_t[:], q_t[:], -ROUND, 1.0, ALU.add, ALU.min))
                    last = nc.vector.tensor_scalar(to, q_t[:], -1.0, None, ALU.max)
                    if k == 0:
                        w.link(last)
                last.then_inc(p_dve, 1)
                w.link(nc.vector.tensor_tensor(a_g[:], a_gq[:], a_gk[:], ALU.mult))
                w.link(nc.vector.tensor_scalar(a_g[:], a_g[:], float(E) ** -0.5, None, ALU.mult))
                dve.wait_ge(p_act, 4)
                nc.vector.tensor_scalar(m_A[:], m_aexp[:], -1.0, None, ALU.mult)
                dve.wait_ge(p_toe, 16)
                nc.vector.tensor_copy(toe[:], taps[:, ::-1])

        prep_tail = None

        tok = "(k p) d -> p k d"

        def turn(w, pe, s, of, bank):
            for k in range(NB):
                mm = pe.transpose(PS[s][:, bank, k * P:(k + 1) * P], of[:, k, :], ident[:])
            mm.then_inc(sg["turned"][s], 1)

        def body(it):
            with nc.Block() as block:
                @block.sync
                def _(sp):
                    for s in range(LANES):
                        i = 2 * it + s
                        sp.dma_start(X[s][:], x[bass.ds(i, 1)].rearrange("o (k p) d -> p (o k) d", p=P))\
                            .then_inc(sg["x_loaded"][s], 16)
                        sp.dma_start(CT[s][:], ctx_1024[bass.ds(i, 1)].rearrange("o c d -> (o c) d"))\
                            .then_inc(sg["ctx_loaded"][s], 16)
                        sp.dma_start(MK[s][:], mask_BxSxS2_ik1[bass.ds(i, 1)]
                                     .rearrange("o (k p) c -> p (o k) c", p=P)).then_inc(sg["mask_loaded"][s], 16)
                    for s in range(LANES):
                        i = 2 * it + s
                        sp.wait_ge(sg["x_ready"][s], 6)
                        sp.dma_start(out[bass.ds(i, 1)].rearrange("o (k p) d -> p (o k) d", p=P), X[s][:])\
                            .then_inc(sg["stored"][s], 16)
                    for s in range(LANES):
                        sp.wait_ge(sg["stored"][s], 16)

                pe_program(block)
                act_program(block)
                dve_program(block)
                pool_program(block)

        def pe_program(block):
            @block.tensor
            def _(pe):
                w = Signals(pe)

                def G(n, s):
                    return sg[n][s]

                def hyena(s):
                    ps = PS[s]
                    pe.wait_ge(G("x_loaded", s), 16)
                    turn(w, pe, s, X[s], 0)
                    pe.wait_ge(G("ctx_loaded", s), 16)
                    pe.transpose(ps[:, 3, 0:C], CT[s][:], ident[0:C, 0:C]).then_inc(G("ctx_turned", s), 1)
                    w.next(G("xT_ready", s))
                    for j in range(2):
                        pe.matmul(ps[:, 1 + j, :], w_in[:, j, :], XT[s][:], start=True, stop=True)\
                            .then_inc(G("u_ready", s), 1)
                    w.next(G("v1_ready", s))
                    w.next(G("ctxT_ready", s))
                    for k in range(NB):
                        mm = pe.transpose(ps[:, 3, k * P:(k + 1) * P], V1[s][:, k * P:(k + 1) * P], ident[:])
                    mm.then_inc(G("turned", s), 1)
                    w.next(G("v_tm", s))
                    for k in range(NB):
                        n = min(2 * P, S - k * P)
                        mm = pe.matmul(ps[:, 0, k * P:k * P + n], VT[s][:, k, :], toe[:, 0:n],
                                       start=(k == 0), stop=(k == NB - 1), skip_group_check=True)
                    mm.then_inc(G("y_ready", s), 1)
                    w.next(G("v3_ready", s))
                    for k in range(NB):
                        mm = pe.matmul(ps[:, 1, k * P:(k + 1) * P], V3[s][:, k * P:(k + 1) * P], w_out[:],
                                       start=True, stop=True)
                    mm.then_inc(G("o_ready", s), 1)

                def cross0(s):
                    ps = PS[s]
                    w.next(G("x_ready", s))
                    turn(w, pe, s, X[s], 0)
                    w.next(G("xT_ready", s))
                    for k in range(NB):
                        mm = pe.matmul(ps[:, 1, k * C:(k + 1) * C], XT[s][:, k * P:(k + 1) * P], CTT[s][:],
                                       start=True, stop=True)
                    mm.then_inc(G("s_ready", s), 1)
                    w.next(G("p_ready", s))
                    for k in range(NB):
                        mm = pe.transpose(ps[0:C, 2, k * P:(k + 1) * P], LE[s][:, k, :], ident[:])
                    mm.then_inc(G("turned", s), 1)
                    w.next(G("pT_ready", s))
                    for k in range(NB):
                        mm = pe.matmul(ps[:, 3, k * P:(k + 1) * P], PT[s][:, k * P:(k + 1) * P], CT[s][:],
                                       start=True, stop=True)
                    mm.then_inc(G("o_ready", s), 1)

                def bitffn(s):
                    ps = PS[s]
                    w.next(G("x_ready", s))
                    w.next(G("q_ready", s))
                    for k in range(NB):
                        mm = pe.transpose(ps[:, 0, :].bitcast(BF16)[:, k * P:(k + 1) * P], QB[s][:, k, :],
                                          ident_bf[:])
                    mm.then_inc(G("turned", s), 1)
                    w.next(G("qT_ready", s))
                    for k in range(NB):
                        pe.matmul(ps[:, k, :], QT[s][:, k * P:(k + 1) * P], q1T[:], start=True, stop=True)\
                            .then_inc(G("h_ready", s), 1)
                    for k in range(NB):
                        w.next(G("q_ready", s))
                        for j in range(FK):
                            mm = pe.transpose(ps[:, k, :].bitcast(BF16)[:, j * P:(j + 1) * P],
                                              HQ[s][:, k, j * P:(j + 1) * P], ident_bf[:])
                        mm.then_inc(G("turned", s), 1)
                    w.next(G("qT_ready", s), NB)
                    for k in range(NB):
                        for j in range(FK):
                            mm = pe.matmul(ps[:, 0, k * P:(k + 1) * P], HT[s][:, k, j, :], q2T[:, j, :],
                                           start=(j == 0), stop=(j == FK - 1))
                    mm.then_inc(G("o_ready", s), 1)

                def scan(s):
                    ps = PS[s]
                    w.next(G("x_ready", s))
                    turn(w, pe, s, X[s], 0)
                    w.next(G("xT_ready", s))
                    for j, bank in enumerate([1, 2, 3, 0]):
                        pe.matmul(ps[:, bank, :], m_in[:, j * P:(j + 1) * P], XT[s][:], start=True, stop=True)\
                            .then_inc(G("u_ready", s), 1)
                    w.next(G("silu_u", s), DJ)
                    for m in range(DJ):
                        for k in range(DJ):
                            mm = pe.matmul(ps[:, 1 + m, :], m_delta[:, k, m * P:(m + 1) * P], UU[s][:, k, :],
                                           start=(k == 0), stop=(k == DJ - 1))
                        mm.then_inc(G("d_ready", s), 1)
                    w.next(G("silu_r", s), DJ)
                    for k in range(DJ):
                        mm = pe.matmul(ps[0:2 * NS, 3, :], m_bc[:, k, :], UU[s][:, k, :],
                                       start=(k == 0), stop=(k == DJ - 1))
                    mm.then_inc(G("bc_ready", s), 1)

                    def broadcast(row_n, bank, ready):
                        pe.matmul(ps[:, bank, :], row_pick[:, row_n, :], BCS[s][:], start=True, stop=True)\
                            .then_inc(G(ready, s), 1)

                    w.next(G("bcs_ready", s))
                    w.next(G("delta_ready", s))
                    broadcast(0, 0, "B_ready")
                    broadcast(NS, 3, "C_ready")
                    for n in range(NS):
                        if n + 1 < NS:
                            w.next(G("dbu_done", s))
                            broadcast(n + 1, 0, "B_ready")
                        w.next(G("hc_done", s))
                        if n + 1 < NS:
                            broadcast(NS + n + 1, 3, "C_ready")
                        for j in range(DJ):
                            mm = pe.matmul(ps[:, 1 + j, :], ident[:], HC[s][:, n % 2, j, :],
                                           start=(n == 0), stop=(n == NS - 1), skip_group_check=True)
                        mm.then_inc(G("y_acc", s), 1)
                    w.next(G("yg_ready", s))
                    for k in range(NB):
                        for j in range(DJ):
                            mm = pe.matmul(ps[:, 0, k * P:(k + 1) * P], TU[s][:, j, k * P:(k + 1) * P],
                                           m_out[:, j, :], start=(j == 0), stop=(j == DJ - 1))
                    mm.then_inc(G("o_ready", s), 1)

                def cross1(s):
                    ps = PS[s]
                    w.next(G("x_ready", s))
                    turn(w, pe, s, X[s], 0)
                    for j in range(2):
                        pe.matmul(ps[0:C, 1 + j, :], CTT[s][:], a_k[:, j * 512:(j + 1) * 512],
                                  start=True, stop=True).then_inc(G("k_ready", s), 1)
                    pe.matmul(ps[0:C, 3, :], CTT[s][:], a_v[:, 0:512], start=True, stop=True)\
                        .then_inc(G("v_ready", s), 1)
                    w.next(G("xT_ready", s))
                    pe.matmul(ps[0:C, 0, :], CTT[s][:], a_v[:, 512:1024], start=True, stop=True)\
                        .then_inc(G("v_ready", s), 1)
                    w.next(G("kn_ready", s))
                    for j in range(HP):
                        mm = pe.transpose(ps[:, 1 + j // 4, (j % 4) * C:(j % 4 + 1) * C],
                                          KN[s][:, 2 * j:2 * j + 2, :].rearrange("p a b -> p (a b)"),
                                          ident[0:C, 0:C])
                    mm.then_inc(G("turned", s), 1)
                    for j in range(HP):
                        bank = [3, 0, 1, 2][j % 4]
                        if j < 2:
                            w.next(G("v_sb", s))
                        elif j == 2:
                            w.next(G("kT_ready", s))
                        elif j >= 4:
                            w.next(G("qsq_ready", s))
                        pe.matmul(ps[:, bank, :], a_q[:, j * P:(j + 1) * P], XT[s][:], start=True, stop=True)\
                            .then_inc(G("q_ready", s), 1)
                    w.next(G("qsq_ready", s), 4)
                    for k in range(NB):
                        for j in range(HP):
                            c = 512 - NB * H + k * H + 2 * j
                            mm = pe.matmul(ps[:, 3, c:c + 2],
                                           QSQ[s][:, j, k * P:(k + 1) * P],
                                           pair_ones[:], start=True, stop=True)
                    mm.then_inc(G("ssq_ready", s), 1)

                    def scores(g):
                        k, half = g // NG, g % NG
                        if g >= 1:
                            w.next(G("s_drained", s))
                        for h in range(2 * HG):
                            hh = half * 2 * HG + h
                            lo = (hh % 2) * E
                            mm = pe.matmul(ps[:, h % 2, (h // 2) * C:(h // 2 + 1) * C],
                                           AQ[s][lo:lo + E, hh // 2, k * P:(k + 1) * P],
                                           KT[s][lo:lo + E, hh // 2, :], start=True, stop=True)
                        mm.then_inc(G("s_ready", s), 1)

                    def weights_turned(u):
                        g = u // 2
                        if u % 2 == 0:
                            w.next(G("p_ready", s))
                        for h in range(HG):
                            mm = pe.transpose(ps[0:C, 2, h * P:(h + 1) * P], SC[s][:, g % 2, u % 2, h, :], ident[:])
                        mm.then_inc(G("turned", s), 1)

                    def values(u):
                        g = u // 2
                        if u >= 1:
                            w.next(G("o_drained", s))
                        for h in range(HG):
                            hh = (g % NG) * 2 * HG + 2 * h + u % 2
                            mm = pe.matmul(ps[:, 3, h * (E + 1):(h + 1) * (E + 1)], AT[s][:, u % 2, h, :],
                                           VV[s][:, hh, :], start=True, stop=True)
                        mm.then_inc(G("o_ready", s), 1)

                    NU = NB * H // HG
                    scores(0)
                    for u in range(NU + 1):
                        if u % 2 == 0 and u // 2 + 1 < NB * NG:
                            scores(u // 2 + 1)
                        if u >= 1:
                            w.next(G("pT_ready", s))
                        if u < NU:
                            weights_turned(u)
                        if u >= 1:
                            values(u - 1)
                    w.next(G("o_drained", s))
                    w.next(G("s_drained", s))

                    def heads_turned(v):
                        k, half = v // 2, v % 2
                        if v >= 2:
                            w.next(G("qT_ready", s))
                        for j in range(4):
                            c = (half * 4 + j) * P
                            mm = pe.transpose(ps[:, v % 2, j * P:(j + 1) * P], ON[s][:, k, c:c + P], ident[:])
                        mm.then_inc(G("turned", s), 1)

                    heads_turned(0)
                    heads_turned(1)
                    for v in range(2 * NB):
                        if v + 2 < 2 * NB:
                            heads_turned(v + 2)
                        else:
                            w.next(G("qT_ready", s))
                        for j in range(4):
                            mm = pe.matmul(ps[:, 3, (v // 2) * P:(v // 2 + 1) * P], OT[:, v % 2, j, :],
                                           a_o[:, (v % 2) * 4 + j, :], start=(v % 2 == 0 and j == 0),
                                           stop=(v % 2 == 1 and j == 3))
                        mm.then_inc(G("wh_used", s), 1)

                def experts(s):
                    ps = PS[s]
                    w.next(G("x_ready", s))
                    w.next(G("xr_ready", s))
                    turn(w, pe, s, R[s], 0)
                    w.next(G("xT_ready", s))
                    for k in range(NB):
                        pe.matmul(ps[:, k, :], XT[s][:, k * P:(k + 1) * P], p_m[:], start=True, stop=True)\
                            .then_inc(G("sim_ready", s), 1)
                    w.next(G("sim_sb", s), NB)

                    def expert_inputs(k):
                        for j in range(2):
                            pe.matmul(ps[:, 2 + j, :], XT[s][:, k * P:(k + 1) * P], p_downT[:, j * 512:(j + 1) * 512],
                                      start=True, stop=True).then_inc(G("z_ready", s), 1)

                    expert_inputs(0)
                    for k in range(NB):
                        for h in range(PH):
                            w.next(G("wh_ready", s))
                            for j in range(2):
                                mm = pe.matmul(ps[:, j, :], ident[:], WH[s][:, h % WB, j * 512:(j + 1) * 512],
                                               start=(h == 0), stop=(h == PH - 1), skip_group_check=True)
                            mm.then_inc(G("wh_used", s), 1)
                        w.next(G("hw_ready", s))
                        for e in range(EB):
                            mm = pe.transpose(ps[:, 2 + e // 4, (e % 4) * P:(e % 4 + 1) * P],
                                              HW[s][:, e * P:(e + 1) * P], ident[:])
                        mm.then_inc(G("turned", s), 1)
                        w.next(G("hwT_ready", s))
                        for e in range(EB):
                            mm = pe.matmul(ps[:, 2, 0:P], HWT[s][:, e, :], p_up[:, e, :],
                                           start=(e == 0), stop=(e == EB - 1))
                        mm.then_inc(G("o_ready", s), 1)
                        w.next(G("o_drained", s))
                        if k + 1 < NB:
                            expert_inputs(k + 1)

                for phase in (hyena, cross0, bitffn, scan, cross1, experts):
                    for s in range(LANES):
                        phase(s)

        def act_program(block):
            @block.scalar
            def _(act):
                w = Signals(act, act_step)

                def G(n, s):
                    return sg[n][s]

                def copy(to, of, signal=None, **kw):
                    ins = nc.scalar.activation(to, of, ACT.Copy, **kw)
                    if signal is not None:
                        ins.then_inc(signal, 1)
                    return ins

                def turned(s, to, of, ready, **kw):
                    w.next(G("turned", s))
                    copy(to, of, G(ready, s), **kw)

                def hyena(s):
                    ps = PS[s]
                    turned(s, XT[s][:], ps[:, 0, :], "xT_ready")
                    w.next(G("ctx_turned", s))
                    copy(CTT[s][:], ps[:, 3, 0:C], G("ctxT_ready", s))
                    for j, c in enumerate((0, 2)):
                        w.next(G("u_ready", s))
                        w.link(nc.scalar.activation(U[s][:, j, :], ps[:, 1 + j, :], ACT.Identity,
                                                    bias=in_b[:, c:c + 1]))
                        nc.scalar.activation(CV[s][:, j, :], U[s][:, j, :], ACT.Identity,
                                             bias=conv_b[:, c:c + 1], scale=conv_w[:, c, 2:3])\
                            .then_inc(G("conv0", s), 1)
                    turned(s, VT[s][:].rearrange("p a b -> p (a b)"), ps[:, 3, :], "v_tm")

                def cross0(s):
                    ps = PS[s]
                    turned(s, XT[s][:], ps[:, 0, :], "xT_ready")
                    w.next(G("l_ready", s))
                    nc.scalar.activation(LE[s][:], LG[s][:], ACT.Exp).then_inc(G("p_ready", s), 1)
                    turned(s, PT[s][:], ps[0:C, 2, :], "pT_ready")

                def bitffn(s):
                    ps = PS[s]
                    turned(s, QT[s][:], ps[:, 0, :].bitcast(BF16)[:, 0:S], "qT_ready")
                    for k in range(NB):
                        w.next(G("hpre_ready", s))
                        w.link(nc.scalar.activation(BIG2[s][:, k, :], BIG1[s][:, k, :], ACT.Gelu))
                        nc.scalar.activation(BIG1[s][:, k, :], BIG2[s][:, k, :], ACT.Square,
                                             accum_out=ST[s][:, 4, k:k + 1]).then_inc(G("g_ready", s), 1)
                    for k in range(NB):
                        turned(s, HT[s][:, k].rearrange("p a b -> p (a b)"),
                               ps[:, k, :].bitcast(BF16)[:, 0:F], "qT_ready")

                def scan(s):
                    ps = PS[s]
                    turned(s, XT[s][:], ps[:, 0, :], "xT_ready")
                    for j, bank in enumerate([1, 2, 3, 0]):
                        w.next(G("u_ready", s))
                        to = TU[s] if j < DJ else TR[s]
                        nc.scalar.activation(to[:, j % DJ, :], ps[:, bank, :], ACT.Tanh, scale=0.5)\
                            .then_inc(G("g_ready", s), 1)
                    for j in range(DJ):
                        w.next(G("d_ready", s))
                        w.link(nc.scalar.activation(SPA[s][:, j, :], ps[:, 1 + j, :], ACT.Abs,
                                                    bias=m_bdelta[:, j:j + 1]))
                        w.link(nc.scalar.activation(SPE[s][:, j, :], SPA[s][:, j, :], ACT.Exp, scale=-1.0))
                        nc.scalar.activation(SPA[s][:, j, :], SPE[s][:, j, :], ACT.Ln, bias=1.0)\
                            .then_inc(G("ln_ready", s), 1)
                    w.next(G("delta_ready", s))
                    for n in range(NS):
                        if n >= 2:
                            w.next(G("scan_done", s))
                        for j in range(DJ):
                            ins = nc.scalar.activation(dA[:, n % 2, j, 1:S], DL[s][:, j, 1:S], ACT.Exp,
                                                       scale=m_A[:, j, n:n + 1])
                        ins.then_inc(G("dA_ready", s), 1)
                    w.next(G("scan_done", s), 2)

                def cross1(s):
                    ps = PS[s]
                    turned(s, XT[s][:], ps[:, 0, :], "xT_ready")
                    for j in range(2):
                        w.next(G("k_ready", s))
                        nc.scalar.activation(KQ[s][:].rearrange("p a b -> p (a b)")[:, j * 512:(j + 1) * 512],
                                             ps[0:C, 1 + j, :], ACT.Square).then_inc(G("ksq_ready", s), 1)
                    for j, bank in enumerate((3, 0)):
                        w.next(G("v_ready", s))
                        copy(VV[s][:, j * 8:(j + 1) * 8, 0:E],
                             ps[0:C, bank, :].rearrange("p (a b) -> p a b", b=E), G("v_sb", s))
                    turned(s, KT[s][:].rearrange("p (a b) c -> p a (b c)", a=2), ps[:, 1:3, 0:4 * C],
                           "kT_ready", scale=a_g[:, 0:1])
                    for j in range(HP):
                        bank = [3, 0, 1, 2][j % 4]
                        w.next(G("q_ready", s))
                        copy(AQ[s][:, j, :], ps[:, bank, :])
                        nc.scalar.activation(QSQ[s][:, j, :], ps[:, bank, :], ACT.Square)\
                            .then_inc(G("qsq_ready", s), 1)
                    NU = NB * H // HG
                    for g in range(NU // 2):
                        w.next(G("l_ready", s))
                        nc.scalar.activation(SC[s][:, g % 2].rearrange("p a b c -> p (a b c)"),
                                             SC[s][:, g % 2].rearrange("p a b c -> p (a b c)"), ACT.Exp)\
                            .then_inc(G("p_ready", s), 1)
                        if g >= 1:
                            for u in (2 * g - 2, 2 * g - 1):
                                turned(s, AT[s][:, u % 2].rearrange("p a b -> p (a b)"), ps[0:C, 2, :], "pT_ready")
                    for u in (NU - 2, NU - 1):
                        turned(s, AT[s][:, u % 2].rearrange("p a b -> p (a b)"), ps[0:C, 2, :], "pT_ready")
                    for v in range(2 * NB):
                        if v >= 2:
                            w.next(G("wh_used", s))
                        turned(s, OT[:, v % 2].rearrange("p a b -> p (a b)"), ps[:, v % 2, :], "qT_ready")
                    w.next(G("wh_used", s), 2)

                def experts(s):
                    ps = PS[s]
                    turned(s, XT[s][:], ps[:, 0, :], "xT_ready", scale=p_norm[:, 0:1])
                    for k in range(NB):
                        w.next(G("sim_ready", s))
                        copy(SIM[s][:, k, :], ps[:, k, :], G("sim_sb", s))
                    for k in range(NB):
                        if k >= 1:
                            pass
                        w.next(G("z_ready", s), 2)
                        nc.scalar.activation(HW[s][:].rearrange("p (a b) -> p a b", a=2), ps[:, 2:4, :], ACT.Gelu)\
                            .then_inc(G("g_sb", s), 1)
                        w.next(G("turned", s))
                        copy(HWT[s][:].rearrange("p (a b) c -> p a (b c)", a=2), ps[:, 2:4, :], G("hwT_ready", s))
                        w.next(G("o_ready", s))
                        copy(OS[s][:, k, :], ps[:, 2, 0:P], G("o_drained", s))

                seen_x = None
                for phase in (hyena, cross0, bitffn, scan, cross1, experts):
                    for s in range(LANES):
                        if phase is cross0 or phase is scan or phase is cross1 or phase is experts:
                            pass
                        skip_o(w, s, phase.__name__, "act")
                        phase(s)

        def skip_o(w, s, phase, engine):
            def passed(name, n):
                key = sg[name][s].name if hasattr(sg[name][s], "name") else str(sg[name][s])
                w.seen[key] = w.seen.get(key, 0) + n

            if engine == "act" and phase == "scan":
                passed("g_ready", 0)
            if engine == "act" and phase == "cross1":
                passed("q_ready", 1 + NB)
            if engine == "act" and phase == "experts":
                passed("o_ready", 4 + NB * H // HG)
            if engine == "pe" and phase == "cross1":
                pass

        def dve_program(block):
            @block.vector
            def _(dve):
                w = Signals(dve, dve_step)

                def G(n, s):
                    return sg[n][s]

                def rsqrt(s, ins):
                    ins.then_inc(G("var_ready", s), 1)
                    w.next(G("rstd_ready", s))

                def normalise(s, of, to, eps, signal):
                    for k in range(NB):
                        ins = nc.vector.bn_stats(BNS[s][:, k, :], of[:, k, :])
                    w.link(ins)
                    for k in range(NB):
                        ins = nc.vector.bn_aggr(MV[s][:, k, :], BNS[s][:, k, :])
                    w.link(ins)
                    rsqrt(s, nc.vector.tensor_scalar(VE[s][:, 0:NB], MV[s][:, :, 1], eps, None, ALU.add))
                    for k in range(NB):
                        ins = nc.vector.tensor_scalar(to[:, k, :], of[:, k, :], MV[s][:, k, 0:1],
                                                      RS[s][:, k:k + 1], ALU.subtract, ALU.mult)
                    if signal is None:
                        w.link(ins)
                    else:
                        ins.then_inc(signal, 1)
                        w.next(signal)

                def residual(s, of, bias):
                    w.link(nc.vector.tensor_tensor(R[s][:], of, X[s][:], ALU.add))
                    if bias is not None:
                        w.link(nc.vector.tensor_tensor(R[s][:], R[s][:], spread(bias[:], 1, NB), ALU.add))
                    normalise(s, R[s], X[s], 1e-5, G("x_ready", s))

                def bank(s, n):
                    return PS[s][:, n, :].rearrange("p (k d) -> p k d", k=NB)

                def hyena(s):
                    ps = PS[s]
                    dve.wait_ge(G("x_loaded", s), 16)
                    for j, c in enumerate((0, 2)):
                        w.next(G("conv0", s))
                        w.link(nc.vector.scalar_tensor_tensor(
                            out=CV[s][:, j, 1:S], in0=U[s][:, j, 0:S - 1], scalar=conv_w[:, c, 1:2],
                            in1=CV[s][:, j, 1:S], op0=ALU.mult, op1=ALU.add))
                        w.link(nc.vector.scalar_tensor_tensor(
                            out=CV[s][:, j, 2:S], in0=U[s][:, j, 0:S - 2], scalar=conv_w[:, c, 0:1],
                            in1=CV[s][:, j, 2:S], op0=ALU.mult, op1=ALU.add))
                    nc.vector.tensor_tensor(V1[s][:], CV[s][:, 1, :], CV[s][:, 0, :], ALU.mult)\
                        .then_inc(G("v1_ready", s), 1)
                    w.next(G("v1_ready", s))
                    w.next(G("y_ready", s))
                    w.link(nc.vector.scalar_tensor_tensor(out=V2[s][:], in0=V1[s][:], scalar=filt_b[:, 0:1],
                                                          in1=ps[:, 0, :], op0=ALU.mult, op1=ALU.add))
                    nc.vector.tensor_tensor(V3[s][:], V2[s][:], CV[s][:, 0, :], ALU.mult)\
                        .then_inc(G("v3_ready", s), 1)
                    dve.wait_ge(G("mask_loaded", s), 16)
                    nc.vector.tensor_scalar(PEN[s][:], MK[s][:], 0, MASKED, ALU.is_equal, ALU.mult)
                    w.next(G("o_ready", s))
                    residual(s, bank(s, 1), b_out)

                def cross0(s):
                    w.next(G("s_ready", s))
                    w.link(nc.vector.scalar_tensor_tensor(
                        out=LG[s][:], in0=PS[s][:, 1, 0:NB * C].rearrange("p (k c) -> p k c", k=NB),
                        scalar=float(D) ** -0.5, in1=PEN[s][:], op0=ALU.mult, op1=ALU.add))
                    w.link(nc.vector.tensor_reduce(ST[s][:, 0, :], LG[s][:], AX.X, ALU.max))
                    nc.vector.tensor_tensor(LG[s][:], LG[s][:], spread(ST[s][:, 0, :], 2, C), ALU.subtract)\
                        .then_inc(G("l_ready", s), 1)
                    w.next(G("p_ready", s))
                    w.link(nc.vector.tensor_reduce(ST[s][:, 1, :], LE[s][:], AX.X, ALU.add))
                    w.link(nc.vector.reciprocal(ST[s][:, 2, :], ST[s][:, 1, :]))
                    w.next(G("o_ready", s))
                    w.link(nc.vector.tensor_tensor(R2[s][:], bank(s, 3), spread(ST[s][:, 2, :], 2, P), ALU.mult))
                    normalise(s, R2[s], R2[s], 1e-5, None)
                    w.link(nc.vector.tensor_tensor(R2[s][:], R2[s][:], spread(gamma[:], 1, NB), ALU.mult))
                    w.link(nc.vector.tensor_tensor(R2[s][:], R2[s][:], spread(beta[:], 1, NB), ALU.add))
                    residual(s, R2[s][:], None)

                def quantise_scales(s, deq):
                    w.link(nc.vector.tensor_tensor(ST[s][:, 1, :], ST[s][:, 0, :], RS[s][:, 0:NB], ALU.mult))
                    w.link(nc.vector.tensor_scalar(ST[s][:, 1, :], ST[s][:, 1, :], 1e-5, None, ALU.max))
                    w.link(nc.vector.reciprocal(ST[s][:, 3, :], ST[s][:, 1, :]))
                    nc.vector.tensor_scalar(ST[s][:, 5, :], ST[s][:, 1, :], deq, None, ALU.mult)
                    w.link(nc.vector.tensor_scalar(ST[s][:, 3, :], ST[s][:, 3, :], 127.0, None, ALU.mult))

                def bitffn(s):
                    ps = PS[s]
                    w.link(nc.vector.tensor_tensor(R2[s][:], X[s][:], X[s][:], ALU.mult))
                    nc.vector.tensor_reduce(ST[s][:, 0, :], X[s][:], AX.X, ALU.max, apply_absolute_value=True)
                    w.link(nc.vector.tensor_reduce(ST[s][:, 2, :], R2[s][:], AX.X, ALU.add))
                    rsqrt(s, nc.vector.tensor_scalar(VE[s][:, 0:NB], ST[s][:, 2, :], 1.0 / D, 1e-6,
                                                     ALU.mult, ALU.add))
                    quantise_scales(s, q_deq[:, 0:1])
                    for k in range(NB):
                        ins = nc.vector.tensor_scalar(QF[s][:, k, :], X[s][:, k, :], RS[s][:, k:k + 1],
                                                      ST[s][:, 3, k:k + 1], ALU.mult, ALU.mult)
                    w.link(ins)
                    nc.vector.tensor_scalar(QB[s][:], QF[s][:], ROUND, -ROUND, ALU.add, ALU.add)\
                        .then_inc(G("q_ready", s), 1)
                    for k in range(NB):
                        w.next(G("h_ready", s))
                        nc.vector.scalar_tensor_tensor(out=BIG1[s][:, k, :], in0=ps[:, k, :],
                                                       scalar=ST[s][:, 5, k:k + 1], in1=b1[:],
                                                       op0=ALU.mult, op1=ALU.add).then_inc(G("hpre_ready", s), 1)
                    w.next(G("g_ready", s), NB)
                    nc.vector.tensor_reduce(ST[s][:, 0, :], BIG2[s], AX.X, ALU.max, apply_absolute_value=True)
                    rsqrt(s, nc.vector.tensor_scalar(VE[s][:, 0:NB], ST[s][:, 4, :], 1.0 / F, 1e-6,
                                                     ALU.mult, ALU.add))
                    quantise_scales(s, q_deq[:, 1:2])
                    for k in range(NB):
                        w.link(nc.vector.tensor_scalar(BIG1[s][:, k, :], BIG2[s][:, k, :], RS[s][:, k:k + 1],
                                                       ST[s][:, 3, k:k + 1], ALU.mult, ALU.mult))
                        nc.vector.tensor_scalar(HQ[s][:, k, :], BIG1[s][:, k, :], ROUND, -ROUND,
                                                ALU.add, ALU.add).then_inc(G("q_ready", s), 1)
                    w.next(G("o_ready", s))
                    w.link(nc.vector.tensor_tensor(R2[s][:], bank(s, 0), spread(ST[s][:, 5, :], 2, P), ALU.mult))
                    w.link(nc.vector.tensor_tensor(R2[s][:], R2[s][:], spread(b2[:], 1, NB), ALU.add))
                    residual(s, R2[s][:], None)

                def scan(s):
                    ps = PS[s]
                    for j, b in enumerate([1, 2, 3, 0]):
                        w.next(G("u_ready", s))
                        w.next(G("g_ready", s))
                        t = TU[s] if j < DJ else TR[s]
                        ins = nc.vector.scalar_tensor_tensor(out=t[:, j % DJ, :], in0=t[:, j % DJ, :], scalar=1.0,
                                                             in1=ps[:, b, :], op0=ALU.add, op1=ALU.mult)
                        if j < DJ:
                            w.link(ins)
                            nc.vector.tensor_scalar(UU[s][:, j, :], t[:, j, :], 0.5, None, ALU.mult)\
                                .then_inc(G("silu_u", s), 1)
                        else:
                            ins.then_inc(G("silu_r", s), 1)
                    w.next(G("silu_u", s), DJ)
                    for j in range(DJ):
                        w.next(G("d_ready", s))
                        w.next(G("ln_ready", s))
                        w.link(nc.vector.tensor_scalar(DL[s][:, j, :], ps[:, 1 + j, :], m_bdelta[:, j:j + 1], 0.0,
                                                       ALU.add, ALU.max))
                    nc.vector.tensor_tensor(DL[s][:], DL[s][:], SPA[s][:], ALU.add).then_inc(G("delta_ready", s), 1)
                    w.next(G("delta_ready", s))
                    nc.vector.tensor_tensor(DU[s][:], DL[s][:], UU[s][:], ALU.mult)
                    w.next(G("bc_ready", s))
                    bc = ps[0:2 * NS, 3, :]
                    w.link(nc.vector.tensor_copy(BCS[s][0:2 * NS, :], bc))
                    w.link(nc.vector.tensor_tensor(BC1[s][:], bc, BCS[s][0:2 * NS, :], ALU.subtract))
                    w.link(nc.vector.tensor_copy(BCM[s][:], BC1[s][:]))
                    nc.vector.tensor_copy(BCS[s][2 * NS:4 * NS, :], BCM[s][:])
                    nc.vector.tensor_tensor(BCS[s][4 * NS:6 * NS, :], BC1[s][:], BCM[s][:], ALU.subtract)\
                        .then_inc(G("bcs_ready", s), 1)
                    flat = "p a b -> p (a b)"
                    for n in range(NS):
                        w.next(G("B_ready", s))
                        nc.vector.tensor_tensor(dBu[s][:], DU[s][:], spread(ps[:, 0, :], 1, DJ), ALU.mult)\
                            .then_inc(G("dbu_done", s), 1)
                        w.next(G("dbu_done", s))
                        w.next(G("dA_ready", s))
                        nc.vector.tensor_tensor_scan(HS[s][:].rearrange(flat), dA[:, n % 2].rearrange(flat),
                                                     dBu[s][:].rearrange(flat), 0.0, ALU.mult, ALU.add)\
                            .then_inc(G("scan_done", s), 1)
                        w.next(G("scan_done", s))
                        w.next(G("C_ready", s))
                        if n >= 2:
                            w.next(G("y_acc", s))
                        nc.vector.tensor_tensor(HC[s][:, n % 2], HS[s][:], spread(ps[:, 3, :], 1, DJ), ALU.mult)\
                            .then_inc(G("hc_done", s), 1)
                    w.next(G("y_acc", s), 2)
                    for j in range(DJ):
                        ins = nc.vector.scalar_tensor_tensor(out=TU[s][:, j, :], in0=UU[s][:, j, :],
                                                             scalar=m_D[:, j:j + 1], in1=ps[:, 1 + j, :],
                                                             op0=ALU.mult, op1=ALU.add)
                    w.link(ins)
                    nc.vector.scalar_tensor_tensor(out=TU[s][:], in0=TU[s][:], scalar=0.5, in1=TR[s][:],
                                                   op0=ALU.mult, op1=ALU.mult).then_inc(G("yg_ready", s), 1)
                    w.next(G("o_ready", s))
                    residual(s, bank(s, 0), None)

                def cross1(s):
                    ps = PS[s]
                    w.next(G("ksq_ready", s), 2)
                    w.link(nc.vector.tensor_reduce(VE[s][0:C, 0:H], KQ[s][:], AX.X, ALU.add))
                    rsqrt(s, nc.vector.tensor_scalar(VE[s][0:C, 0:H], VE[s][0:C, 0:H], 1.0 / E, 1e-6,
                                                     ALU.mult, ALU.add))
                    w.next(G("k_ready", s), 2)
                    for j in range(2):
                        ins = nc.vector.tensor_tensor(
                            KN[s][:, j * 8:(j + 1) * 8, :], ps[0:C, 1 + j, :].rearrange("p (a b) -> p a b", b=E),
                            spread(RS[s][0:C, j * 8:(j + 1) * 8], 2, E), ALU.mult)
                    ins.then_inc(G("kn_ready", s), 1)
                    w.next(G("ssq_ready", s))
                    rsqrt(s, nc.vector.tensor_scalar(VE[s][:, 0:NB * H], ps[:, 3, 512 - NB * H:512], 1.0 / E, 1e-6,
                                                     ALU.mult, ALU.add))

                    def out_unit(u):
                        w.next(G("o_ready", s))
                        o = ps[:, 3, 0:HG * (E + 1)].rearrange("p (h e) -> p h e", e=E + 1)
                        w.link(nc.vector.reciprocal(RD[s][:], o[:, :, E]))
                        g = u // 2
                        c = (g % NG) * 2 * HG * E
                        to = ON[s][:, g // NG, c:c + 2 * HG * E].rearrange("p (h a e) -> p a h e", a=2, e=E)[:, u % 2]
                        nc.vector.tensor_tensor(to, o[:, :, 0:E], spread(RD[s][:], 2, E), ALU.mult)\
                            .then_inc(G("o_drained", s), 1)

                    for g in range(NB * NG):
                        k, half = g // NG, g % NG
                        w.next(G("s_ready", s))
                        raw = ps[:, 0:2, 0:HG * C].rearrange("p a (h c) -> p a h c", c=C)
                        mx = MX[s]
                        r0 = k * H + half * 2 * HG
                        rs = RS[s][:, r0:r0 + 2 * HG].rearrange("p (h a) -> p a h", a=2)
                        w.link(nc.vector.tensor_reduce(mx, raw, AX.X, ALU.max))
                        nc.vector.tensor_tensor(SC[s][:, g % 2], raw, spread(mx, 3, C), ALU.subtract)\
                            .then_inc(G("s_drained", s), 1)
                        w.next(G("s_drained", s))
                        nc.vector.tensor_tensor(SC[s][:, g % 2], SC[s][:, g % 2], spread(rs, 3, C), ALU.mult)\
                            .then_inc(G("l_ready", s), 1)
                        if g >= 1:
                            out_unit(2 * g - 2)
                            out_unit(2 * g - 1)
                    out_unit(2 * NB * NG - 2)
                    out_unit(2 * NB * NG - 1)
                    w.next(G("wh_used", s), 2 * NB)
                    residual(s, bank(s, 3), a_bo)

                def experts(s):
                    ps = PS[s]
                    w.link(nc.vector.tensor_tensor(R2[s][:], X[s][:], X[s][:], ALU.mult))
                    w.link(nc.vector.tensor_reduce(ST[s][:, 2, :], R2[s][:], AX.X, ALU.add))
                    rsqrt(s, nc.vector.tensor_scalar(VE[s][:, 0:NB], ST[s][:, 2, :], 1.0 / D, 1e-6,
                                                     ALU.mult, ALU.add))
                    for k in range(NB):
                        ins = nc.vector.tensor_scalar(R[s][:, k, :], X[s][:, k, :], RS[s][:, k:k + 1], None, ALU.mult)
                    ins.then_inc(G("xr_ready", s), 1)

                    def thresholds(k):
                        w.next(G("sim_sb", s))
                        sims = SIM[s][:, k, :].rearrange("p (a h n) -> p a h n", a=2, h=PH)
                        for a in range(2):
                            for h in range(PH):
                                ins = nc.vector.max(T8[s][:, a, h, :], sims[:, a, h, :])
                        w.link(ins)
                        w.link(nc.vector.tensor_tensor(A64[s][:], spread(T8[s][:, 0], 3, TOP),
                                                       spread(T8[s][:, 1], 2, TOP), ALU.add))
                        for h in range(PH):
                            ins = nc.vector.max(TT[s][:, h, :], A64[s][:, h].rearrange("p a b -> p (a b)"))
                        w.link(ins)
                        w.link(nc.vector.tensor_scalar(TH[s][:], TT[s][:, :, TOP - 1], 0.0, None, ALU.max))

                    def gates(k):
                        sims = SIM[s][:, k, :].rearrange("p (a h n) -> p a h n", a=2, h=PH)
                        for h in range(PH):
                            v = SV[s][:].rearrange("p (i j) -> p i j", i=NK)
                            w.link(nc.vector.tensor_tensor(v, spread(sims[:, 0, h, :], 2, NK),
                                                           spread(sims[:, 1, h, :], 1, NK), ALU.add))
                            if k * PH + h >= WB:
                                w.next(G("wh_used", s))
                            w_ins = nc.vector.scalar_tensor_tensor(
                                out=WH[s][:, h % WB, :], in0=SV[s][:], scalar=TH[s][:, h:h + 1], in1=SV[s][:],
                                op0=ALU.is_ge, op1=ALU.mult)
                            w_ins.then_inc(G("wh_ready", s), 1)
                            w.next(G("wh_ready", s))
                        gates_used = None

                    thresholds(0)
                    for k in range(NB):
                        gates(k)
                        w.next(G("wh_used", s), 4 if k == NB - 1 else 0) if k == NB - 1 else \
                            dve.wait_ge(G("wh_used", s), 2 * NB + (k + 1) * PH)
                        w.next(G("g_sb", s))
                        nc.vector.tensor_tensor(HW[s][:], HW[s][:], ps[:, 0:2, :].rearrange("p a b -> p (a b)"), ALU.mult)\
                            .then_inc(G("hw_ready", s), 1)
                        if k + 1 < NB:
                            thresholds(k + 1)
                    w.next(G("o_drained", s), NB)
                    residual(s, OS[s][:], None)

                def passed(name, s, n):
                    key = sg[name][s].name if hasattr(sg[name][s], "name") else str(sg[name][s])
                    w.seen[key] = w.seen.get(key, 0) + n

                for phase in (hyena, cross0, bitffn, scan, cross1, experts):
                    for s in range(LANES):
                        if phase is experts:
                            passed("o_drained", s, NB * H // HG)
                        phase(s)

        def pool_program(block):
            @block.gpsimd
            def _(pool):
                w = Signals(pool)

                def rsqrt(s, n):
                    for _ in range(n):
                        w.next(sg["var_ready"][s])
                        nc.gpsimd.tensor_tensor(RS[s][:], VE[s][:], minus_half[:], ALU.pow)\
                            .then_inc(sg["rstd_ready"][s], 1)

                for n in (1, 2, 3, 1, 3, 2):
                    for s in range(LANES):
                        rsqrt(s, n)

        with nc.Fori(0, B // LANES) as it:
            body(it)
            for q in lane_sems:
                nc.gpsimd.sem_clear(q)
            nc.all_engine_barrier()


_INS = ['x', 'ctx_1024', 'mask_BxSxS2_ik1', 'L0_attn_w_in', 'L0_attn_b_in', 'L0_attn_w_conv',
        'L0_attn_b_conv', 'L0_attn_w1', 'L0_attn_b1', 'L0_attn_w2', 'L0_attn_b2', 'L0_attn_w3',
        'L0_attn_filt_bias', 'L0_attn_w_out', 'L0_attn_b_out', 'L0_xattn_gamma', 'L0_xattn_beta',
        'L0_ffn_w1', 'L0_ffn_b1', 'L0_ffn_w2', 'L0_ffn_b2', 'L1_attn_W_in', 'L1_attn_W_delta',
        'L1_attn_b_delta', 'L1_attn_W_B', 'L1_attn_W_C', 'L1_attn_A_log', 'L1_attn_D_param',
        'L1_attn_W_out', 'L1_xattn_Wq', 'L1_xattn_Wk', 'L1_xattn_Wv', 'L1_xattn_Wo', 'L1_xattn_bo',
        'L1_xattn_gq', 'L1_xattn_gk', 'L1_ffn_w_q', 'L1_ffn_keys', 'L1_ffn_expert_down',
        'L1_ffn_expert_up', 'L1_ffn_norm_w']


def kernel(**inputs):
    import numpy as _np
    import concourse.bacc as _bacc
    from concourse import mybir as _mybir
    from concourse.bass_utils import run_bass_kernel_spmd as _run

    nc = _bacc.Bacc("TRN2", target_bir_lowering=False, num_devices=1)
    arrays, args = {}, []
    for name in _INS:
        a = _np.ascontiguousarray(inputs[name])
        arrays[f"in_{name}_dram"] = a
        args.append(nc.dram_tensor(f"in_{name}_dram", a.shape, _mybir.dt.from_np(a.dtype), kind="ExternalInput").ap())
    args.append(nc.dram_tensor("out_0_dram", inputs["x"].shape, F32, kind="ExternalOutput").ap())
    decoder(nc, *args)
    r = _run(nc, [arrays], core_ids=[0])
    return r.results[0]["out_0_dram"]
```

```python
from contextlib import ExitStack

import numpy as np

import concourse.bass as bass
from concourse import mybir

ALU = mybir.AluOpType
ACT = mybir.ActivationFunctionType
AX = mybir.AxisListType
F32 = mybir.dt.float32
BF16 = mybir.dt.bfloat16
I32 = mybir.dt.int32

P = 128
MASKED = -9000000000000000.0
ROUND = 12582912.0


def spread(ap, axis, n):
    dims = [list(d) for d in ap.ap]
    dims.insert(axis, [0, n])
    return bass.AP(ap.tensor, ap.offset, dims)


class Signals:

    def __init__(self, eng, step=None):
        self.eng, self.step, self.steps, self.seen = eng, step, 0, {}

    def next(self, sem, n=1):
        key = sem.name if hasattr(sem, "name") else str(sem)
        self.seen[key] = self.seen.get(key, 0) + n
        self.eng.wait_ge(sem, self.seen[key])

    def link(self, instruction):
        self.steps += 1
        instruction.then_inc(self.step, 1)
        self.eng.wait_ge(self.step, self.steps)


def decoder(nc, x, ctx_1024, mask_BxSxS2_ik1, L0_attn_w_in, L0_attn_b_in, L0_attn_w_conv,
            L0_attn_b_conv, L0_attn_w1, L0_attn_b1, L0_attn_w2, L0_attn_b2, L0_attn_w3,
            L0_attn_filt_bias, L0_attn_w_out, L0_attn_b_out, L0_xattn_gamma, L0_xattn_beta,
            L0_ffn_w1, L0_ffn_b1, L0_ffn_w2, L0_ffn_b2, L1_attn_W_in, L1_attn_W_delta,
            L1_attn_b_delta, L1_attn_W_B, L1_attn_W_C, L1_attn_A_log, L1_attn_D_param,
            L1_attn_W_out, L1_xattn_Wq, L1_xattn_Wk, L1_xattn_Wv, L1_xattn_Wo, L1_xattn_bo,
            L1_xattn_gq, L1_xattn_gk, L1_ffn_w_q, L1_ffn_keys, L1_ffn_expert_down,
            L1_ffn_expert_up, L1_ffn_norm_w, out):
    B, S, D = x.shape
    C = ctx_1024.shape[1]
    NB = S // P
    FW = L0_attn_w2.shape[0]
    F = L0_ffn_w1.shape[0]
    FK = F // P
    DI = L1_attn_W_delta.shape[0]
    DJ = DI // P
    NS = L1_attn_W_B.shape[1]
    H, E = L1_xattn_Wq.shape[1:]
    HP = H * E // P
    PH, NK = L1_ffn_keys.shape[:2]
    NE = L1_ffn_expert_down.shape[0]
    EB = NE // P
    TOP = 8
    HG = 4
    NG = H // (2 * HG)
    LANES = 2
    LAG = 0
    WB = 4
    assert D == P and DJ == 2 and NE == NK * NK and 3 * 2 * NS <= P and F <= 512

    h_pad = nc.dram_tensor("h_pad", (3 * P,), F32, kind="Internal").ap()

    with ExitStack() as ctx:
        def sb(name, shape, dt=F32):
            return ctx.enter_context(nc.sbuf_tensor(name, shape, dt))

        def sem(name):
            return ctx.enter_context(nc.semaphore(name))

        def lanes(make, name, *a):
            return [make(f"{name}{s}", *a) for s in range(LANES)]

        PS = [ctx.enter_context(nc.psum_tensor(f"ps{s}", [P, 4, 512], F32)) for s in range(LANES)]

        ident = sb("ident", [P, P])
        ident_bf = sb("ident_bf", [P, P], BF16)
        ones = sb("ones", [P, P])
        pair_ones = sb("pair_ones", [P, 2])
        minus_half = sb("minus_half", [P, 64])
        row_pick = sb("row_pick", [96, 2 * NS, P], BF16)

        w_in = sb("w_in", [P, 2, P])
        conv_w = sb("conv_w", [P, 3, 3])
        conv_b = sb("conv_b", [P, 3])
        in_b = sb("in_b", [P, 3])
        f_w1 = sb("f_w1", [3, FW])
        f_b1 = sb("f_b1", [FW, 1])
        f_w2 = sb("f_w2", [FW, FW])
        f_b2 = sb("f_b2", [FW, 1])
        f_w3 = sb("f_w3", [FW, P])
        f_t = sb("f_t", [3, 1])
        f_z = sb("f_z", [FW, 1])
        f_e = sb("f_e", [FW, 1])
        f_h1 = sb("f_h1", [FW, 1])
        f_h2 = sb("f_h2", [FW, 1])
        f_decay = sb("f_decay", [1, P])
        f_row = sb("f_row", [1, 3 * P])
        fb_row = sb("fb_row", [1, P])
        filt_b = sb("filt_b", [P, 1])
        toe = sb("toe", [P, 2 * P])
        w_out = sb("w_out", [P, P])
        b_out = sb("b_out", [P, P])
        gamma = sb("gamma", [P, P])
        beta = sb("beta", [P, P])
        q_abs = sb("q_abs", [P, 2])
        q_clip = sb("q_clip", [P, 2])
        q_scale = sb("q_scale", [P, 2])
        q_deq = sb("q_deq", [P, 2])
        q1T = sb("q1T", [P, F], BF16)
        q2T = sb("q2T", [P, FK, P], BF16)
        b1 = sb("b1", [P, F])
        b2 = sb("b2", [P, P])
        m_in = sb("m_in", [P, 2 * DI])
        m_delta = sb("m_delta", [P, DJ, DI])
        m_bdelta = sb("m_bdelta", [P, DJ])
        m_bc = sb("m_bc", [P, DJ, 2 * NS])
        m_alog = sb("m_alog", [P, DJ, NS])
        m_aexp = sb("m_aexp", [P, DJ, NS])
        m_A = sb("m_A", [P, DJ, NS])
        m_D = sb("m_D", [P, DJ])
        m_out = sb("m_out", [P, DJ, P])
        a_q = sb("a_q", [P, H * E])
        a_k = sb("a_k", [P, H * E])
        a_v = sb("a_v", [P, H * E])
        a_o = sb("a_o", [P, HP, P])
        a_bo = sb("a_bo", [P, P])
        a_gq = sb("a_gq", [P, 1])
        a_gk = sb("a_gk", [P, 1])
        a_g = sb("a_g", [P, 1])
        p_m = sb("p_m", [P, 2 * PH * NK])
        p_downT = sb("p_downT", [P, NE])
        p_up = sb("p_up", [P, EB, P])
        p_norm = sb("p_norm", [P, 1])

        X = lanes(sb, "x", [P, NB, P])
        R = lanes(sb, "r", [P, NB, P])
        R2 = lanes(sb, "r2", [P, NB, P])
        XT = lanes(sb, "xT", [P, S])
        CT = lanes(sb, "c", [C, P])
        CTT = lanes(sb, "cT", [P, C])
        MK = lanes(sb, "mask", [P, NB, C], I32)
        BNS = lanes(sb, "bns", [P, NB, 6])
        MV = lanes(sb, "mv", [P, NB, 2])
        VE = lanes(sb, "ve", [P, 64])
        RS = lanes(sb, "rs", [P, 64])
        ST = lanes(sb, "st", [P, 6, NB])
        VV = lanes(sb, "vv", [C, H, E + 1])

        WORDS = 12 * 1024
        mem = lanes(sb, "mem", [P, WORDS])

        def carve(arena, sizes):
            at, pieces = 0, {}
            for name, (rows, shape, dt) in sizes.items():
                n = int(np.prod(shape))
                words = n if dt is not BF16 else n // 2
                piece = arena[0:rows, at:at + words]
                if dt is BF16:
                    piece = piece.bitcast(BF16)
                if len(shape) > 1:
                    axes = "abcd"[:len(shape)]
                    piece = piece.rearrange(f"p ({' '.join(axes)}) -> p {' '.join(axes)}",
                                            **dict(zip(axes[1:], shape[1:])))
                pieces[name] = piece
                at += words
            assert at <= arena.shape[1], (at, arena.shape)
            return pieces

        def per_lane(**sizes):
            made = [carve(mem[s], sizes) for s in range(LANES)]
            return [[m[name] for m in made] for name in sizes]

        U, CV, V1, V2, V3, VT, PEN = per_lane(
            u=(P, (2, S), F32), cv=(P, (2, S), F32), v1=(P, (S,), F32), v2=(P, (S,), F32),
            v3=(P, (S,), F32), vt=(P, (NB, P), F32), pen=(P, (NB, C), F32))
        pen_at = 8 * S
        _, LG, LE, PT = per_lane(
            hyena=(P, (pen_at + NB * C,), F32), lg=(P, (NB, C), F32), le=(P, (NB, C), F32), pt=(C, (S,), F32))
        BIG1, BIG2, QF, QB, QT, HQ, HT = per_lane(
            pre=(P, (NB, F), F32), act=(P, (NB, F), F32), qf=(P, (NB, P), F32), qb=(P, (NB, P), BF16),
            qt=(P, (S,), BF16), hq=(P, (NB, F), BF16), ht=(P, (NB, FK, P), BF16))
        TU, TR, UU, SPA, SPE, DL, DU, BCS, BC1, BCM, dBu, HS, HC = per_lane(
            tu=(P, (DJ, S), F32), tr=(P, (DJ, S), F32), uu=(P, (DJ, S), F32), spa=(P, (DJ, S), F32),
            spe=(P, (DJ, S), F32), dl=(P, (DJ, S), F32), du=(P, (DJ, S), F32), bcs=(96, (S,), BF16),
            bc1=(2 * NS, (S,), F32), bcm=(2 * NS, (S,), BF16), dbu=(P, (DJ, S), F32), hs=(P, (DJ, S), F32),
            hc=(P, (2, DJ, S), F32))
        _, dA = per_lane(front=(P, (3 * DJ * S,), F32), da=(P, (2, DJ, S), F32))
        ON, AQ, KN, KT, SC, AT, MX, RD = per_lane(
            on=(P, (NB, H * E), F32), aq=(P, (HP, S), F32), kn=(C, (H, E), F32), kt=(P, (HP, C), F32),
            sc=(P, (2, 2, HG, C), F32), at=(C, (2, HG, P), F32), mx=(P, (2, HG), F32), rd=(P, (HG,), F32))
        QSQ, = per_lane(qsq=(P, (HP, S), F32))
        _, OT = per_lane(front=(P, (NB * H * E,), F32), ot=(P, (2, 4, P), F32))
        _, KQ = per_lane(front=(P, (NB * H * E + HP * S + H * E + HP * C,), F32), kq=(C, (H, E), F32))
        SIM, OS, A64, T8, TT, TH, SV, WH, HW, HWT = per_lane(
            sim=(P, (NB, 2 * PH * NK), F32), os=(P, (NB, P), F32), a64=(P, (PH, TOP, TOP), F32),
            t8=(P, (2, PH, TOP), F32), tt=(P, (PH, TOP), F32), th=(P, (PH,), F32), sv=(P, (NE,), F32),
            wh=(P, (WB, NE), F32), hw=(P, (NE,), F32), hwT=(P, (EB, P), F32))

        prep = carve(mem[0], dict(q1_w=(P, (FK, P), F32), q2_w=(P, (F,), F32), q_t=(P, (F,), F32),
                                  p_q=(P, (2 * PH, P), F32), p_keys=(P, (2, 2, P), F32),
                                  p_keysT=(P, (4, P), F32), p_down=(P, (EB, P), F32),
                                  q1_n=(P, (FK, P), BF16), q2_n=(P, (F,), BF16),
                                  taps=(P, (2 * P,), F32)))
        q1_w, q2_w, q_t, p_q, p_keys, p_keysT, p_down, q1_n, q2_n, taps = prep.values()

        p_load = sem("p_load")
        p_const = sem("p_const")
        p_step_dve, p_step_act, p_step_pool = sem("p_step_dve"), sem("p_step_act"), sem("p_step_pool")
        p_pe = sem("p_pe")
        p_act = sem("p_act")
        p_dve = sem("p_dve")
        p_hrow = sem("p_hrow")
        p_hout = sem("p_hout")
        p_toe = sem("p_toe")

        names = """x_loaded ctx_loaded mask_loaded stored x_ready turned xT_ready u_ready u_sb
            conv0 v1_ready v_tm y_ready v3_ready o_ready var_ready rstd_ready ctx_turned ctxT_ready
            s_ready l_ready p_ready pT_ready q_ready qT_ready h_ready hpre_ready g_ready silu_u
            silu_r d_ready bc_ready ln_ready delta_ready bcs_ready B_ready C_ready dA_ready
            dbu_done scan_done hc_done y_acc yg_ready k_ready ksq_ready kn_ready kT_ready v_ready
            v_sb qsq_ready ssq_ready s_drained o_drained xr_ready sim_ready sim_sb wh_ready wh_used
            z_ready g_sb hw_ready hwT_ready t_ready aq_ready heads_used eo_ready eo_drained""".split()
        sg = {n: [sem(f"{n}{s}") for s in range(LANES)] for n in names}
        dve_step, act_step = sem("dve_step"), sem("act_step")
        lane_sems = [q for n in names for q in sg[n]] + [dve_step, act_step]

        def column(ap):
            return ap.rearrange("(p o) -> p o", o=1)

        def row(ap):
            return ap.rearrange("(o p) -> o p", o=1)

        def down(ap, n=P):
            return bass.AP(ap.tensor, ap.offset, [[0, n], *[list(d) for d in ap.ap]])

        loads = [
            (f_w1[:], L0_attn_w1), (f_b1[:], column(L0_attn_b1)), (f_w2[:], L0_attn_w2),
            (f_b2[:], column(L0_attn_b2)), (f_w3[:], L0_attn_w3), (fb_row[:], row(L0_attn_filt_bias)),
            (filt_b[:], column(L0_attn_filt_bias)),
            (w_in[:, 0, :], L0_attn_w_in[:, 0:P]), (w_in[:, 1, :], L0_attn_w_in[:, 2 * P:3 * P]),
            (conv_w[:], L0_attn_w_conv.rearrange("(c p) o k -> p c (o k)", p=P)),
            (conv_b[:], L0_attn_b_conv.rearrange("(c p) -> p c", p=P)),
            (in_b[:], L0_attn_b_in.rearrange("(c p) -> p c", p=P)),
            (w_out[:], L0_attn_w_out), (b_out[:], down(L0_attn_b_out)),
            (gamma[:], down(L0_xattn_gamma)), (beta[:], down(L0_xattn_beta)),
            (q1_w[:], L0_ffn_w1.rearrange("(k p) d -> p k d", p=P)), (q2_w[:], L0_ffn_w2),
            (b1[:], down(L0_ffn_b1)), (b2[:], down(L0_ffn_b2)),
            (m_in[:], L1_attn_W_in), (m_delta[:], L1_attn_W_delta.rearrange("(k p) m -> p k m", p=P)),
            (m_bdelta[:], L1_attn_b_delta.rearrange("(k p) -> p k", p=P)),
            (m_bc[:, :, 0:NS], L1_attn_W_B.rearrange("(k p) n -> p k n", p=P)),
            (m_bc[:, :, NS:2 * NS], L1_attn_W_C.rearrange("(k p) n -> p k n", p=P)),
            (m_alog[:], L1_attn_A_log.rearrange("(k p) n -> p k n", p=P)),
            (m_D[:], L1_attn_D_param.rearrange("(k p) -> p k", p=P)),
            (m_out[:], L1_attn_W_out.rearrange("(k p) m -> p k m", p=P)),
            (a_q[:], L1_xattn_Wq.rearrange("d h e -> d (h e)")),
            (a_k[:], L1_xattn_Wk.rearrange("d h e -> d (h e)")),
            (a_v[:], L1_xattn_Wv.rearrange("d h e -> d (h e)")),
            (a_o[:], L1_xattn_Wo.rearrange("(j t) e d -> (t e) j d", t=2)),
            (a_bo[:], down(L1_xattn_bo)),
            (a_gq[0:E, :], column(L1_xattn_gq)), (a_gq[E:2 * E, :], column(L1_xattn_gq)),
            (a_gk[0:E, :], column(L1_xattn_gk)), (a_gk[E:2 * E, :], column(L1_xattn_gk)),
            (p_q[:], L1_ffn_w_q.rearrange("(j e) d -> e j d", e=P)),
            (p_keys[:], L1_ffn_keys.rearrange("(t h) k j e -> (h k) t j e", t=2)),
            (p_down[:], L1_ffn_expert_down.rearrange("(b p) d -> p b d", p=P)),
            (p_up[:], L1_ffn_expert_up.rearrange("(b p) d -> p b d", p=P)),
            (p_norm[:], column(L1_ffn_norm_w)),
        ]
        ALL_LOADED = 16 * len(loads)

        with nc.Block() as block:
            @block.sync
            def _(sp):
                with nc.allow_non_contiguous_dma("small vectors down the partitions"):
                    for to, of in loads:
                        sp.dma_start(to, of).then_inc(p_load, 16)
                sp.wait_ge(p_hrow, 1)
                sp.dma_start(row(h_pad), f_row[:]).then_inc(p_hout, 16)
                sp.wait_ge(p_hout, 16)
                sp.dma_start(taps[:], bass.AP(h_pad.tensor, 0, [[1, P], [1, 2 * P]])).then_inc(p_toe, 16)

            @block.gpsimd
            def _(pool):
                w = Signals(pool, p_step_pool)
                w.link(nc.gpsimd.memset(minus_half[:], -0.5))
                w.link(nc.gpsimd.memset(ones[:], 1.0))
                w.link(nc.gpsimd.memset(ident[:], 0.0))
                w.link(nc.gpsimd.affine_select(out=ident[:], in_=ident[:], compare_op=ALU.not_equal,
                                               fill=1.0, base=0, pattern=[[-1, P]], channel_multiplier=1))
                w.link(nc.gpsimd.memset(row_pick[:], 0.0))
                for g in range(3):
                    w.link(nc.gpsimd.affine_select(
                        out=row_pick[:], in_=row_pick[:], compare_op=ALU.not_equal, fill=1.0,
                        base=-2 * NS * g, pattern=[[-1, 2 * NS], [0, P]], channel_multiplier=1))
                w.link(nc.gpsimd.memset(pair_ones[:], 0.0))
                w.link(nc.gpsimd.memset(pair_ones[0:E, 0:1], 1.0))
                w.link(nc.gpsimd.memset(pair_ones[E:2 * E, 1:2], 1.0))
                w.link(nc.gpsimd.memset(f_t[:], 0.0))
                for s in range(LANES):
                    w.link(nc.gpsimd.memset(VE[s][:], 1.0))
                    w.link(nc.gpsimd.memset(VV[s][:, :, E:E + 1], 1.0))
                nc.gpsimd.memset(f_row[:], 0.0).then_inc(p_const, 1)

            @block.tensor
            def _(pe):
                w = Signals(pe)
                pe.wait_ge(p_load, ALL_LOADED)
                pe.wait_ge(p_const, 1)
                pe.matmul(PS[0][0:FW, 0, 0:1], f_w1[:], f_t[:], start=True, stop=True).then_inc(p_pe, 1)
                pe.wait_ge(p_dve, 1)
                pe.matmul(PS[0][0:FW, 0, 1:2], f_w2[:], f_h1[:], start=True, stop=True).then_inc(p_pe, 1)
                pe.wait_ge(p_dve, 2)
                pe.matmul(PS[0][0:1, 0, 128:256], f_h2[:], f_w3[:, :], start=True, stop=True).then_inc(p_pe, 1)
                pe.wait_ge(p_dve, 3)
                pe.matmul(PS[0][:, 1, 0:2], ones[:], q_abs[:], start=True, stop=True).then_inc(p_pe, 1)
                for n in range(4):
                    mm = pe.transpose(PS[0][:, 2, n * P:(n + 1) * P], p_keys[:, n // 2, n % 2, :], ident[:])
                mm.then_inc(p_pe, 1)
                for n in range(EB):
                    mm = pe.transpose(PS[1][:, n // 4, (n % 4) * P:(n % 4 + 1) * P], p_down[:, n, :], ident[:])
                mm.then_inc(p_pe, 1)
                pe.wait_ge(p_act, 5)
                for j in range(2):
                    for h in range(PH):
                        c = (j * PH + h) * NK
                        n = (h // 4) * 2 + j
                        mm = pe.matmul(PS[0][:, 3, c:c + NK], p_q[:, 2 * h + j, :],
                                       p_keysT[:, n, (h % 4) * NK:(h % 4 + 1) * NK], start=True, stop=True)
                mm.then_inc(p_pe, 1)
                pe.wait_ge(p_dve, 4)
                for k in range(FK):
                    pe.transpose(PS[1][:, 2, :].bitcast(BF16)[:, k * P:(k + 1) * P], q1_n[:, k, :], ident_bf[:])
                for k in range(FK):
                    mm = pe.transpose(PS[1][:, 3, :].bitcast(BF16)[:, k * P:(k + 1) * P],
                                      q2_n[:, k * P:(k + 1) * P], ident_bf[:])
                mm.then_inc(p_pe, 1)

            @block.scalar
            def _(act):
                w = Signals(act, p_step_act)
                act.wait_ge(p_load, ALL_LOADED)
                act.wait_ge(p_const, 1)
                for n in range(2):
                    act.wait_ge(p_step_dve, n + 1)
                    nc.scalar.activation(f_e[:], f_z[:], ACT.Tanh, scale=0.5).then_inc(p_act, 1)
                w.link(nc.scalar.activation(f_decay[:], fb_row[:], ACT.Abs))
                nc.scalar.activation(f_decay[:], f_decay[:], ACT.Exp, scale=-0.0).then_inc(p_act, 1)
                nc.scalar.activation(m_aexp[:], m_alog[:], ACT.Exp).then_inc(p_act, 1)
                act.wait_ge(p_pe, 5)
                nc.scalar.activation(p_keysT[:].rearrange("p a b -> p (a b)"), PS[0][:, 2, :], ACT.Copy)\
                    .then_inc(p_act, 1)
                act.wait_ge(p_pe, 6)
                nc.scalar.activation(p_downT[:].rearrange("p (a b) -> p a b", a=2), PS[1][:, 0:2, :], ACT.Copy)
                act.wait_ge(p_pe, 7)
                nc.scalar.activation(p_m[:], PS[0][:, 3, :], ACT.Copy)
                act.wait_ge(p_pe, 8)
                nc.scalar.activation(q1T[:], PS[1][:, 2, :].bitcast(BF16)[:, 0:F], ACT.Copy)
                nc.scalar.activation(q2T[:].rearrange("p a b -> p (a b)"),
                                     PS[1][:, 3, :].bitcast(BF16)[:, 0:F], ACT.Copy)

            @block.vector
            def _(dve):
                w = Signals(dve, p_step_dve)
                dve.wait_ge(p_load, ALL_LOADED)
                dve.wait_ge(p_const, 1)
                for n, (b, h) in enumerate([(f_b1, f_h1), (f_b2, f_h2)]):
                    dve.wait_ge(p_pe, n + 1)
                    w.link(nc.vector.tensor_tensor(f_z[:], PS[0][0:FW, 0, n:n + 1], b[:], ALU.add))
                    dve.wait_ge(p_act, n + 1)
                    w.steps += 0
                    nc.vector.scalar_tensor_tensor(out=h[:], in0=f_e[:], scalar=1.0, in1=f_z[:],
                                                   op0=ALU.add, op1=ALU.mult)
                    dve.drain()
                    nc.vector.tensor_scalar(h[:], h[:], 0.5, None, ALU.mult).then_inc(p_dve, 1)
                nc.vector.tensor_copy(ident_bf[:], ident[:])
                nc.vector.tensor_reduce(q_abs[:, 0:1], q1_w[:].rearrange("p a b -> p (a b)"), AX.X, ALU.add,
                                        apply_absolute_value=True)
                nc.vector.tensor_reduce(q_abs[:, 1:2], q2_w[:], AX.X, ALU.add,
                                        apply_absolute_value=True).then_inc(p_dve, 1)
                dve.wait_ge(p_pe, 3)
                dve.wait_ge(p_act, 3)
                nc.vector.tensor_tensor(f_row[:, P:2 * P], PS[0][0:1, 0, 128:256][:, ::-1],
                                        f_decay[:, ::-1], ALU.mult).then_inc(p_hrow, 1)
                dve.wait_ge(p_pe, 4)
                w.link(nc.vector.tensor_scalar(q_clip[:], PS[0][:, 1, 0:2], 1.0 / (F * D), 1e-5,
                                               ALU.mult, ALU.max))
                w.link(nc.vector.reciprocal(q_scale[:], q_clip[:]))
                nc.vector.tensor_scalar(q_deq[:], q_clip[:], 1.0 / 127.0, None, ALU.mult)
                for k, (of, to) in enumerate([(q1_w[:].rearrange("p a b -> p (a b)"),
                                               q1_n[:].rearrange("p a b -> p (a b)")), (q2_w[:], q2_n[:])]):
                    w.link(nc.vector.tensor_scalar(q_t[:], of, q_scale[:, k:k + 1], ROUND, ALU.mult, ALU.add))
                    w.link(nc.vector.tensor_scalar(q_t[:], q_t[:], -ROUND, 1.0, ALU.add, ALU.min))
                    last = nc.vector.tensor_scalar(to, q_t[:], -1.0, None, ALU.max)
                    if k == 0:
                        w.link(last)
                last.then_inc(p_dve, 1)
                w.link(nc.vector.tensor_tensor(a_g[:], a_gq[:], a_gk[:], ALU.mult))
                w.link(nc.vector.tensor_scalar(a_g[:], a_g[:], float(E) ** -0.5, None, ALU.mult))
                dve.wait_ge(p_act, 4)
                nc.vector.tensor_scalar(m_A[:], m_aexp[:], -1.0, None, ALU.mult)
                dve.wait_ge(p_toe, 16)
                nc.vector.tensor_copy(toe[:], taps[:, ::-1])

        def in_turn(program):
            runs = [program(s) for s in range(LANES)]
            stage = [next(r) for r in runs]
            while any(n is not None for n in stage):
                s = min((n + LAG * s, s) for s, n in enumerate(stage) if n is not None)[1]
                stage[s] = next(runs[s], None)

        def sublayers(phases):
            def program(s):
                for n, phase in enumerate(phases):
                    for stage in phase(s):
                        yield 100 * n + stage
            return program

        def body(it):
            with nc.Block() as block:
                @block.sync
                def _(sp):
                    for s in range(LANES):
                        i = 2 * it + s
                        sp.dma_start(X[s][:], x[bass.ds(i, 1)].rearrange("o (k p) d -> p (o k) d", p=P))\
                            .then_inc(sg["x_loaded"][s], 16)
                        sp.dma_start(CT[s][:], ctx_1024[bass.ds(i, 1)].rearrange("o c d -> (o c) d"))\
                            .then_inc(sg["ctx_loaded"][s], 16)
                        sp.dma_start(MK[s][:], mask_BxSxS2_ik1[bass.ds(i, 1)]
                                     .rearrange("o (k p) c -> p (o k) c", p=P)).then_inc(sg["mask_loaded"][s], 16)
                    for s in range(LANES):
                        i = 2 * it + s
                        sp.wait_ge(sg["x_ready"][s], 6)
                        sp.dma_start(out[bass.ds(i, 1)].rearrange("o (k p) d -> p (o k) d", p=P), X[s][:])\
                            .then_inc(sg["stored"][s], 16)
                    for s in range(LANES):
                        sp.wait_ge(sg["stored"][s], 16)

                pe_program(block)
                act_program(block)
                dve_program(block)
                pool_program(block)

        def pe_program(block):
            @block.tensor
            def _(pe):
                w = Signals(pe)

                def G(n, s):
                    return sg[n][s]

                def turn(s, of, bank):
                    for k in range(NB):
                        mm = pe.transpose(PS[s][:, bank, k * P:(k + 1) * P], of[:, k, :], ident[:])
                    mm.then_inc(G("turned", s), 1)

                def hyena(s):
                    ps = PS[s]
                    yield 0
                    pe.wait_ge(G("x_loaded", s), 16)
                    turn(s, X[s], 0)
                    pe.wait_ge(G("ctx_loaded", s), 16)
                    pe.transpose(ps[:, 3, 0:C], CT[s][:], ident[0:C, 0:C]).then_inc(G("ctx_turned", s), 1)
                    yield 1
                    w.next(G("xT_ready", s))
                    for j in range(2):
                        pe.matmul(ps[:, 1 + j, :], w_in[:, j, :], XT[s][:], start=True, stop=True)\
                            .then_inc(G("u_ready", s), 1)
                    yield 2
                    w.next(G("v1_ready", s))
                    w.next(G("ctxT_ready", s))
                    for k in range(NB):
                        mm = pe.transpose(ps[:, 3, k * P:(k + 1) * P], V1[s][:, k * P:(k + 1) * P], ident[:])
                    mm.then_inc(G("turned", s), 1)
                    yield 3
                    w.next(G("v_tm", s))
                    for k in range(NB):
                        n = min(2 * P, S - k * P)
                        mm = pe.matmul(ps[:, 0, k * P:k * P + n], VT[s][:, k, :], toe[:, 0:n],
                                       start=(k == 0), stop=(k == NB - 1), skip_group_check=True)
                    mm.then_inc(G("y_ready", s), 1)
                    yield 4
                    w.next(G("v3_ready", s))
                    for k in range(NB):
                        mm = pe.matmul(ps[:, 1, k * P:(k + 1) * P], V3[s][:, k * P:(k + 1) * P], w_out[:],
                                       start=True, stop=True)
                    mm.then_inc(G("o_ready", s), 1)

                def cross0(s):
                    ps = PS[s]
                    yield 0
                    w.next(G("x_ready", s))
                    turn(s, X[s], 0)
                    yield 1
                    w.next(G("xT_ready", s))
                    for k in range(NB):
                        mm = pe.matmul(ps[:, 1, k * C:(k + 1) * C], XT[s][:, k * P:(k + 1) * P], CTT[s][:],
                                       start=True, stop=True)
                    mm.then_inc(G("s_ready", s), 1)
                    yield 2
                    w.next(G("p_ready", s))
                    for k in range(NB):
                        mm = pe.transpose(ps[0:C, 2, k * P:(k + 1) * P], LE[s][:, k, :], ident[:])
                    mm.then_inc(G("turned", s), 1)
                    yield 3
                    w.next(G("pT_ready", s))
                    for k in range(NB):
                        mm = pe.matmul(ps[:, 3, k * P:(k + 1) * P], PT[s][:, k * P:(k + 1) * P], CT[s][:],
                                       start=True, stop=True)
                    mm.then_inc(G("o_ready", s), 1)

                def bitffn(s):
                    ps = PS[s]
                    yield 1
                    w.next(G("x_ready", s))
                    w.next(G("q_ready", s))
                    for k in range(NB):
                        mm = pe.transpose(ps[:, 0, :].bitcast(BF16)[:, k * P:(k + 1) * P], QB[s][:, k, :],
                                          ident_bf[:])
                    mm.then_inc(G("turned", s), 1)
                    yield 2
                    w.next(G("qT_ready", s))
                    for k in range(NB):
                        pe.matmul(ps[:, k, :], QT[s][:, k * P:(k + 1) * P], q1T[:], start=True, stop=True)\
                            .then_inc(G("h_ready", s), 1)
                    yield 4
                    for k in range(NB):
                        w.next(G("q_ready", s))
                        for j in range(FK):
                            mm = pe.transpose(ps[:, k, :].bitcast(BF16)[:, j * P:(j + 1) * P],
                                              HQ[s][:, k, j * P:(j + 1) * P], ident_bf[:])
                        mm.then_inc(G("turned", s), 1)
                    yield 5
                    w.next(G("qT_ready", s), NB)
                    for k in range(NB):
                        for j in range(FK):
                            mm = pe.matmul(ps[:, 0, k * P:(k + 1) * P], HT[s][:, k, j, :], q2T[:, j, :],
                                           start=(j == 0), stop=(j == FK - 1))
                    mm.then_inc(G("o_ready", s), 1)

                def scan(s):
                    ps = PS[s]
                    yield 0
                    w.next(G("x_ready", s))
                    turn(s, X[s], 0)
                    yield 1
                    w.next(G("xT_ready", s))
                    for j, bank in enumerate([1, 2, 3, 0]):
                        pe.matmul(ps[:, bank, :], m_in[:, j * P:(j + 1) * P], XT[s][:], start=True, stop=True)\
                            .then_inc(G("u_ready", s), 1)
                    yield 2
                    w.next(G("silu_u", s), DJ)
                    for m in range(DJ):
                        for k in range(DJ):
                            mm = pe.matmul(ps[:, 1 + m, :], m_delta[:, k, m * P:(m + 1) * P], UU[s][:, k, :],
                                           start=(k == 0), stop=(k == DJ - 1))
                        mm.then_inc(G("d_ready", s), 1)
                    w.next(G("silu_r", s), DJ)
                    for k in range(DJ):
                        mm = pe.matmul(ps[0:2 * NS, 3, :], m_bc[:, k, :], UU[s][:, k, :],
                                       start=(k == 0), stop=(k == DJ - 1))
                    mm.then_inc(G("bc_ready", s), 1)

                    def broadcast(row_n, bank, ready):
                        pe.matmul(ps[:, bank, :], row_pick[:, row_n, :], BCS[s][:], start=True, stop=True)\
                            .then_inc(G(ready, s), 1)

                    yield 3
                    w.next(G("bcs_ready", s))
                    w.next(G("delta_ready", s))
                    broadcast(0, 0, "B_ready")
                    broadcast(NS, 3, "C_ready")
                    for n in range(NS):
                        yield 4 + n
                        if n + 1 < NS:
                            w.next(G("dbu_done", s))
                            broadcast(n + 1, 0, "B_ready")
                        w.next(G("hc_done", s))
                        if n + 1 < NS:
                            broadcast(NS + n + 1, 3, "C_ready")
                        for j in range(DJ):
                            mm = pe.matmul(ps[:, 1 + j, :], ident[:], HC[s][:, n % 2, j, :],
                                           start=(n == 0), stop=(n == NS - 1), skip_group_check=True)
                        mm.then_inc(G("y_acc", s), 1)
                    yield 5 + NS
                    w.next(G("yg_ready", s))
                    for k in range(NB):
                        for j in range(DJ):
                            mm = pe.matmul(ps[:, 0, k * P:(k + 1) * P], TU[s][:, j, k * P:(k + 1) * P],
                                           m_out[:, j, :], start=(j == 0), stop=(j == DJ - 1))
                    mm.then_inc(G("o_ready", s), 1)

                def cross1(s):
                    ps = PS[s]
                    yield 0
                    w.next(G("x_ready", s))
                    turn(s, X[s], 0)
                    for j in range(2):
                        pe.matmul(ps[0:C, 1 + j, :], CTT[s][:], a_k[:, j * 512:(j + 1) * 512],
                                  start=True, stop=True).then_inc(G("k_ready", s), 1)
                    pe.matmul(ps[0:C, 3, :], CTT[s][:], a_v[:, 0:512], start=True, stop=True)\
                        .then_inc(G("v_ready", s), 1)
                    yield 1
                    w.next(G("xT_ready", s))
                    pe.matmul(ps[0:C, 0, :], CTT[s][:], a_v[:, 512:1024], start=True, stop=True)\
                        .then_inc(G("v_ready", s), 1)
                    yield 2
                    w.next(G("kn_ready", s))
                    for j in range(HP):
                        mm = pe.transpose(ps[:, 1 + j // 4, (j % 4) * C:(j % 4 + 1) * C],
                                          KN[s][:, 2 * j:2 * j + 2, :].rearrange("p a b -> p (a b)"),
                                          ident[0:C, 0:C])
                    mm.then_inc(G("turned", s), 1)
                    for j in range(HP):
                        yield 3 + j
                        bank = [3, 0, 1, 2][j % 4]
                        if j < 2:
                            w.next(G("v_sb", s))
                        elif j == 2:
                            w.next(G("kT_ready", s))
                        elif j >= 4:
                            w.next(G("qsq_ready", s))
                        pe.matmul(ps[:, bank, :], a_q[:, j * P:(j + 1) * P], XT[s][:], start=True, stop=True)\
                            .then_inc(G("aq_ready", s), 1)
                    yield 11
                    w.next(G("qsq_ready", s), 4)
                    for k in range(NB):
                        for j in range(HP):
                            c = 512 - NB * H + k * H + 2 * j
                            mm = pe.matmul(ps[:, 3, c:c + 2], QSQ[s][:, j, k * P:(k + 1) * P],
                                           pair_ones[:], start=True, stop=True)
                    mm.then_inc(G("ssq_ready", s), 1)

                    def scores(g):
                        k, half = g // NG, g % NG
                        if g >= 1:
                            w.next(G("s_drained", s))
                        for h in range(2 * HG):
                            hh = half * 2 * HG + h
                            lo = (hh % 2) * E
                            mm = pe.matmul(ps[:, h % 2, (h // 2) * C:(h // 2 + 1) * C],
                                           AQ[s][lo:lo + E, hh // 2, k * P:(k + 1) * P],
                                           KT[s][lo:lo + E, hh // 2, :], start=True, stop=True)
                        mm.then_inc(G("s_ready", s), 1)

                    def weights_turned(u):
                        g = u // 2
                        if u % 2 == 0:
                            w.next(G("p_ready", s))
                        for h in range(HG):
                            mm = pe.transpose(ps[0:C, 2, h * P:(h + 1) * P], SC[s][:, g % 2, u % 2, h, :], ident[:])
                        mm.then_inc(G("turned", s), 1)

                    def values(u):
                        g = u // 2
                        if u >= 1:
                            w.next(G("o_drained", s))
                        for h in range(HG):
                            hh = (g % NG) * 2 * HG + 2 * h + u % 2
                            mm = pe.matmul(ps[:, 3, h * (E + 1):(h + 1) * (E + 1)], AT[s][:, u % 2, h, :],
                                           VV[s][:, hh, :], start=True, stop=True)
                        mm.then_inc(G("o_ready", s), 1)

                    NU = NB * H // HG
                    yield 19
                    scores(0)
                    for u in range(NU + 1):
                        yield 20 + u
                        if u % 2 == 0 and u // 2 + 1 < NB * NG:
                            scores(u // 2 + 1)
                        if u >= 1:
                            w.next(G("pT_ready", s))
                        if u < NU:
                            weights_turned(u)
                        if u >= 1:
                            values(u - 1)
                    w.next(G("s_drained", s))

                    def heads_turned(v):
                        k, half = v // 2, v % 2
                        for j in range(4):
                            c = (half * 4 + j) * P
                            mm = pe.transpose(ps[:, v % 2, j * P:(j + 1) * P], ON[s][:, k, c:c + P], ident[:])
                        mm.then_inc(G("turned", s), 1)

                    for v in range(2 * NB + 1):
                        yield 40 + v
                        if v == 0:
                            w.next(G("o_drained", s))
                        if v < 2 * NB:
                            heads_turned(v)
                        if v >= 1:
                            w.next(G("t_ready", s))
                            for j in range(4):
                                mm = pe.matmul(ps[:, 3, (v - 1) // 2 * P:((v - 1) // 2 + 1) * P],
                                               OT[s][:, (v - 1) % 2, j, :], a_o[:, (v - 1) % 2 * 4 + j, :],
                                               start=((v - 1) % 2 == 0 and j == 0),
                                               stop=((v - 1) % 2 == 1 and j == 3))
                            mm.then_inc(G("heads_used", s), 1)

                def experts(s):
                    ps = PS[s]
                    yield 1
                    w.next(G("x_ready", s))
                    w.next(G("xr_ready", s))
                    turn(s, R[s], 0)
                    yield 2
                    w.next(G("xT_ready", s))
                    for k in range(NB):
                        pe.matmul(ps[:, k, :], XT[s][:, k * P:(k + 1) * P], p_m[:], start=True, stop=True)\
                            .then_inc(G("sim_ready", s), 1)

                    def expert_inputs(k):
                        for j in range(2):
                            pe.matmul(ps[:, 2 + j, :], XT[s][:, k * P:(k + 1) * P], p_downT[:, j * 512:(j + 1) * 512],
                                      start=True, stop=True).then_inc(G("z_ready", s), 1)

                    yield 3
                    w.next(G("sim_sb", s), NB)
                    expert_inputs(0)
                    for k in range(NB):
                        for h in range(PH):
                            yield 10 + 20 * k + h
                            w.next(G("wh_ready", s))
                            for j in range(2):
                                mm = pe.matmul(ps[:, j, :], ident[:], WH[s][:, h % WB, j * 512:(j + 1) * 512],
                                               start=(h == 0), stop=(h == PH - 1), skip_group_check=True)
                            mm.then_inc(G("wh_used", s), 1)
                        yield 18 + 20 * k
                        w.next(G("hw_ready", s))
                        for e in range(EB):
                            mm = pe.transpose(ps[:, 2 + e // 4, (e % 4) * P:(e % 4 + 1) * P],
                                              HW[s][:, e * P:(e + 1) * P], ident[:])
                        mm.then_inc(G("turned", s), 1)
                        yield 19 + 20 * k
                        w.next(G("hwT_ready", s))
                        for e in range(EB):
                            mm = pe.matmul(ps[:, 2, 0:P], HWT[s][:, e, :], p_up[:, e, :],
                                           start=(e == 0), stop=(e == EB - 1))
                        mm.then_inc(G("eo_ready", s), 1)
                        yield 20 + 20 * k
                        w.next(G("eo_drained", s))
                        if k + 1 < NB:
                            expert_inputs(k + 1)

                in_turn(sublayers([hyena, cross0, bitffn, scan, cross1, experts]))

        def act_program(block):
            @block.scalar
            def _(act):
                w = Signals(act, act_step)

                def G(n, s):
                    return sg[n][s]

                def copy(to, of, signal=None, **kw):
                    ins = nc.scalar.activation(to, of, ACT.Copy, **kw)
                    if signal is not None:
                        ins.then_inc(signal, 1)
                    return ins

                def turned(s, to, of, ready, **kw):
                    w.next(G("turned", s))
                    copy(to, of, G(ready, s), **kw)

                def hyena(s):
                    ps = PS[s]
                    yield 0
                    turned(s, XT[s][:], ps[:, 0, :], "xT_ready")
                    w.next(G("ctx_turned", s))
                    copy(CTT[s][:], ps[:, 3, 0:C], G("ctxT_ready", s))
                    yield 1
                    for j, c in enumerate((0, 2)):
                        w.next(G("u_ready", s))
                        w.link(nc.scalar.activation(U[s][:, j, :], ps[:, 1 + j, :], ACT.Identity,
                                                    bias=in_b[:, c:c + 1]))
                        nc.scalar.activation(CV[s][:, j, :], U[s][:, j, :], ACT.Identity,
                                             bias=conv_b[:, c:c + 1], scale=conv_w[:, c, 2:3])\
                            .then_inc(G("conv0", s), 1)
                    yield 2
                    turned(s, VT[s][:].rearrange("p a b -> p (a b)"), ps[:, 3, :], "v_tm")

                def cross0(s):
                    ps = PS[s]
                    yield 0
                    turned(s, XT[s][:], ps[:, 0, :], "xT_ready")
                    yield 1
                    w.next(G("l_ready", s))
                    nc.scalar.activation(LE[s][:], LG[s][:], ACT.Exp).then_inc(G("p_ready", s), 1)
                    yield 2
                    turned(s, PT[s][:], ps[0:C, 2, :], "pT_ready")

                def bitffn(s):
                    ps = PS[s]
                    yield 1
                    turned(s, QT[s][:], ps[:, 0, :].bitcast(BF16)[:, 0:S], "qT_ready")
                    yield 2
                    for k in range(NB):
                        w.next(G("hpre_ready", s))
                        w.link(nc.scalar.activation(BIG2[s][:, k, :], BIG1[s][:, k, :], ACT.Gelu))
                        nc.scalar.activation(BIG1[s][:, k, :], BIG2[s][:, k, :], ACT.Square,
                                             accum_out=ST[s][:, 4, k:k + 1]).then_inc(G("g_ready", s), 1)
                    yield 4
                    for k in range(NB):
                        turned(s, HT[s][:, k].rearrange("p a b -> p (a b)"),
                               ps[:, k, :].bitcast(BF16)[:, 0:F], "qT_ready")

                def scan(s):
                    ps = PS[s]
                    yield 0
                    turned(s, XT[s][:], ps[:, 0, :], "xT_ready")
                    yield 1
                    for j, bank in enumerate([1, 2, 3, 0]):
                        w.next(G("u_ready", s))
                        to = TU[s] if j < DJ else TR[s]
                        nc.scalar.activation(to[:, j % DJ, :], ps[:, bank, :], ACT.Tanh, scale=0.5)\
                            .then_inc(G("g_ready", s), 1)
                    yield 2
                    for j in range(DJ):
                        w.next(G("d_ready", s))
                        w.link(nc.scalar.activation(SPA[s][:, j, :], ps[:, 1 + j, :], ACT.Abs,
                                                    bias=m_bdelta[:, j:j + 1]))
                        w.link(nc.scalar.activation(SPE[s][:, j, :], SPA[s][:, j, :], ACT.Exp, scale=-1.0))
                        nc.scalar.activation(SPA[s][:, j, :], SPE[s][:, j, :], ACT.Ln, bias=1.0)\
                            .then_inc(G("ln_ready", s), 1)
                    for n in range(NS):
                        yield 3 + n
                        if n == 0:
                            w.next(G("delta_ready", s))
                        if n >= 2:
                            w.next(G("scan_done", s))
                        for j in range(DJ):
                            ins = nc.scalar.activation(dA[s][:, n % 2, j, 1:S], DL[s][:, j, 1:S], ACT.Exp,
                                                       scale=m_A[:, j, n:n + 1])
                        ins.then_inc(G("dA_ready", s), 1)

                def cross1(s):
                    ps = PS[s]
                    yield 0
                    turned(s, XT[s][:], ps[:, 0, :], "xT_ready")
                    for j in range(2):
                        w.next(G("k_ready", s))
                        nc.scalar.activation(KQ[s][:].rearrange("p a b -> p (a b)")[:, j * 512:(j + 1) * 512],
                                             ps[0:C, 1 + j, :], ACT.Square).then_inc(G("ksq_ready", s), 1)
                    yield 1
                    for j, bank in enumerate((3, 0)):
                        w.next(G("v_ready", s))
                        copy(VV[s][:, j * 8:(j + 1) * 8, 0:E],
                             ps[0:C, bank, :].rearrange("p (a b) -> p a b", b=E), G("v_sb", s))
                    yield 2
                    turned(s, KT[s][:].rearrange("p (a b) c -> p a (b c)", a=2), ps[:, 1:3, 0:4 * C],
                           "kT_ready", scale=a_g[:, 0:1])
                    for j in range(HP):
                        yield 3 + j
                        bank = [3, 0, 1, 2][j % 4]
                        w.next(G("aq_ready", s))
                        copy(AQ[s][:, j, :], ps[:, bank, :])
                        nc.scalar.activation(QSQ[s][:, j, :], ps[:, bank, :], ACT.Square)\
                            .then_inc(G("qsq_ready", s), 1)

                    def exponentials(g):
                        w.next(G("l_ready", s))
                        nc.scalar.activation(SC[s][:, g % 2].rearrange("p a b c -> p (a b c)"),
                                             SC[s][:, g % 2].rearrange("p a b c -> p (a b c)"), ACT.Exp)\
                            .then_inc(G("p_ready", s), 1)

                    NU = NB * H // HG
                    yield 19
                    exponentials(0)
                    for u in range(NU):
                        yield 20 + u
                        turned(s, AT[s][:, u % 2].rearrange("p a b -> p (a b)"), ps[0:C, 2, :], "pT_ready")
                        if u % 2 == 0 and u // 2 + 1 < NU // 2:
                            exponentials(u // 2 + 1)
                    for v in range(2 * NB):
                        yield 40 + v
                        if v >= 2:
                            w.next(G("heads_used", s))
                        turned(s, OT[s][:, v % 2].rearrange("p a b -> p (a b)"), ps[:, v % 2, :], "t_ready")

                def experts(s):
                    ps = PS[s]
                    yield 1
                    turned(s, XT[s][:], ps[:, 0, :], "xT_ready", scale=p_norm[:, 0:1])
                    yield 2
                    for k in range(NB):
                        w.next(G("sim_ready", s))
                        copy(SIM[s][:, k, :], ps[:, k, :], G("sim_sb", s))

                    def activations():
                        w.next(G("z_ready", s), 2)
                        nc.scalar.activation(HW[s][:].rearrange("p (a b) -> p a b", a=2), ps[:, 2:4, :], ACT.Gelu)\
                            .then_inc(G("g_sb", s), 1)

                    yield 3
                    activations()
                    for k in range(NB):
                        yield 18 + 20 * k
                        w.next(G("turned", s))
                        copy(HWT[s][:].rearrange("p (a b) c -> p a (b c)", a=2), ps[:, 2:4, :], G("hwT_ready", s))
                        yield 19 + 20 * k
                        w.next(G("eo_ready", s))
                        copy(OS[s][:, k, :], ps[:, 2, 0:P], G("eo_drained", s))
                        yield 20 + 20 * k
                        if k + 1 < NB:
                            activations()

                in_turn(sublayers([hyena, cross0, bitffn, scan, cross1, experts]))

        def dve_program(block):
            @block.vector
            def _(dve):
                w = Signals(dve, dve_step)

                def G(n, s):
                    return sg[n][s]

                def statistics(s, of, eps):
                    for k in range(NB):
                        ins = nc.vector.bn_stats(BNS[s][:, k, :], of[:, k, :])
                    w.link(ins)
                    for k in range(NB):
                        ins = nc.vector.bn_aggr(MV[s][:, k, :], BNS[s][:, k, :])
                    w.link(ins)
                    nc.vector.tensor_scalar(VE[s][:, 0:NB], MV[s][:, :, 1], eps, None, ALU.add)\
                        .then_inc(G("var_ready", s), 1)

                def normalised(s, of, to):
                    w.next(G("rstd_ready", s))
                    for k in range(NB):
                        ins = nc.vector.tensor_scalar(to[:, k, :], of[:, k, :], MV[s][:, k, 0:1],
                                                      RS[s][:, k:k + 1], ALU.subtract, ALU.mult)
                    return ins

                def residual(s, of, bias):
                    w.link(nc.vector.tensor_tensor(R[s][:], of, X[s][:], ALU.add))
                    if bias is not None:
                        w.link(nc.vector.tensor_tensor(R[s][:], R[s][:], spread(bias[:], 1, NB), ALU.add))
                    statistics(s, R[s], 1e-5)

                def new_x(s):
                    normalised(s, R[s], X[s]).then_inc(G("x_ready", s), 1)
                    w.next(G("x_ready", s))

                def bank(s, n):
                    return PS[s][:, n, :].rearrange("p (k d) -> p k d", k=NB)

                def hyena(s):
                    ps = PS[s]
                    yield 1
                    dve.wait_ge(G("x_loaded", s), 16)
                    for j, c in enumerate((0, 2)):
                        w.next(G("conv0", s))
                        w.link(nc.vector.scalar_tensor_tensor(
                            out=CV[s][:, j, 1:S], in0=U[s][:, j, 0:S - 1], scalar=conv_w[:, c, 1:2],
                            in1=CV[s][:, j, 1:S], op0=ALU.mult, op1=ALU.add))
                        w.link(nc.vector.scalar_tensor_tensor(
                            out=CV[s][:, j, 2:S], in0=U[s][:, j, 0:S - 2], scalar=conv_w[:, c, 0:1],
                            in1=CV[s][:, j, 2:S], op0=ALU.mult, op1=ALU.add))
                    nc.vector.tensor_tensor(V1[s][:], CV[s][:, 1, :], CV[s][:, 0, :], ALU.mult)\
                        .then_inc(G("v1_ready", s), 1)
                    w.next(G("v1_ready", s))
                    dve.wait_ge(G("mask_loaded", s), 16)
                    nc.vector.tensor_scalar(PEN[s][:], MK[s][:], 0, MASKED, ALU.is_equal, ALU.mult)
                    yield 3
                    w.next(G("y_ready", s))
                    w.link(nc.vector.scalar_tensor_tensor(out=V2[s][:], in0=V1[s][:], scalar=filt_b[:, 0:1],
                                                          in1=ps[:, 0, :], op0=ALU.mult, op1=ALU.add))
                    nc.vector.tensor_tensor(V3[s][:], V2[s][:], CV[s][:, 0, :], ALU.mult)\
                        .then_inc(G("v3_ready", s), 1)
                    yield 4
                    w.next(G("o_ready", s))
                    residual(s, bank(s, 1), b_out)
                    yield 5
                    new_x(s)

                def cross0(s):
                    yield 1
                    w.next(G("s_ready", s))
                    w.link(nc.vector.scalar_tensor_tensor(
                        out=LG[s][:], in0=PS[s][:, 1, 0:NB * C].rearrange("p (k c) -> p k c", k=NB),
                        scalar=float(D) ** -0.5, in1=PEN[s][:], op0=ALU.mult, op1=ALU.add))
                    w.link(nc.vector.tensor_reduce(ST[s][:, 0, :], LG[s][:], AX.X, ALU.max))
                    nc.vector.tensor_tensor(LG[s][:], LG[s][:], spread(ST[s][:, 0, :], 2, C), ALU.subtract)\
                        .then_inc(G("l_ready", s), 1)
                    yield 2
                    w.next(G("p_ready", s))
                    w.link(nc.vector.tensor_reduce(ST[s][:, 1, :], LE[s][:], AX.X, ALU.add))
                    w.link(nc.vector.reciprocal(ST[s][:, 2, :], ST[s][:, 1, :]))
                    yield 3
                    w.next(G("o_ready", s))
                    w.link(nc.vector.tensor_tensor(R2[s][:], bank(s, 3), spread(ST[s][:, 2, :], 2, P), ALU.mult))
                    statistics(s, R2[s], 1e-5)
                    yield 4
                    w.link(normalised(s, R2[s], R2[s]))
                    w.link(nc.vector.tensor_tensor(R2[s][:], R2[s][:], spread(gamma[:], 1, NB), ALU.mult))
                    w.link(nc.vector.tensor_tensor(R2[s][:], R2[s][:], spread(beta[:], 1, NB), ALU.add))
                    residual(s, R2[s][:], None)
                    yield 5
                    new_x(s)

                def mean_squares(s, source, n):
                    nc.vector.tensor_scalar(VE[s][:, 0:NB], source, 1.0 / n, 1e-6, ALU.mult, ALU.add)\
                        .then_inc(G("var_ready", s), 1)

                def quantise_scales(s, deq):
                    w.next(G("rstd_ready", s))
                    w.link(nc.vector.tensor_tensor(ST[s][:, 1, :], ST[s][:, 0, :], RS[s][:, 0:NB], ALU.mult))
                    w.link(nc.vector.tensor_scalar(ST[s][:, 1, :], ST[s][:, 1, :], 1e-5, None, ALU.max))
                    w.link(nc.vector.reciprocal(ST[s][:, 3, :], ST[s][:, 1, :]))
                    nc.vector.tensor_scalar(ST[s][:, 5, :], ST[s][:, 1, :], deq, None, ALU.mult)
                    w.link(nc.vector.tensor_scalar(ST[s][:, 3, :], ST[s][:, 3, :], 127.0, None, ALU.mult))

                def bitffn(s):
                    ps = PS[s]
                    yield 0
                    w.link(nc.vector.tensor_tensor(R2[s][:], X[s][:], X[s][:], ALU.mult))
                    nc.vector.tensor_reduce(ST[s][:, 0, :], X[s][:], AX.X, ALU.max, apply_absolute_value=True)
                    w.link(nc.vector.tensor_reduce(ST[s][:, 2, :], R2[s][:], AX.X, ALU.add))
                    mean_squares(s, ST[s][:, 2, :], D)
                    yield 1
                    quantise_scales(s, q_deq[:, 0:1])
                    for k in range(NB):
                        ins = nc.vector.tensor_scalar(QF[s][:, k, :], X[s][:, k, :], RS[s][:, k:k + 1],
                                                      ST[s][:, 3, k:k + 1], ALU.mult, ALU.mult)
                    w.link(ins)
                    nc.vector.tensor_scalar(QB[s][:], QF[s][:], ROUND, -ROUND, ALU.add, ALU.add)\
                        .then_inc(G("q_ready", s), 1)
                    yield 2
                    for k in range(NB):
                        w.next(G("h_ready", s))
                        nc.vector.scalar_tensor_tensor(out=BIG1[s][:, k, :], in0=ps[:, k, :],
                                                       scalar=ST[s][:, 5, k:k + 1], in1=b1[:],
                                                       op0=ALU.mult, op1=ALU.add).then_inc(G("hpre_ready", s), 1)
                    yield 3
                    w.next(G("g_ready", s), NB)
                    nc.vector.tensor_reduce(ST[s][:, 0, :], BIG2[s], AX.X, ALU.max, apply_absolute_value=True)
                    mean_squares(s, ST[s][:, 4, :], F)
                    yield 4
                    quantise_scales(s, q_deq[:, 1:2])
                    for k in range(NB):
                        w.link(nc.vector.tensor_scalar(BIG1[s][:, k, :], BIG2[s][:, k, :], RS[s][:, k:k + 1],
                                                       ST[s][:, 3, k:k + 1], ALU.mult, ALU.mult))
                        nc.vector.tensor_scalar(HQ[s][:, k, :], BIG1[s][:, k, :], ROUND, -ROUND,
                                                ALU.add, ALU.add).then_inc(G("q_ready", s), 1)
                    yield 5
                    w.next(G("o_ready", s))
                    w.link(nc.vector.tensor_tensor(R2[s][:], bank(s, 0), spread(ST[s][:, 5, :], 2, P), ALU.mult))
                    w.link(nc.vector.tensor_tensor(R2[s][:], R2[s][:], spread(b2[:], 1, NB), ALU.add))
                    residual(s, R2[s][:], None)
                    yield 6
                    new_x(s)

                def scan(s):
                    ps = PS[s]
                    yield 1
                    for j, b in enumerate([1, 2, 3, 0]):
                        w.next(G("u_ready", s))
                        w.next(G("g_ready", s))
                        t = TU[s] if j < DJ else TR[s]
                        ins = nc.vector.scalar_tensor_tensor(out=t[:, j % DJ, :], in0=t[:, j % DJ, :], scalar=1.0,
                                                             in1=ps[:, b, :], op0=ALU.add, op1=ALU.mult)
                        if j < DJ:
                            w.link(ins)
                            nc.vector.tensor_scalar(UU[s][:, j, :], t[:, j, :], 0.5, None, ALU.mult)\
                                .then_inc(G("silu_u", s), 1)
                        else:
                            ins.then_inc(G("silu_r", s), 1)
                    w.next(G("silu_u", s), DJ)
                    yield 2
                    w.next(G("bc_ready", s))
                    bc = ps[0:2 * NS, 3, :]
                    w.link(nc.vector.tensor_copy(BCS[s][0:2 * NS, :], bc))
                    w.link(nc.vector.tensor_tensor(BC1[s][:], bc, BCS[s][0:2 * NS, :], ALU.subtract))
                    w.link(nc.vector.tensor_copy(BCM[s][:], BC1[s][:]))
                    nc.vector.tensor_copy(BCS[s][2 * NS:4 * NS, :], BCM[s][:])
                    nc.vector.tensor_tensor(BCS[s][4 * NS:6 * NS, :], BC1[s][:], BCM[s][:], ALU.subtract)\
                        .then_inc(G("bcs_ready", s), 1)
                    for j in range(DJ):
                        w.next(G("d_ready", s))
                        w.next(G("ln_ready", s))
                        w.link(nc.vector.tensor_scalar(DL[s][:, j, :], ps[:, 1 + j, :], m_bdelta[:, j:j + 1], 0.0,
                                                       ALU.add, ALU.max))
                    w.link(nc.vector.tensor_tensor(DL[s][:], DL[s][:], SPA[s][:], ALU.add))
                    nc.vector.memset(dA[s][:, :, :, 0:1], 0.0).then_inc(G("delta_ready", s), 1)
                    w.next(G("delta_ready", s))
                    w.link(nc.vector.tensor_tensor(DU[s][:], DL[s][:], UU[s][:], ALU.mult))
                    flat = "p a b -> p (a b)"
                    for n in range(NS):
                        yield 4 + n
                        w.next(G("B_ready", s))
                        nc.vector.tensor_tensor(dBu[s][:], DU[s][:], spread(ps[:, 0, :], 1, DJ), ALU.mult)\
                            .then_inc(G("dbu_done", s), 1)
                        w.next(G("dbu_done", s))
                        w.next(G("dA_ready", s))
                        nc.vector.tensor_tensor_scan(HS[s][:].rearrange(flat), dA[s][:, n % 2].rearrange(flat),
                                                     dBu[s][:].rearrange(flat), 0.0, ALU.mult, ALU.add)\
                            .then_inc(G("scan_done", s), 1)
                        w.next(G("scan_done", s))
                        w.next(G("C_ready", s))
                        if n >= 2:
                            w.next(G("y_acc", s))
                        nc.vector.tensor_tensor(HC[s][:, n % 2], HS[s][:], spread(ps[:, 3, :], 1, DJ), ALU.mult)\
                            .then_inc(G("hc_done", s), 1)
                    yield 5 + NS
                    w.next(G("y_acc", s), 2)
                    for j in range(DJ):
                        ins = nc.vector.scalar_tensor_tensor(out=TU[s][:, j, :], in0=UU[s][:, j, :],
                                                             scalar=m_D[:, j:j + 1], in1=ps[:, 1 + j, :],
                                                             op0=ALU.mult, op1=ALU.add)
                    w.link(ins)
                    nc.vector.scalar_tensor_tensor(out=TU[s][:], in0=TU[s][:], scalar=0.5, in1=TR[s][:],
                                                   op0=ALU.mult, op1=ALU.mult).then_inc(G("yg_ready", s), 1)
                    yield 6 + NS
                    w.next(G("o_ready", s))
                    residual(s, bank(s, 0), None)
                    yield 7 + NS
                    new_x(s)

                def cross1(s):
                    ps = PS[s]
                    yield 1
                    w.next(G("ksq_ready", s), 2)
                    w.link(nc.vector.tensor_reduce(VE[s][0:C, 0:H], KQ[s][:], AX.X, ALU.add))
                    nc.vector.tensor_scalar(VE[s][0:C, 0:H], VE[s][0:C, 0:H], 1.0 / E, 1e-6,
                                            ALU.mult, ALU.add).then_inc(G("var_ready", s), 1)
                    yield 2
                    w.next(G("rstd_ready", s))
                    w.next(G("k_ready", s), 2)
                    for j in range(2):
                        ins = nc.vector.tensor_tensor(
                            KN[s][:, j * 8:(j + 1) * 8, :], ps[0:C, 1 + j, :].rearrange("p (a b) -> p a b", b=E),
                            spread(RS[s][0:C, j * 8:(j + 1) * 8], 2, E), ALU.mult)
                    ins.then_inc(G("kn_ready", s), 1)
                    yield 11
                    w.next(G("ssq_ready", s))
                    nc.vector.tensor_scalar(VE[s][:, 0:NB * H], ps[:, 3, 512 - NB * H:512], 1.0 / E, 1e-6,
                                            ALU.mult, ALU.add).then_inc(G("var_ready", s), 1)

                    def softmax(g):
                        k, half = g // NG, g % NG
                        w.next(G("s_ready", s))
                        raw = ps[:, 0:2, 0:HG * C].rearrange("p a (h c) -> p a h c", c=C)
                        mx = MX[s]
                        r0 = k * H + half * 2 * HG
                        rs = RS[s][:, r0:r0 + 2 * HG].rearrange("p (h a) -> p a h", a=2)
                        w.link(nc.vector.tensor_reduce(mx, raw, AX.X, ALU.max))
                        nc.vector.tensor_tensor(SC[s][:, g % 2], raw, spread(mx, 3, C), ALU.subtract)\
                            .then_inc(G("s_drained", s), 1)
                        w.next(G("s_drained", s))
                        if half == 0:
                            w.next(G("rstd_ready", s))
                        nc.vector.tensor_tensor(SC[s][:, g % 2], SC[s][:, g % 2], spread(rs, 3, C), ALU.mult)\
                            .then_inc(G("l_ready", s), 1)

                    def out_unit(u):
                        w.next(G("o_ready", s))
                        o = ps[:, 3, 0:HG * (E + 1)].rearrange("p (h e) -> p h e", e=E + 1)
                        w.link(nc.vector.reciprocal(RD[s][:], o[:, :, E]))
                        g = u // 2
                        c = (g % NG) * 2 * HG * E
                        to = ON[s][:, g // NG, c:c + 2 * HG * E].rearrange("p (h a e) -> p a h e", a=2, e=E)[:, u % 2]
                        nc.vector.tensor_tensor(to, o[:, :, 0:E], spread(RD[s][:], 2, E), ALU.mult)\
                            .then_inc(G("o_drained", s), 1)

                    NU = NB * H // HG
                    yield 19
                    softmax(0)
                    for u in range(NU + 1):
                        yield 20 + u
                        if u % 2 == 0 and u // 2 + 1 < NU // 2:
                            softmax(u // 2 + 1)
                        if u >= 1:
                            out_unit(u - 1)
                    yield 50
                    w.next(G("heads_used", s), 2 * NB)
                    residual(s, bank(s, 3), a_bo)
                    yield 51
                    new_x(s)

                def experts(s):
                    ps = PS[s]
                    yield 0
                    w.link(nc.vector.tensor_tensor(R2[s][:], X[s][:], X[s][:], ALU.mult))
                    w.link(nc.vector.tensor_reduce(ST[s][:, 2, :], R2[s][:], AX.X, ALU.add))
                    mean_squares(s, ST[s][:, 2, :], D)
                    yield 1
                    w.next(G("rstd_ready", s))
                    for k in range(NB):
                        ins = nc.vector.tensor_scalar(R[s][:, k, :], X[s][:, k, :], RS[s][:, k:k + 1], None, ALU.mult)
                    ins.then_inc(G("xr_ready", s), 1)

                    def thresholds(k):
                        w.next(G("sim_sb", s))
                        sims = SIM[s][:, k, :].rearrange("p (a h n) -> p a h n", a=2, h=PH)
                        for a in range(2):
                            for h in range(PH):
                                ins = nc.vector.max(T8[s][:, a, h, :], sims[:, a, h, :])
                        w.link(ins)
                        w.link(nc.vector.tensor_tensor(A64[s][:], spread(T8[s][:, 0], 3, TOP),
                                                       spread(T8[s][:, 1], 2, TOP), ALU.add))
                        for h in range(PH):
                            ins = nc.vector.max(TT[s][:, h, :], A64[s][:, h].rearrange("p a b -> p (a b)"))
                        w.link(ins)
                        w.link(nc.vector.tensor_scalar(TH[s][:], TT[s][:, :, TOP - 1], 0.0, None, ALU.max))

                    yield 3
                    thresholds(0)
                    for k in range(NB):
                        sims = SIM[s][:, k, :].rearrange("p (a h n) -> p a h n", a=2, h=PH)
                        for h in range(PH):
                            yield 10 + 20 * k + h
                            v = SV[s][:].rearrange("p (i j) -> p i j", i=NK)
                            w.link(nc.vector.tensor_tensor(v, spread(sims[:, 0, h, :], 2, NK),
                                                           spread(sims[:, 1, h, :], 1, NK), ALU.add))
                            if k * PH + h >= WB:
                                w.next(G("wh_used", s))
                            nc.vector.scalar_tensor_tensor(
                                out=WH[s][:, h % WB, :], in0=SV[s][:], scalar=TH[s][:, h:h + 1], in1=SV[s][:],
                                op0=ALU.is_ge, op1=ALU.mult).then_inc(G("wh_ready", s), 1)
                            w.next(G("wh_ready", s))
                        yield 18 + 20 * k
                        dve.wait_ge(G("wh_used", s), (k + 1) * PH)
                        w.next(G("g_sb", s))
                        nc.vector.tensor_tensor(HW[s][:], HW[s][:], ps[:, 0:2, :].rearrange("p a b -> p (a b)"),
                                                ALU.mult).then_inc(G("hw_ready", s), 1)
                        if k + 1 < NB:
                            yield 19 + 20 * k
                            thresholds(k + 1)
                    yield 94
                    w.next(G("eo_drained", s), NB)
                    residual(s, OS[s][:], None)
                    yield 95
                    new_x(s)

                in_turn(sublayers([hyena, cross0, bitffn, scan, cross1, experts]))

        def pool_program(block):
            @block.gpsimd
            def _(pool):
                w = Signals(pool)

                def rsqrt(s, rows, n, pieces=1):
                    w.next(sg["var_ready"][s])
                    for i in range(pieces):
                        nc.gpsimd.tensor_tensor(RS[s][0:rows, i * n:(i + 1) * n], VE[s][0:rows, i * n:(i + 1) * n],
                                                minus_half[0:rows, 0:n], ALU.pow)\
                            .then_inc(sg["rstd_ready"][s], 1)

                def program(s):
                    for stage in (4, 103, 104, 200, 203, 205, 306 + NS):
                        yield stage
                        rsqrt(s, P, NB)
                    yield 401
                    rsqrt(s, C, H)
                    yield 411
                    rsqrt(s, P, H, NB)
                    for stage in (450, 500, 594):
                        yield stage
                        rsqrt(s, P, NB)

                in_turn(program)

        with nc.Fori(0, B // LANES) as it:
            body(it)
            for q in lane_sems:
                nc.gpsimd.sem_clear(q)
            nc.all_engine_barrier()


_INS = ['x', 'ctx_1024', 'mask_BxSxS2_ik1', 'L0_attn_w_in', 'L0_attn_b_in', 'L0_attn_w_conv',
        'L0_attn_b_conv', 'L0_attn_w1', 'L0_attn_b1', 'L0_attn_w2', 'L0_attn_b2', 'L0_attn_w3',
        'L0_attn_filt_bias', 'L0_attn_w_out', 'L0_attn_b_out', 'L0_xattn_gamma', 'L0_xattn_beta',
        'L0_ffn_w1', 'L0_ffn_b1', 'L0_ffn_w2', 'L0_ffn_b2', 'L1_attn_W_in', 'L1_attn_W_delta',
        'L1_attn_b_delta', 'L1_attn_W_B', 'L1_attn_W_C', 'L1_attn_A_log', 'L1_attn_D_param',
        'L1_attn_W_out', 'L1_xattn_Wq', 'L1_xattn_Wk', 'L1_xattn_Wv', 'L1_xattn_Wo', 'L1_xattn_bo',
        'L1_xattn_gq', 'L1_xattn_gk', 'L1_ffn_w_q', 'L1_ffn_keys', 'L1_ffn_expert_down',
        'L1_ffn_expert_up', 'L1_ffn_norm_w']


def kernel(**inputs):
    import numpy as _np
    import concourse.bacc as _bacc
    from concourse import mybir as _mybir
    from concourse.bass_utils import run_bass_kernel_spmd as _run

    nc = _bacc.Bacc("TRN2", target_bir_lowering=False, num_devices=1)
    arrays, args = {}, []
    for name in _INS:
        a = _np.ascontiguousarray(inputs[name])
        arrays[f"in_{name}_dram"] = a
        args.append(nc.dram_tensor(f"in_{name}_dram", a.shape, _mybir.dt.from_np(a.dtype), kind="ExternalInput").ap())
    args.append(nc.dram_tensor("out_0_dram", inputs["x"].shape, F32, kind="ExternalOutput").ap())
    decoder(nc, *args)
    r = _run(nc, [arrays], core_ids=[0])
    return r.results[0]["out_0_dram"]
```

```python
from contextlib import ExitStack

import numpy as np

import concourse.bass as bass
from concourse import mybir

ALU = mybir.AluOpType
ACT = mybir.ActivationFunctionType
AX = mybir.AxisListType
F32 = mybir.dt.float32
BF16 = mybir.dt.bfloat16
I32 = mybir.dt.int32

P = 128
MASKED = -9000000000000000.0
ROUND = 12582912.0


def spread(ap, axis, n):
    dims = [list(d) for d in ap.ap]
    dims.insert(axis, [0, n])
    return bass.AP(ap.tensor, ap.offset, dims)


class Signals:

    def __init__(self, eng, step=None):
        self.eng, self.step, self.steps, self.seen = eng, step, 0, {}

    def next(self, sem, n=1):
        key = sem.name if hasattr(sem, "name") else str(sem)
        self.seen[key] = self.seen.get(key, 0) + n
        self.eng.wait_ge(sem, self.seen[key])

    def link(self, instruction):
        self.steps += 1
        instruction.then_inc(self.step, 1)
        self.eng.wait_ge(self.step, self.steps)


def decoder(nc, x, ctx_1024, mask_BxSxS2_ik1, L0_attn_w_in, L0_attn_b_in, L0_attn_w_conv,
            L0_attn_b_conv, L0_attn_w1, L0_attn_b1, L0_attn_w2, L0_attn_b2, L0_attn_w3,
            L0_attn_filt_bias, L0_attn_w_out, L0_attn_b_out, L0_xattn_gamma, L0_xattn_beta,
            L0_ffn_w1, L0_ffn_b1, L0_ffn_w2, L0_ffn_b2, L1_attn_W_in, L1_attn_W_delta,
            L1_attn_b_delta, L1_attn_W_B, L1_attn_W_C, L1_attn_A_log, L1_attn_D_param,
            L1_attn_W_out, L1_xattn_Wq, L1_xattn_Wk, L1_xattn_Wv, L1_xattn_Wo, L1_xattn_bo,
            L1_xattn_gq, L1_xattn_gk, L1_ffn_w_q, L1_ffn_keys, L1_ffn_expert_down,
            L1_ffn_expert_up, L1_ffn_norm_w, out):
    B, S, D = x.shape
    C = ctx_1024.shape[1]
    NB = S // P
    FW = L0_attn_w2.shape[0]
    F = L0_ffn_w1.shape[0]
    FK = F // P
    DI = L1_attn_W_delta.shape[0]
    DJ = DI // P
    NS = L1_attn_W_B.shape[1]
    H, E = L1_xattn_Wq.shape[1:]
    HP = H * E // P
    PH, NK = L1_ffn_keys.shape[:2]
    NE = L1_ffn_expert_down.shape[0]
    EB = NE // P
    TOP = 8
    CANDIDATES = [(0, 1, 8), (1, 4, 4), (4, 8, 1)]
    NC = sum((i1 - i0) * nj for i0, i1, nj in CANDIDATES)
    LANES = 2
    LAG = 0
    WB = 4
    GB = 3
    POOL_LANE = 0
    ACT_HEADS = (4, 7)
    assert D == P and DJ == 2 and NE == NK * NK and 3 * 2 * NS <= P and F <= 512

    h_pad = nc.dram_tensor("h_pad", (3 * P,), F32, kind="Internal").ap()

    with ExitStack() as ctx:
        def sb(name, shape, dt=F32):
            return ctx.enter_context(nc.sbuf_tensor(name, shape, dt))

        def sem(name):
            return ctx.enter_context(nc.semaphore(name))

        def lanes(make, name, *a):
            return [make(f"{name}{s}", *a) for s in range(LANES)]

        PS = [ctx.enter_context(nc.psum_tensor(f"ps{s}", [P, 4, 512], F32)) for s in range(LANES)]

        ident = sb("ident", [P, P])
        ident_bf = sb("ident_bf", [P, P], BF16)
        ones = sb("ones", [P, P])
        pair_pick = sb("pair_pick", [P, HP, H])
        minus_half = sb("minus_half", [P, 64])
        row_pick = sb("row_pick", [96, 2 * NS, P], BF16)

        w_in = sb("w_in", [P, 2, P])
        conv_w = sb("conv_w", [P, 3, 3])
        conv_b = sb("conv_b", [P, 3])
        in_b = sb("in_b", [P, 3])
        f_w1 = sb("f_w1", [3, FW])
        f_b1 = sb("f_b1", [FW, 1])
        f_w2 = sb("f_w2", [FW, FW])
        f_b2 = sb("f_b2", [FW, 1])
        f_w3 = sb("f_w3", [FW, P])
        f_t = sb("f_t", [3, 1])
        f_z = sb("f_z", [FW, 1])
        f_e = sb("f_e", [FW, 1])
        f_h1 = sb("f_h1", [FW, 1])
        f_h2 = sb("f_h2", [FW, 1])
        f_decay = sb("f_decay", [1, P])
        f_row = sb("f_row", [1, 3 * P])
        fb_row = sb("fb_row", [1, P])
        filt_b = sb("filt_b", [P, 1])
        toe = sb("toe", [P, 2 * P])
        w_out = sb("w_out", [P, P])
        b_out = sb("b_out", [P, P])
        gamma = sb("gamma", [P, P])
        beta = sb("beta", [P, P])
        q_abs = sb("q_abs", [P, 2])
        q_clip = sb("q_clip", [P, 2])
        q_scale = sb("q_scale", [P, 2])
        q_deq = sb("q_deq", [P, 2])
        q1T = sb("q1T", [P, F], BF16)
        q2T = sb("q2T", [P, FK, P], BF16)
        b1 = sb("b1", [P, F])
        b2 = sb("b2", [P, P])
        m_in = sb("m_in", [P, 2 * DI])
        m_delta = sb("m_delta", [P, DJ, DI])
        m_bdelta = sb("m_bdelta", [P, DJ])
        m_bc = sb("m_bc", [P, DJ, 2 * NS])
        m_alog = sb("m_alog", [P, DJ, NS])
        m_aexp = sb("m_aexp", [P, DJ, NS])
        m_A = sb("m_A", [P, DJ, NS])
        m_D = sb("m_D", [P, DJ])
        m_out = sb("m_out", [P, DJ, P])
        a_q = sb("a_q", [P, H * E])
        a_k = sb("a_k", [P, H * E])
        a_vo = sb("a_vo", [P, H, P])
        a_bo = sb("a_bo", [P, P])
        a_gq = sb("a_gq", [P, 1])
        a_gk = sb("a_gk", [P, 1])
        a_g = sb("a_g", [P, 1])
        p_m = sb("p_m", [P, 2 * PH * NK])
        p_downT = sb("p_downT", [P, NE])
        p_up = sb("p_up", [P, EB, P])
        p_norm = sb("p_norm", [P, 1])

        X = lanes(sb, "x", [P, NB, P])
        R = lanes(sb, "r", [P, NB, P])
        R2 = lanes(sb, "r2", [P, NB, P])
        XT = lanes(sb, "xT", [P, S])
        CT = lanes(sb, "c", [C, P])
        CTT = lanes(sb, "cT", [P, C])
        MK = lanes(sb, "mask", [P, NB, C], I32)
        BNS = lanes(sb, "bns", [P, NB, 6])
        MV = lanes(sb, "mv", [P, NB, 2])
        VE = lanes(sb, "ve", [P, 64])
        RS = lanes(sb, "rs", [P, 64])
        ST = lanes(sb, "st", [P, 6, NB])

        WORDS = 12600
        mem = lanes(sb, "mem", [P, WORDS])

        def carve(arena, sizes):
            at, pieces = 0, {}
            for name, (rows, shape, dt) in sizes.items():
                n = int(np.prod(shape))
                words = n if dt is not BF16 else n // 2
                piece = arena[0:rows, at:at + words]
                if dt is BF16:
                    piece = piece.bitcast(BF16)
                if len(shape) > 1:
                    axes = "abcd"[:len(shape)]
                    piece = piece.rearrange(f"p ({' '.join(axes)}) -> p {' '.join(axes)}",
                                            **dict(zip(axes[1:], shape[1:])))
                pieces[name] = piece
                at += words
            assert at <= arena.shape[1], (at, arena.shape)
            return pieces

        def per_lane(**sizes):
            made = [carve(mem[s], sizes) for s in range(LANES)]
            return [[m[name] for m in made] for name in sizes]

        U, CV, V1, V2, V3, VT, PEN = per_lane(
            u=(P, (2, S), F32), cv=(P, (2, S), F32), v1=(P, (S,), F32), v2=(P, (S,), F32),
            v3=(P, (S,), F32), vt=(P, (NB, P), F32), pen=(P, (NB, C), F32))
        pen_at = 8 * S
        _, LG, LE, PT = per_lane(
            hyena=(P, (pen_at + NB * C,), F32), lg=(P, (NB, C), F32), le=(P, (NB, C), F32), pt=(C, (S,), F32))
        BIG1, BIG2, QF, QB, QT, HQ, HT = per_lane(
            pre=(P, (NB, F), F32), act=(P, (NB, F), F32), qf=(P, (NB, P), F32), qb=(P, (NB, P), BF16),
            qt=(P, (S,), BF16), hq=(P, (NB, F), BF16), ht=(P, (NB, FK, P), BF16))
        TU, TR, UU, SPA, SPE, DL, DU, BCS, BC1, BCM, dBu, HS, HC = per_lane(
            tu=(P, (DJ, S), F32), tr=(P, (DJ, S), F32), uu=(P, (DJ, S), F32), spa=(P, (DJ, S), F32),
            spe=(P, (DJ, S), F32), dl=(P, (DJ, S), F32), du=(P, (DJ, S), F32), bcs=(96, (S,), BF16),
            bc1=(2 * NS, (S,), F32), bcm=(2 * NS, (S,), BF16), dbu=(P, (DJ, S), F32), hs=(P, (DJ, S), F32),
            hc=(P, (2, DJ, S), F32))
        _, CSB = per_lane(front=(P, (7 * DJ * S + S // 2,), F32), csb=(P, (S,), F32))
        _, dA = per_lane(front=(P, (3 * DJ * S,), F32), da=(P, (2, DJ, S), F32))
        AT, SC, MX, RD = per_lane(
            at=(C, (2, 2, S), F32), sc=(P, (GB, 2, NB, C), F32), mx=(P, (2, NB), F32), rd=(P, (GB, 2, NB), F32))
        squares_end = HP * S + S
        assert squares_end >= 4 * S + GB * (2 * NB * C + 2 * NB) + 2 * NB
        _, AQ, KT, VW = per_lane(
            front=(P, (squares_end,), F32), aq=(P, (HP, S), F32), kt=(P, (HP, C), F32), vw=(C, (H, P), F32))
        KN, KQ = per_lane(kn=(C, (H, E), F32), kq=(C, (H, E), F32))
        QSQ, = per_lane(qsq=(P, (HP, S), F32))
        _, SSQ = per_lane(front=(P, (HP * S,), F32), ssq=(H, (S,), F32))
        SIM, OS, SUMS, T8, TT, TH, SV, WH, HW, HWT, SVA = per_lane(
            sim=(P, (NB, 2 * PH * NK), F32), os=(P, (NB, P), F32), sums=(P, (PH, NC), F32),
            t8=(P, (2, PH, TOP), F32), tt=(P, (PH, TOP), F32), th=(P, (PH,), F32), sv=(P, (NE,), F32),
            wh=(P, (WB, NE), F32), hw=(P, (NE,), F32), hwT=(P, (EB, P), F32), sva=(P, (2, NE), F32))

        prep = carve(mem[0], dict(q1_w=(P, (FK, P), F32), q2_w=(P, (F,), F32), q_t=(P, (F,), F32),
                                  p_q=(P, (2 * PH, P), F32), p_keys=(P, (2, 2, P), F32),
                                  p_keysT=(P, (4, P), F32), p_down=(P, (EB, P), F32), a_v=(P, (H * E,), F32),
                                  a_vT=(P, (HP, P), F32), a_o=(P, (HP, P), F32),
                                  q1_n=(P, (FK, P), BF16), q2_n=(P, (F,), BF16),
                                  taps=(P, (2 * P,), F32)))
        q1_w, q2_w, q_t, p_q, p_keys, p_keysT, p_down, a_v, a_vT, a_o, q1_n, q2_n, taps = prep.values()

        p_load = sem("p_load")
        p_const = sem("p_const")
        p_step_dve, p_step_act, p_step_pool = sem("p_step_dve"), sem("p_step_act"), sem("p_step_pool")
        p_pe = sem("p_pe")
        p_act = sem("p_act")
        p_dve = sem("p_dve")
        p_hrow = sem("p_hrow")
        p_late = sem("p_late")
        p_toe = sem("p_toe")

        names = """x_loaded ctx_loaded mask_loaded stored x_ready turned xT_ready u_ready
            conv0 v1_ready y_ready v3_ready o_ready var_ready rstd_ready
            s_ready l_ready p_ready pT_ready q_ready qT_ready h_ready hpre_ready g_ready silu_u
            silu_r d_ready bc_ready ln_ready delta_ready bcs_ready B_ready C_ready dA_ready
            dbu_done scan_done hc_done y_acc yg_ready k_ready ksq_ready kn_ready kT_ready v_ready
            v_sb qsq_ready ssq_ready ssq_sb aq_sb s_drained xr_ready sim_ready sim_sb wh_ready wh_used
            z_ready g_sb hw_ready hwT_ready aq_ready own_done pn_ready wT_ready ssq_turned eo_ready
            eo_drained asum_ready c_sb softplus_step""".split()
        sg = {n: [sem(f"{n}{s}") for s in range(LANES)] for n in names}
        dve_step, act_step = sem("dve_step"), sem("act_step")
        lane_sems = [q for n in names for q in sg[n]] + [dve_step, act_step]

        def column(ap):
            return ap.rearrange("(p o) -> p o", o=1)

        def row(ap):
            return ap.rearrange("(o p) -> o p", o=1)

        def down(ap, n=P):
            return bass.AP(ap.tensor, ap.offset, [[0, n], *[list(d) for d in ap.ap]])

        loads = [
            (f_w1[:], L0_attn_w1),
            (f_b1[:], column(L0_attn_b1)),
            (f_w2[:], L0_attn_w2),
            (f_b2[:], column(L0_attn_b2)),
            (f_w3[:], L0_attn_w3),
            (fb_row[:], row(L0_attn_filt_bias)),
            (q1_w[:], L0_ffn_w1.rearrange("(k p) d -> p k d", p=P)),
            (q2_w[:], L0_ffn_w2),
            (p_keys[:], L1_ffn_keys.rearrange("(t h) k j e -> (h k) t j e", t=2)),
            (p_q[:], L1_ffn_w_q.rearrange("(j e) d -> e j d", e=P)),
            (p_down[:], L1_ffn_expert_down.rearrange("(b p) d -> p b d", p=P)),
            (filt_b[:], column(L0_attn_filt_bias)),
            (w_in[:, 0, :], L0_attn_w_in[:, 0:P]),
            (w_in[:, 1, :], L0_attn_w_in[:, 2 * P:3 * P]),
            (conv_w[:], L0_attn_w_conv.rearrange("(c p) o k -> p c (o k)", p=P)),
            (conv_b[:], L0_attn_b_conv.rearrange("(c p) -> p c", p=P)),
            (in_b[:], L0_attn_b_in.rearrange("(c p) -> p c", p=P)),
            (w_out[:], L0_attn_w_out),
            (m_alog[:], L1_attn_A_log.rearrange("(k p) n -> p k n", p=P)),
            (a_gq[0:E, :], column(L1_xattn_gq)),
            (a_gq[E:2 * E, :], column(L1_xattn_gq)),
            (a_gk[0:E, :], column(L1_xattn_gk)),
            (a_gk[E:2 * E, :], column(L1_xattn_gk)),
            (a_v[:], L1_xattn_Wv.rearrange("d h e -> d (h e)")),
            (a_o[:], L1_xattn_Wo.rearrange("(j t) e d -> (t e) j d", t=2)),
        ]
        late_loads = [
            (b_out[:], down(L0_attn_b_out)),
            (gamma[:], down(L0_xattn_gamma)),
            (beta[:], down(L0_xattn_beta)),
            (b1[:], down(L0_ffn_b1)),
            (b2[:], down(L0_ffn_b2)),
            (m_in[:], L1_attn_W_in),
            (m_delta[:], L1_attn_W_delta.rearrange("(k p) m -> p k m", p=P)),
            (m_bdelta[:], L1_attn_b_delta.rearrange("(k p) -> p k", p=P)),
            (m_bc[:, :, 0:NS], L1_attn_W_B.rearrange("(k p) n -> p k n", p=P)),
            (m_bc[:, :, NS:2 * NS], L1_attn_W_C.rearrange("(k p) n -> p k n", p=P)),
            (m_D[:], L1_attn_D_param.rearrange("(k p) -> p k", p=P)),
            (m_out[:], L1_attn_W_out.rearrange("(k p) m -> p k m", p=P)),
            (a_q[:], L1_xattn_Wq.rearrange("d h e -> d (h e)")),
            (a_k[:], L1_xattn_Wk.rearrange("d h e -> d (h e)")),
            (a_bo[:], down(L1_xattn_bo)),
            (p_up[:], L1_ffn_expert_up.rearrange("(b p) d -> p b d", p=P)),
            (p_norm[:], column(L1_ffn_norm_w)),
        ]
        ALL_LOADED = 16 * len(loads)
        ALL_LATE = 16 * len(late_loads)

        with nc.Block() as block:
            @block.sync
            def _(sp):
                with nc.allow_non_contiguous_dma("small vectors down the partitions"):
                    for to, of in loads[0::2]:
                        sp.dma_start(to, of).then_inc(p_load, 16)
                    for to, of in late_loads:
                        sp.dma_start(to, of).then_inc(p_late, 16)
                sp.wait_ge(p_hrow, 1)
                sp.dma_start(row(h_pad), f_row[:]).then_inc(p_toe, 16)
                sp.wait_ge(p_toe, 16)
                sp.dma_start(taps[:], bass.AP(h_pad.tensor, 0, [[1, P], [1, 2 * P]])).then_inc(p_toe, 16)

            @block.gpsimd
            def _(pool):
                w = Signals(pool, p_step_pool)
                w.link(nc.gpsimd.memset(minus_half[:], -0.5))
                w.link(nc.gpsimd.memset(ones[:], 1.0))
                w.link(nc.gpsimd.memset(ident[:], 0.0))
                w.link(nc.gpsimd.affine_select(out=ident[:], in_=ident[:], compare_op=ALU.not_equal,
                                               fill=1.0, base=0, pattern=[[-1, P]], channel_multiplier=1))
                w.link(nc.gpsimd.memset(row_pick[:], 0.0))
                for g in range(3):
                    w.link(nc.gpsimd.affine_select(
                        out=row_pick[:], in_=row_pick[:], compare_op=ALU.not_equal, fill=1.0,
                        base=-2 * NS * g, pattern=[[-1, 2 * NS], [0, P]], channel_multiplier=1))
                w.link(nc.gpsimd.memset(pair_pick[:], 0.0))
                for j in range(HP):
                    nc.gpsimd.memset(pair_pick[0:E, j, 2 * j:2 * j + 1], 1.0)
                    nc.gpsimd.memset(pair_pick[E:2 * E, j, 2 * j + 1:2 * j + 2], 1.0)
                w.link(nc.gpsimd.memset(f_t[:], 0.0))
                for s in range(LANES):
                    w.link(nc.gpsimd.memset(VE[s][:], 1.0))
                nc.gpsimd.memset(f_row[:], 0.0).then_inc(p_const, 1)

            @block.tensor
            def _(pe):
                w = Signals(pe)
                pe.wait_ge(p_load, ALL_LOADED)
                pe.wait_ge(p_const, 1)
                pe.matmul(PS[0][0:FW, 0, 0:1], f_w1[:], f_t[:], start=True, stop=True).then_inc(p_pe, 1)
                pe.wait_ge(p_dve, 1)
                pe.matmul(PS[0][0:FW, 0, 1:2], f_w2[:], f_h1[:], start=True, stop=True).then_inc(p_pe, 1)
                pe.wait_ge(p_dve, 2)
                pe.matmul(PS[0][0:1, 0, 128:256], f_h2[:], f_w3[:, :], start=True, stop=True).then_inc(p_pe, 1)
                pe.wait_ge(p_dve, 3)
                pe.matmul(PS[0][:, 1, 0:2], ones[:], q_abs[:], start=True, stop=True).then_inc(p_pe, 1)
                for n in range(4):
                    mm = pe.transpose(PS[0][:, 2, n * P:(n + 1) * P], p_keys[:, n // 2, n % 2, :], ident[:])
                mm.then_inc(p_pe, 1)
                for n in range(EB):
                    mm = pe.transpose(PS[1][:, n // 4, (n % 4) * P:(n % 4 + 1) * P], p_down[:, n, :], ident[:])
                mm.then_inc(p_pe, 1)
                pe.wait_ge(p_act, 5)
                for j in range(2):
                    for h in range(PH):
                        c = (j * PH + h) * NK
                        n = (h // 4) * 2 + j
                        mm = pe.matmul(PS[0][:, 3, c:c + NK], p_q[:, 2 * h + j, :],
                                       p_keysT[:, n, (h % 4) * NK:(h % 4 + 1) * NK], start=True, stop=True)
                mm.then_inc(p_pe, 1)
                pe.wait_ge(p_dve, 4)
                for k in range(FK):
                    pe.transpose(PS[1][:, 2, :].bitcast(BF16)[:, k * P:(k + 1) * P], q1_n[:, k, :], ident_bf[:])
                for k in range(FK):
                    mm = pe.transpose(PS[1][:, 3, :].bitcast(BF16)[:, k * P:(k + 1) * P],
                                      q2_n[:, k * P:(k + 1) * P], ident_bf[:])
                mm.then_inc(p_pe, 1)
                pe.wait_ge(p_act, 6)
                for j in range(HP):
                    mm = pe.transpose(PS[1][:, j // 4, (j % 4) * P:(j % 4 + 1) * P], a_v[:, j * P:(j + 1) * P],
                                      ident[:])
                mm.then_inc(p_pe, 1)
                pe.wait_ge(p_act, 8)
                for j in range(HP):
                    for a in range(2):
                        mm = pe.matmul(PS[a][:, 2 + j // 4, (j % 4) * P:(j % 4 + 1) * P],
                                       a_vT[a * E:(a + 1) * E, j, :], a_o[a * E:(a + 1) * E, j, :],
                                       start=True, stop=True)
                mm.then_inc(p_pe, 1)

            @block.scalar
            def _(act):
                w = Signals(act, p_step_act)
                with nc.allow_non_contiguous_dma("small vectors down the partitions"):
                    for to, of in loads[1::2]:
                        act.dma_start(to, of).then_inc(p_load, 16)
                act.wait_ge(p_load, ALL_LOADED)
                act.wait_ge(p_const, 1)
                for n in range(2):
                    act.wait_ge(p_step_dve, n + 1)
                    nc.scalar.activation(f_e[:], f_z[:], ACT.Tanh, scale=0.5).then_inc(p_act, 1)
                w.link(nc.scalar.activation(f_decay[:], fb_row[:], ACT.Abs))
                nc.scalar.activation(f_decay[:], f_decay[:], ACT.Exp, scale=-0.0).then_inc(p_act, 1)
                nc.scalar.activation(m_aexp[:], m_alog[:], ACT.Exp).then_inc(p_act, 1)
                act.wait_ge(p_pe, 5)
                nc.scalar.activation(p_keysT[:].rearrange("p a b -> p (a b)"), PS[0][:, 2, :], ACT.Copy)\
                    .then_inc(p_act, 1)
                act.wait_ge(p_pe, 6)
                nc.scalar.activation(p_downT[:].rearrange("p (a b) -> p a b", a=2), PS[1][:, 0:2, :], ACT.Copy)\
                    .then_inc(p_act, 1)
                act.wait_ge(p_pe, 7)
                nc.scalar.activation(p_m[:], PS[0][:, 3, :], ACT.Copy)
                act.wait_ge(p_pe, 8)
                nc.scalar.activation(q1T[:], PS[1][:, 2, :].bitcast(BF16)[:, 0:F], ACT.Copy)
                nc.scalar.activation(q2T[:].rearrange("p a b -> p (a b)"),
                                     PS[1][:, 3, :].bitcast(BF16)[:, 0:F], ACT.Copy).then_inc(p_act, 1)
                act.wait_ge(p_pe, 9)
                nc.scalar.activation(a_vT[:].rearrange("p (a b) c -> p a (b c)", a=2), PS[1][:, 0:2, :], ACT.Copy)\
                    .then_inc(p_act, 1)
                act.wait_ge(p_pe, 10)
                for a in range(2):
                    for b in range(2):
                        nc.scalar.activation(a_vo[:, 8 * b:8 * b + 8, :].rearrange("p (j a) d -> p a j d", a=2)[:, a],
                                             PS[a][:, 2 + b, :].rearrange("p (j d) -> p j d", d=P), ACT.Copy)

            @block.vector
            def _(dve):
                w = Signals(dve, p_step_dve)
                dve.wait_ge(p_load, ALL_LOADED)
                dve.wait_ge(p_const, 1)
                for n, (b, h) in enumerate([(f_b1, f_h1), (f_b2, f_h2)]):
                    dve.wait_ge(p_pe, n + 1)
                    w.link(nc.vector.tensor_tensor(f_z[:], PS[0][0:FW, 0, n:n + 1], b[:], ALU.add))
                    dve.wait_ge(p_act, n + 1)
                    nc.vector.scalar_tensor_tensor(out=h[:], in0=f_e[:], scalar=1.0, in1=f_z[:],
                                                   op0=ALU.add, op1=ALU.mult)
                    dve.drain()
                    nc.vector.tensor_scalar(h[:], h[:], 0.5, None, ALU.mult).then_inc(p_dve, 1)
                nc.vector.tensor_copy(ident_bf[:], ident[:])
                nc.vector.tensor_reduce(q_abs[:, 0:1], q1_w[:].rearrange("p a b -> p (a b)"), AX.X, ALU.add,
                                        apply_absolute_value=True)
                nc.vector.tensor_reduce(q_abs[:, 1:2], q2_w[:], AX.X, ALU.add,
                                        apply_absolute_value=True).then_inc(p_dve, 1)
                dve.wait_ge(p_pe, 3)
                dve.wait_ge(p_act, 3)
                nc.vector.tensor_tensor(f_row[:, P:2 * P], PS[0][0:1, 0, 128:256][:, ::-1],
                                        f_decay[:, ::-1], ALU.mult).then_inc(p_hrow, 1)
                dve.wait_ge(p_pe, 4)
                w.link(nc.vector.tensor_scalar(q_clip[:], PS[0][:, 1, 0:2], 1.0 / (F * D), 1e-5,
                                               ALU.mult, ALU.max))
                w.link(nc.vector.reciprocal(q_scale[:], q_clip[:]))
                nc.vector.tensor_scalar(q_deq[:], q_clip[:], 1.0 / 127.0, None, ALU.mult)
                for k, (of, to) in enumerate([(q1_w[:].rearrange("p a b -> p (a b)"),
                                               q1_n[:].rearrange("p a b -> p (a b)")), (q2_w[:], q2_n[:])]):
                    w.link(nc.vector.tensor_scalar(q_t[:], of, q_scale[:, k:k + 1], ROUND, ALU.mult, ALU.add))
                    w.link(nc.vector.tensor_scalar(q_t[:], q_t[:], -ROUND, 1.0, ALU.add, ALU.min))
                    last = nc.vector.tensor_scalar(to, q_t[:], -1.0, None, ALU.max)
                    if k == 0:
                        w.link(last)
                last.then_inc(p_dve, 1)
                w.link(nc.vector.tensor_tensor(a_g[:], a_gq[:], a_gk[:], ALU.mult))
                w.link(nc.vector.tensor_scalar(a_g[:], a_g[:], float(E) ** -0.5, None, ALU.mult))
                dve.wait_ge(p_act, 4)
                nc.vector.tensor_scalar(m_A[:], m_aexp[:], -1.0, None, ALU.mult)
                dve.wait_ge(p_toe, 32)
                nc.vector.tensor_copy(toe[:], taps[:, ::-1])

        def in_turn(program):
            runs = [program(s) for s in range(LANES)]
            stage = [next(r) for r in runs]
            while any(n is not None for n in stage):
                s = min((n + LAG * s, s) for s, n in enumerate(stage) if n is not None)[1]
                stage[s] = next(runs[s], None)

        def sublayers(phases):
            def program(s):
                for n, phase in enumerate(phases):
                    for stage in phase(s):
                        yield 100 * n + stage
            return program

        def body(it):
            with nc.Block() as block:
                @block.sync
                def _(sp):
                    for s in range(LANES):
                        i = 2 * it + s
                        sp.dma_start(X[s][:], x[bass.ds(i, 1)].rearrange("o (k p) d -> p (o k) d", p=P))\
                            .then_inc(sg["x_loaded"][s], 16)
                        sp.dma_start(CT[s][:], ctx_1024[bass.ds(i, 1)].rearrange("o c d -> (o c) d"))\
                            .then_inc(sg["ctx_loaded"][s], 16)
                        sp.dma_start(MK[s][:], mask_BxSxS2_ik1[bass.ds(i, 1)]
                                     .rearrange("o (k p) c -> p (o k) c", p=P)).then_inc(sg["mask_loaded"][s], 16)
                    for s in range(LANES):
                        i = 2 * it + s
                        sp.wait_ge(sg["x_ready"][s], 6)
                        sp.dma_start(out[bass.ds(i, 1)].rearrange("o (k p) d -> p (o k) d", p=P), X[s][:])\
                            .then_inc(sg["stored"][s], 16)
                    for s in range(LANES):
                        sp.wait_ge(sg["stored"][s], 16)

                pe_program(block)
                act_program(block)
                dve_program(block)
                pool_program(block)

        def pe_program(block):
            @block.tensor
            def _(pe):
                w = Signals(pe)

                def G(n, s):
                    return sg[n][s]

                def turn(s, of, bank):
                    for k in range(NB):
                        mm = pe.transpose(PS[s][:, bank, k * P:(k + 1) * P], of[:, k, :], ident[:])
                    mm.then_inc(G("turned", s), 1)

                def hyena(s):
                    ps = PS[s]
                    yield 0
                    pe.wait_ge(G("x_loaded", s), 16)
                    turn(s, X[s], 0)
                    pe.wait_ge(G("ctx_loaded", s), 16)
                    pe.transpose(ps[:, 3, 0:C], CT[s][:], ident[0:C, 0:C]).then_inc(G("turned", s), 1)
                    yield 1
                    w.next(G("xT_ready", s))
                    for j in range(2):
                        pe.matmul(ps[:, 1 + j, :], w_in[:, j, :], XT[s][:], start=True, stop=True)\
                            .then_inc(G("u_ready", s), 1)
                    yield 2
                    w.next(G("v1_ready", s))
                    w.next(G("xT_ready", s))
                    for k in range(NB):
                        mm = pe.transpose(ps[:, 3, k * P:(k + 1) * P], V1[s][:, k * P:(k + 1) * P], ident[:])
                    mm.then_inc(G("turned", s), 1)
                    yield 3
                    w.next(G("xT_ready", s))
                    for k in range(NB):
                        n = min(2 * P, S - k * P)
                        mm = pe.matmul(ps[:, 0, k * P:k * P + n], VT[s][:, k, :], toe[:, 0:n],
                                       start=(k == 0), stop=(k == NB - 1), skip_group_check=True)
                    mm.then_inc(G("y_ready", s), 1)
                    yield 4
                    w.next(G("v3_ready", s))
                    for k in range(NB):
                        mm = pe.matmul(ps[:, 1, k * P:(k + 1) * P], V3[s][:, k * P:(k + 1) * P], w_out[:],
                                       start=True, stop=True)
                    mm.then_inc(G("o_ready", s), 1)

                def cross0(s):
                    ps = PS[s]
                    yield 0
                    w.next(G("x_ready", s))
                    turn(s, X[s], 0)
                    yield 1
                    w.next(G("xT_ready", s))
                    for k in range(NB):
                        mm = pe.matmul(ps[:, 1, k * C:(k + 1) * C], XT[s][:, k * P:(k + 1) * P], CTT[s][:],
                                       start=True, stop=True)
                    mm.then_inc(G("s_ready", s), 1)
                    yield 2
                    w.next(G("p_ready", s))
                    for k in range(NB):
                        mm = pe.transpose(ps[0:C, 2, k * P:(k + 1) * P], LE[s][:, k, :], ident[:])
                    mm.then_inc(G("turned", s), 1)
                    yield 3
                    w.next(G("pT_ready", s))
                    for k in range(NB):
                        mm = pe.matmul(ps[:, 3, k * P:(k + 1) * P], PT[s][:, k * P:(k + 1) * P], CT[s][:],
                                       start=True, stop=True)
                    mm.then_inc(G("o_ready", s), 1)

                def bitffn(s):
                    ps = PS[s]
                    yield 1
                    w.next(G("x_ready", s))
                    w.next(G("q_ready", s))
                    for k in range(NB):
                        mm = pe.transpose(ps[:, 0, :].bitcast(BF16)[:, k * P:(k + 1) * P], QB[s][:, k, :],
                                          ident_bf[:])
                    mm.then_inc(G("turned", s), 1)
                    yield 2
                    w.next(G("qT_ready", s))
                    for k in range(NB):
                        pe.matmul(ps[:, k, :], QT[s][:, k * P:(k + 1) * P], q1T[:], start=True, stop=True)\
                            .then_inc(G("h_ready", s), 1)
                    yield 4
                    for k in range(NB):
                        w.next(G("q_ready", s))
                        for j in range(FK):
                            mm = pe.transpose(ps[:, k, :].bitcast(BF16)[:, j * P:(j + 1) * P],
                                              HQ[s][:, k, j * P:(j + 1) * P], ident_bf[:])
                        mm.then_inc(G("turned", s), 1)
                    yield 5
                    w.next(G("qT_ready", s), NB)
                    for k in range(NB):
                        for j in range(FK):
                            mm = pe.matmul(ps[:, 0, k * P:(k + 1) * P], HT[s][:, k, j, :], q2T[:, j, :],
                                           start=(j == 0), stop=(j == FK - 1))
                    mm.then_inc(G("o_ready", s), 1)

                def scan(s):
                    ps = PS[s]
                    pe.wait_ge(p_late, ALL_LATE)
                    yield 0
                    w.next(G("x_ready", s))
                    turn(s, X[s], 0)
                    yield 1
                    w.next(G("xT_ready", s))
                    for j, bank in enumerate([1, 2, 3, 0]):
                        pe.matmul(ps[:, bank, :], m_in[:, j * P:(j + 1) * P], XT[s][:], start=True, stop=True)\
                            .then_inc(G("u_ready", s), 1)
                    yield 2
                    w.next(G("silu_u", s), DJ)
                    for m in range(DJ):
                        for k in range(DJ):
                            mm = pe.matmul(ps[:, 1 + m, :], m_delta[:, k, m * P:(m + 1) * P], UU[s][:, k, :],
                                           start=(k == 0), stop=(k == DJ - 1))
                        mm.then_inc(G("d_ready", s), 1)
                    w.next(G("silu_r", s), DJ)
                    for k in range(DJ):
                        mm = pe.matmul(ps[0:2 * NS, 3, :], m_bc[:, k, :], UU[s][:, k, :],
                                       start=(k == 0), stop=(k == DJ - 1))
                    mm.then_inc(G("bc_ready", s), 1)

                    def broadcast(row_n, bank, ready):
                        pe.matmul(ps[:, bank, :], row_pick[:, row_n, :], BCS[s][:], start=True, stop=True)\
                            .then_inc(G(ready, s), 1)

                    yield 3
                    w.next(G("bcs_ready", s))
                    w.next(G("delta_ready", s))
                    broadcast(0, 0, "B_ready")
                    broadcast(NS, 3, "C_ready")
                    for n in range(NS):
                        yield 4.1 + n
                        if n + 1 < NS:
                            w.next(G("dbu_done", s))
                            broadcast(n + 1, 0, "B_ready")
                        yield 4.5 + n
                        if n + 1 < NS and s == POOL_LANE:
                            w.next(G("c_sb", s))
                            broadcast(NS + n + 1, 3, "C_ready")
                        w.next(G("hc_done", s))
                        if n + 1 < NS and s != POOL_LANE:
                            broadcast(NS + n + 1, 3, "C_ready")
                        for j in range(DJ):
                            mm = pe.matmul(ps[:, 1 + j, :], ident[:], HC[s][:, n % 2, j, :],
                                           start=(n == 0), stop=(n == NS - 1), skip_group_check=True)
                        mm.then_inc(G("y_acc", s), 1)
                    yield 5 + NS
                    w.next(G("yg_ready", s))
                    for k in range(NB):
                        for j in range(DJ):
                            mm = pe.matmul(ps[:, 0, k * P:(k + 1) * P], TU[s][:, j, k * P:(k + 1) * P],
                                           m_out[:, j, :], start=(j == 0), stop=(j == DJ - 1))
                    mm.then_inc(G("o_ready", s), 1)

                def cross1(s):
                    ps = PS[s]
                    yield 0
                    w.next(G("x_ready", s))
                    turn(s, X[s], 0)
                    for j in range(2):
                        pe.matmul(ps[0:C, 1 + j, :], CTT[s][:], a_k[:, j * 512:(j + 1) * 512],
                                  start=True, stop=True).then_inc(G("k_ready", s), 1)

                    def values(n):
                        pe.matmul(ps[0:C, (3, 0)[n % 2], :], CTT[s][:],
                                  a_vo[:, 4 * n:4 * n + 4, :].rearrange("p h d -> p (h d)"), start=True, stop=True)\
                            .then_inc(G("v_ready", s), 1)

                    values(0)
                    yield 1
                    w.next(G("xT_ready", s))
                    values(1)
                    for n in (2, 3):
                        yield 1 + 0.3 * (n - 1)
                        w.next(G("v_sb", s))
                        values(n)
                    yield 2
                    w.next(G("kn_ready", s))
                    for j in range(HP):
                        mm = pe.transpose(ps[:, 1 + j // 4, (j % 4) * C:(j % 4 + 1) * C],
                                          KN[s][:, 2 * j:2 * j + 2, :].rearrange("p a b -> p (a b)"),
                                          ident[0:C, 0:C])
                    mm.then_inc(G("turned", s), 1)

                    def squares(j):
                        w.next(G("qsq_ready", s))
                        return pe.matmul(ps[0:H, 3, :], pair_pick[:, j, :], QSQ[s][:, j, :],
                                         start=(j == 0), stop=(j == HP - 1))

                    for j in range(HP):
                        yield 3 + j
                        if j == 0:
                            w.next(G("v_sb", s), 2)
                        elif j == 1:
                            w.next(G("kT_ready", s))
                        elif j >= 3:
                            w.next(G("aq_sb", s))
                        pe.matmul(ps[:, j % 3, :], a_q[:, j * P:(j + 1) * P], XT[s][:], start=True, stop=True)\
                            .then_inc(G("aq_ready", s), 1)
                        if j >= 1:
                            yield 3.5 + j
                            squares(j - 1)
                    yield 11
                    squares(HP - 1).then_inc(G("ssq_ready", s), 1)
                    yield 12
                    w.next(G("ssq_sb", s))
                    for k in range(NB):
                        mm = pe.transpose(ps[:, 3, k * H:(k + 1) * H], SSQ[s][:, k * P:(k + 1) * P],
                                          ident[0:H, 0:H])
                    mm.then_inc(G("ssq_turned", s), 1)

                    def scores(j):
                        if j >= 1:
                            w.next(G("s_drained", s))
                        for k in range(NB):
                            for a in range(2):
                                mm = pe.matmul(ps[:, a, k * C:(k + 1) * C],
                                               AQ[s][a * E:(a + 1) * E, j, k * P:(k + 1) * P],
                                               KT[s][a * E:(a + 1) * E, j, :], start=True, stop=True)
                        mm.then_inc(G("s_ready", s), 1)

                    def weights_turned(j, a):
                        if a == 0:
                            w.next(G("pn_ready", s))
                        if j or a:
                            w.next(G("wT_ready", s))
                        for k in range(NB):
                            mm = pe.transpose(ps[0:C, 2, k * P:(k + 1) * P], SC[s][:, j % GB, a, k, :], ident[:])
                        mm.then_inc(G("turned", s), 1)

                    def attended(j, a):
                        return pe.matmul(ps[:, 3, :], VW[s][:, 2 * j + a, :], AT[s][:, j % 2, a, :],
                                         start=(j == 0 and a == 0), stop=(j == HP - 1 and a == 1))

                    yield 19
                    w.next(G("aq_sb", s), 3)
                    scores(0)
                    yield 19.15
                    scores(1)
                    for j in range(HP):
                        if j + 2 < HP:
                            yield 20.15 + 3 * j
                            scores(j + 2)
                        yield 21.5 + 3 * j
                        weights_turned(j, 0)
                        if j:
                            attended(j - 1, 1)
                        yield 22 + 3 * j
                        weights_turned(j, 1)
                        attended(j, 0)
                    yield 44
                    w.next(G("wT_ready", s))
                    attended(HP - 1, 1).then_inc(G("aq_ready", s), 1)
                    yield 46
                    w.next(G("xT_ready", s))
                    w.next(G("s_drained", s))
                    for k in range(NB):
                        mm = pe.transpose(ps[:, 0, k * P:(k + 1) * P], XT[s][:, k * P:(k + 1) * P], ident[:])
                    mm.then_inc(G("o_ready", s), 1)

                def experts(s):
                    ps = PS[s]
                    yield 1
                    w.next(G("x_ready", s))
                    w.next(G("xr_ready", s))
                    turn(s, R[s], 0)
                    yield 2
                    w.next(G("xT_ready", s))
                    for k in range(NB):
                        pe.matmul(ps[:, k, :], XT[s][:, k * P:(k + 1) * P], p_m[:], start=True, stop=True)\
                            .then_inc(G("sim_ready", s), 1)

                    def expert_inputs(k):
                        for j in range(2):
                            pe.matmul(ps[:, 2 + j, :], XT[s][:, k * P:(k + 1) * P], p_downT[:, j * 512:(j + 1) * 512],
                                      start=True, stop=True).then_inc(G("z_ready", s), 1)

                    yield 3
                    w.next(G("sim_sb", s), NB)
                    expert_inputs(0)
                    for k in range(NB):
                        for h in range(PH):
                            yield 10.6 + 20 * k + h
                            w.next(G("wh_ready", s))
                            for j in range(2):
                                mm = pe.matmul(ps[:, j, :], ident[:], WH[s][:, h % WB, j * 512:(j + 1) * 512],
                                               start=(h == 0), stop=(h == PH - 1), skip_group_check=True)
                            mm.then_inc(G("wh_used", s), 1)
                        yield 18 + 20 * k
                        w.next(G("hw_ready", s))
                        for e in range(EB):
                            mm = pe.transpose(ps[:, 2 + e // 4, (e % 4) * P:(e % 4 + 1) * P],
                                              HW[s][:, e * P:(e + 1) * P], ident[:])
                        mm.then_inc(G("turned", s), 1)
                        yield 19 + 20 * k
                        w.next(G("hwT_ready", s))
                        for e in range(EB):
                            mm = pe.matmul(ps[:, 2, 0:P], HWT[s][:, e, :], p_up[:, e, :],
                                           start=(e == 0), stop=(e == EB - 1))
                        mm.then_inc(G("eo_ready", s), 1)
                        yield 20 + 20 * k
                        w.next(G("eo_drained", s))
                        if k + 1 < NB:
                            expert_inputs(k + 1)

                in_turn(sublayers([hyena, cross0, bitffn, scan, cross1, experts]))

        def act_program(block):
            @block.scalar
            def _(act):
                w = Signals(act, act_step)

                def G(n, s):
                    return sg[n][s]

                def copy(to, of, signal=None, **kw):
                    ins = nc.scalar.activation(to, of, ACT.Copy, **kw)
                    if signal is not None:
                        ins.then_inc(signal, 1)
                    return ins

                def turned(s, to, of, ready, **kw):
                    w.next(G("turned", s))
                    copy(to, of, G(ready, s), **kw)

                def hyena(s):
                    ps = PS[s]
                    yield 0
                    turned(s, XT[s][:], ps[:, 0, :], "xT_ready")
                    turned(s, CTT[s][:], ps[:, 3, 0:C], "xT_ready")
                    yield 1
                    for j, c in enumerate((0, 2)):
                        w.next(G("u_ready", s))
                        w.link(nc.scalar.activation(U[s][:, j, :], ps[:, 1 + j, :], ACT.Identity,
                                                    bias=in_b[:, c:c + 1]))
                        nc.scalar.activation(CV[s][:, j, :], U[s][:, j, :], ACT.Identity,
                                             bias=conv_b[:, c:c + 1], scale=conv_w[:, c, 2:3])\
                            .then_inc(G("conv0", s), 1)
                    yield 2
                    turned(s, VT[s][:].rearrange("p a b -> p (a b)"), ps[:, 3, :], "xT_ready")

                def cross0(s):
                    ps = PS[s]
                    yield 0
                    turned(s, XT[s][:], ps[:, 0, :], "xT_ready")
                    yield 1
                    w.next(G("l_ready", s))
                    nc.scalar.activation(LE[s][:], LG[s][:], ACT.Exp).then_inc(G("p_ready", s), 1)
                    yield 2
                    turned(s, PT[s][:], ps[0:C, 2, :], "pT_ready")

                def bitffn(s):
                    ps = PS[s]
                    yield 1
                    turned(s, QT[s][:], ps[:, 0, :].bitcast(BF16)[:, 0:S], "qT_ready")
                    yield 2
                    for k in range(NB):
                        w.next(G("hpre_ready", s))
                        w.link(nc.scalar.activation(BIG2[s][:, k, :], BIG1[s][:, k, :], ACT.Gelu))
                        nc.scalar.activation(BIG1[s][:, k, :], BIG2[s][:, k, :], ACT.Square,
                                             accum_out=ST[s][:, 4, k:k + 1]).then_inc(G("g_ready", s), 1)
                    yield 4
                    for k in range(NB):
                        turned(s, HT[s][:, k].rearrange("p a b -> p (a b)"),
                               ps[:, k, :].bitcast(BF16)[:, 0:F], "qT_ready")

                def scan(s):
                    ps = PS[s]
                    act.wait_ge(p_late, ALL_LATE)
                    yield 0
                    turned(s, XT[s][:], ps[:, 0, :], "xT_ready")
                    yield 1
                    for j, bank in enumerate([1, 2, 3, 0]):
                        w.next(G("u_ready", s))
                        to = TU[s] if j < DJ else TR[s]
                        nc.scalar.activation(to[:, j % DJ, :], ps[:, bank, :], ACT.Tanh, scale=0.5)\
                            .then_inc(G("g_ready", s), 1)
                    yield 2
                    for j in range(DJ):
                        w.next(G("d_ready", s))
                        ins = nc.scalar.activation(SPA[s][:, j, :], ps[:, 1 + j, :], ACT.Abs,
                                                   bias=m_bdelta[:, j:j + 1])
                        ins.then_inc(G("softplus_step", s), 1)
                    yield 2.2
                    w.next(G("softplus_step", s), DJ)
                    nc.scalar.activation(SPE[s][:], SPA[s][:], ACT.Exp, scale=-1.0).then_inc(G("softplus_step", s), 1)
                    yield 2.4
                    w.next(G("softplus_step", s))
                    nc.scalar.activation(SPA[s][:], SPE[s][:], ACT.Ln, bias=1.0).then_inc(G("ln_ready", s), 1)
                    for n in range(NS):
                        yield 3 + n
                        if n == 0:
                            w.next(G("delta_ready", s))
                        if n >= 2:
                            w.next(G("scan_done", s))
                        for j in range(DJ):
                            ins = nc.scalar.activation(dA[s][:, n % 2, j, 1:S], DL[s][:, j, 1:S], ACT.Exp,
                                                       scale=m_A[:, j, n:n + 1])
                        ins.then_inc(G("dA_ready", s), 1)
                        if s == POOL_LANE:
                            yield 3.6 + n
                            w.next(G("C_ready", s))
                            if n >= 1:
                                w.next(G("hc_done", s))
                            copy(CSB[s][:], ps[:, 3, :], G("c_sb", s))

                def cross1(s):
                    ps = PS[s]
                    yield 0
                    turned(s, XT[s][:], ps[:, 0, :], "xT_ready")
                    for j in range(2):
                        w.next(G("k_ready", s))
                        nc.scalar.activation(KQ[s][:].rearrange("p a b -> p (a b)")[:, j * 512:(j + 1) * 512],
                                             ps[0:C, 1 + j, :], ACT.Square).then_inc(G("ksq_ready", s), 1)
                    yield 1
                    for n in range(4):
                        yield 1 + 0.3 * max(n - 1, 0)
                        w.next(G("v_ready", s))
                        copy(VW[s][:, 4 * n:4 * n + 4, :].rearrange("p h d -> p (h d)"),
                             ps[0:C, (3, 0)[n % 2], :], G("v_sb", s))
                    yield 2
                    turned(s, KT[s][:].rearrange("p (a b) c -> p a (b c)", a=2), ps[:, 1:3, 0:4 * C],
                           "kT_ready", scale=a_g[:, 0:1])
                    for j in range(HP):
                        yield 3.2 + j
                        w.next(G("aq_sb", s))
                        nc.scalar.activation(QSQ[s][:, j, :], AQ[s][:, j, :], ACT.Square)\
                            .then_inc(G("qsq_ready", s), 1)
                    yield 11.5
                    w.next(G("ssq_ready", s))
                    copy(SSQ[s][:], ps[0:H, 3, :], G("ssq_sb", s))

                    def exponentials(j):
                        w.next(G("l_ready", s))
                        nc.scalar.activation(SC[s][:, j % GB].rearrange("p a b c -> p (a b c)"),
                                             SC[s][:, j % GB].rearrange("p a b c -> p (a b c)"), ACT.Exp)\
                            .then_inc(G("p_ready", s), 1)

                    yield 19.3
                    exponentials(0)
                    for j in range(HP):
                        yield 20.3 + 3 * j
                        if j + 1 < HP:
                            exponentials(j + 1)
                        for a in range(2):
                            yield 21.5 + 3 * j + 0.5 * a
                            turned(s, AT[s][:, j % 2, a, :], ps[0:C, 2, :], "wT_ready")
                    yield 45
                    w.next(G("aq_ready", s), HP + 1)
                    copy(XT[s][:], ps[:, 3, :], G("xT_ready", s))

                def experts(s):
                    ps = PS[s]
                    yield 1
                    turned(s, XT[s][:], ps[:, 0, :], "xT_ready", scale=p_norm[:, 0:1])
                    yield 2
                    for k in range(NB):
                        w.next(G("sim_ready", s))
                        copy(SIM[s][:, k, :], ps[:, k, :], G("sim_sb", s))

                    def activations():
                        w.next(G("z_ready", s), 2)
                        nc.scalar.activation(HW[s][:].rearrange("p (a b) -> p a b", a=2), ps[:, 2:4, :], ACT.Gelu)\
                            .then_inc(G("g_sb", s), 1)

                    def sums(k, h):
                        n = k * len(ACT_HEADS) + ACT_HEADS.index(h)
                        if n >= 2:
                            last = n - 2
                            act.wait_ge(G("wh_ready", s), last // len(ACT_HEADS) * PH
                                        + ACT_HEADS[last % len(ACT_HEADS)] + 1)
                        sims = SIM[s][:, k, :].rearrange("p (a h n) -> p a h n", a=2, h=PH)
                        for i in range(NK):
                            ins = nc.scalar.activation(SVA[s][:, n % 2, i * NK:(i + 1) * NK], sims[:, 1, h, :],
                                                       ACT.Identity, bias=sims[:, 0, h, i:i + 1])
                        ins.then_inc(G("asum_ready", s), 1)

                    yield 3
                    w.next(G("sim_sb", s), NB)
                    activations()
                    for k in range(NB):
                        for h in ACT_HEADS:
                            yield 9.3 + 20 * k + h
                            sums(k, h)
                        yield 18 + 20 * k
                        w.next(G("turned", s))
                        copy(HWT[s][:].rearrange("p (a b) c -> p a (b c)", a=2), ps[:, 2:4, :], G("hwT_ready", s))
                        yield 19 + 20 * k
                        w.next(G("eo_ready", s))
                        copy(OS[s][:, k, :], ps[:, 2, 0:P], G("eo_drained", s))
                        yield 20 + 20 * k
                        if k + 1 < NB:
                            activations()

                in_turn(sublayers([hyena, cross0, bitffn, scan, cross1, experts]))

        def dve_program(block):
            @block.vector
            def _(dve):
                w = Signals(dve, dve_step)

                def G(n, s):
                    return sg[n][s]

                def statistics(s, of, eps):
                    for k in range(NB):
                        ins = nc.vector.bn_stats(BNS[s][:, k, :], of[:, k, :])
                    w.link(ins)
                    for k in range(NB):
                        ins = nc.vector.bn_aggr(MV[s][:, k, :], BNS[s][:, k, :])
                    w.link(ins)
                    nc.vector.tensor_scalar(VE[s][:, 0:NB], MV[s][:, :, 1], eps, None, ALU.add)\
                        .then_inc(G("var_ready", s), 1)

                def normalised(s, of, to):
                    w.next(G("rstd_ready", s))
                    for k in range(NB):
                        ins = nc.vector.tensor_scalar(to[:, k, :], of[:, k, :], MV[s][:, k, 0:1],
                                                      RS[s][:, k:k + 1], ALU.subtract, ALU.mult)
                    return ins

                def residual(s, of, bias):
                    w.link(nc.vector.tensor_tensor(R[s][:], of, X[s][:], ALU.add))
                    if bias is not None:
                        w.link(nc.vector.tensor_tensor(R[s][:], R[s][:], spread(bias[:], 1, NB), ALU.add))
                    statistics(s, R[s], 1e-5)

                def new_x(s):
                    normalised(s, R[s], X[s]).then_inc(G("x_ready", s), 1)
                    w.next(G("x_ready", s))

                def bank(s, n):
                    return PS[s][:, n, :].rearrange("p (k d) -> p k d", k=NB)

                def hyena(s):
                    ps = PS[s]
                    yield 1
                    dve.wait_ge(G("x_loaded", s), 16)
                    for j, c in enumerate((0, 2)):
                        w.next(G("conv0", s))
                        w.link(nc.vector.scalar_tensor_tensor(
                            out=CV[s][:, j, 1:S], in0=U[s][:, j, 0:S - 1], scalar=conv_w[:, c, 1:2],
                            in1=CV[s][:, j, 1:S], op0=ALU.mult, op1=ALU.add))
                        w.link(nc.vector.scalar_tensor_tensor(
                            out=CV[s][:, j, 2:S], in0=U[s][:, j, 0:S - 2], scalar=conv_w[:, c, 0:1],
                            in1=CV[s][:, j, 2:S], op0=ALU.mult, op1=ALU.add))
                    nc.vector.tensor_tensor(V1[s][:], CV[s][:, 1, :], CV[s][:, 0, :], ALU.mult)\
                        .then_inc(G("v1_ready", s), 1)
                    w.next(G("v1_ready", s))
                    dve.wait_ge(G("mask_loaded", s), 16)
                    nc.vector.tensor_scalar(PEN[s][:], MK[s][:], 0, MASKED, ALU.is_equal, ALU.mult)
                    yield 3
                    w.next(G("y_ready", s))
                    w.link(nc.vector.scalar_tensor_tensor(out=V2[s][:], in0=V1[s][:], scalar=filt_b[:, 0:1],
                                                          in1=ps[:, 0, :], op0=ALU.mult, op1=ALU.add))
                    nc.vector.tensor_tensor(V3[s][:], V2[s][:], CV[s][:, 0, :], ALU.mult)\
                        .then_inc(G("v3_ready", s), 1)
                    yield 4
                    dve.wait_ge(p_late, ALL_LATE)
                    w.next(G("o_ready", s))
                    residual(s, bank(s, 1), b_out)
                    yield 5
                    new_x(s)

                def cross0(s):
                    yield 1
                    w.next(G("s_ready", s))
                    w.link(nc.vector.scalar_tensor_tensor(
                        out=LG[s][:], in0=PS[s][:, 1, 0:NB * C].rearrange("p (k c) -> p k c", k=NB),
                        scalar=float(D) ** -0.5, in1=PEN[s][:], op0=ALU.mult, op1=ALU.add))
                    w.link(nc.vector.tensor_reduce(ST[s][:, 0, :], LG[s][:], AX.X, ALU.max))
                    nc.vector.tensor_tensor(LG[s][:], LG[s][:], spread(ST[s][:, 0, :], 2, C), ALU.subtract)\
                        .then_inc(G("l_ready", s), 1)
                    yield 2
                    w.next(G("p_ready", s))
                    w.link(nc.vector.tensor_reduce(ST[s][:, 1, :], LE[s][:], AX.X, ALU.add))
                    w.link(nc.vector.reciprocal(ST[s][:, 2, :], ST[s][:, 1, :]))
                    yield 3
                    w.next(G("o_ready", s))
                    w.link(nc.vector.tensor_tensor(R2[s][:], bank(s, 3), spread(ST[s][:, 2, :], 2, P), ALU.mult))
                    statistics(s, R2[s], 1e-5)
                    yield 4
                    w.link(normalised(s, R2[s], R2[s]))
                    w.link(nc.vector.tensor_tensor(R2[s][:], R2[s][:], spread(gamma[:], 1, NB), ALU.mult))
                    w.link(nc.vector.tensor_tensor(R2[s][:], R2[s][:], spread(beta[:], 1, NB), ALU.add))
                    residual(s, R2[s][:], None)
                    yield 5
                    new_x(s)

                def mean_squares(s, source, n):
                    nc.vector.tensor_scalar(VE[s][:, 0:NB], source, 1.0 / n, 1e-6, ALU.mult, ALU.add)\
                        .then_inc(G("var_ready", s), 1)

                def quantise_scales(s, deq):
                    w.next(G("rstd_ready", s))
                    w.link(nc.vector.tensor_tensor(ST[s][:, 1, :], ST[s][:, 0, :], RS[s][:, 0:NB], ALU.mult))
                    w.link(nc.vector.tensor_scalar(ST[s][:, 1, :], ST[s][:, 1, :], 1e-5, None, ALU.max))
                    w.link(nc.vector.reciprocal(ST[s][:, 3, :], ST[s][:, 1, :]))
                    nc.vector.tensor_scalar(ST[s][:, 5, :], ST[s][:, 1, :], deq, None, ALU.mult)
                    w.link(nc.vector.tensor_scalar(ST[s][:, 3, :], ST[s][:, 3, :], 127.0, None, ALU.mult))

                def bitffn(s):
                    ps = PS[s]
                    yield 0
                    w.link(nc.vector.tensor_tensor(R2[s][:], X[s][:], X[s][:], ALU.mult))
                    nc.vector.tensor_reduce(ST[s][:, 0, :], X[s][:], AX.X, ALU.max, apply_absolute_value=True)
                    w.link(nc.vector.tensor_reduce(ST[s][:, 2, :], R2[s][:], AX.X, ALU.add))
                    mean_squares(s, ST[s][:, 2, :], D)
                    yield 1
                    quantise_scales(s, q_deq[:, 0:1])
                    for k in range(NB):
                        ins = nc.vector.tensor_scalar(QF[s][:, k, :], X[s][:, k, :], RS[s][:, k:k + 1],
                                                      ST[s][:, 3, k:k + 1], ALU.mult, ALU.mult)
                    w.link(ins)
                    nc.vector.tensor_scalar(QB[s][:], QF[s][:], ROUND, -ROUND, ALU.add, ALU.add)\
                        .then_inc(G("q_ready", s), 1)
                    yield 2
                    for k in range(NB):
                        w.next(G("h_ready", s))
                        nc.vector.scalar_tensor_tensor(out=BIG1[s][:, k, :], in0=ps[:, k, :],
                                                       scalar=ST[s][:, 5, k:k + 1], in1=b1[:],
                                                       op0=ALU.mult, op1=ALU.add).then_inc(G("hpre_ready", s), 1)
                    yield 3
                    w.next(G("g_ready", s), NB)
                    nc.vector.tensor_reduce(ST[s][:, 0, :], BIG2[s], AX.X, ALU.max, apply_absolute_value=True)
                    mean_squares(s, ST[s][:, 4, :], F)
                    yield 4
                    quantise_scales(s, q_deq[:, 1:2])
                    for k in range(NB):
                        w.link(nc.vector.tensor_scalar(BIG1[s][:, k, :], BIG2[s][:, k, :], RS[s][:, k:k + 1],
                                                       ST[s][:, 3, k:k + 1], ALU.mult, ALU.mult))
                        nc.vector.tensor_scalar(HQ[s][:, k, :], BIG1[s][:, k, :], ROUND, -ROUND,
                                                ALU.add, ALU.add).then_inc(G("q_ready", s), 1)
                    yield 5
                    w.next(G("o_ready", s))
                    w.link(nc.vector.tensor_tensor(R2[s][:], bank(s, 0), spread(ST[s][:, 5, :], 2, P), ALU.mult))
                    w.link(nc.vector.tensor_tensor(R2[s][:], R2[s][:], spread(b2[:], 1, NB), ALU.add))
                    residual(s, R2[s][:], None)
                    yield 6
                    new_x(s)

                def scan(s):
                    ps = PS[s]
                    yield 1
                    for j, b in enumerate([1, 2, 3, 0]):
                        w.next(G("u_ready", s))
                        w.next(G("g_ready", s))
                        t = TU[s] if j < DJ else TR[s]
                        ins = nc.vector.scalar_tensor_tensor(out=t[:, j % DJ, :], in0=t[:, j % DJ, :], scalar=1.0,
                                                             in1=ps[:, b, :], op0=ALU.add, op1=ALU.mult)
                        if j < DJ:
                            w.link(ins)
                            nc.vector.tensor_scalar(UU[s][:, j, :], t[:, j, :], 0.5, None, ALU.mult)\
                                .then_inc(G("silu_u", s), 1)
                        else:
                            ins.then_inc(G("silu_r", s), 1)
                    w.next(G("silu_u", s), DJ)
                    yield 2
                    w.next(G("bc_ready", s))
                    bc = ps[0:2 * NS, 3, :]
                    w.link(nc.vector.tensor_copy(BCS[s][0:2 * NS, :], bc))
                    w.link(nc.vector.tensor_tensor(BC1[s][:], bc, BCS[s][0:2 * NS, :], ALU.subtract))
                    w.link(nc.vector.tensor_copy(BCM[s][:], BC1[s][:]))
                    nc.vector.tensor_copy(BCS[s][2 * NS:4 * NS, :], BCM[s][:])
                    nc.vector.tensor_tensor(BCS[s][4 * NS:6 * NS, :], BC1[s][:], BCM[s][:], ALU.subtract)\
                        .then_inc(G("bcs_ready", s), 1)
                    w.next(G("d_ready", s), DJ)
                    w.next(G("softplus_step", s), DJ)
                    for j in range(DJ):
                        nc.vector.tensor_scalar(DL[s][:, j, :], ps[:, 1 + j, :], m_bdelta[:, j:j + 1], 0.0,
                                                ALU.add, ALU.max).then_inc(G("own_done", s), 1)
                    yield 2.5
                    w.next(G("own_done", s), DJ)
                    w.next(G("ln_ready", s))
                    w.link(nc.vector.tensor_tensor(DL[s][:], DL[s][:], SPA[s][:], ALU.add))
                    nc.vector.memset(dA[s][:, :, :, 0:1], 0.0).then_inc(G("delta_ready", s), 1)
                    w.next(G("delta_ready", s))
                    w.link(nc.vector.tensor_tensor(DU[s][:], DL[s][:], UU[s][:], ALU.mult))
                    flat = "p a b -> p (a b)"
                    for n in range(NS):
                        yield 4 + n
                        w.next(G("B_ready", s))
                        nc.vector.tensor_tensor(dBu[s][:], DU[s][:], spread(ps[:, 0, :], 1, DJ), ALU.mult)\
                            .then_inc(G("dbu_done", s), 1)
                        yield 4.2 + n
                        w.next(G("dbu_done", s))
                        w.next(G("dA_ready", s))
                        hs = (HS, TU)[n % 2][s]
                        if s == POOL_LANE and n >= 2:
                            w.next(G("hc_done", s))
                        nc.vector.tensor_tensor_scan(hs[:].rearrange(flat), dA[s][:, n % 2].rearrange(flat),
                                                     dBu[s][:].rearrange(flat), 0.0, ALU.mult, ALU.add)\
                            .then_inc(G("scan_done", s), 1)
                        if s == POOL_LANE:
                            continue
                        yield 4.4 + n
                        w.next(G("scan_done", s))
                        w.next(G("C_ready", s))
                        if n >= 2:
                            w.next(G("y_acc", s))
                        nc.vector.tensor_tensor(HC[s][:, n % 2], hs[:], spread(ps[:, 3, :], 1, DJ), ALU.mult)\
                            .then_inc(G("hc_done", s), 1)
                    yield 5 + NS
                    w.next(G("y_acc", s), NS if s == POOL_LANE else 2)
                    for j in range(DJ):
                        ins = nc.vector.scalar_tensor_tensor(out=TU[s][:, j, :], in0=UU[s][:, j, :],
                                                             scalar=m_D[:, j:j + 1], in1=ps[:, 1 + j, :],
                                                             op0=ALU.mult, op1=ALU.add)
                    w.link(ins)
                    nc.vector.scalar_tensor_tensor(out=TU[s][:], in0=TU[s][:], scalar=0.5, in1=TR[s][:],
                                                   op0=ALU.mult, op1=ALU.mult).then_inc(G("yg_ready", s), 1)
                    yield 6 + NS
                    w.next(G("o_ready", s))
                    residual(s, bank(s, 0), None)
                    yield 7 + NS
                    new_x(s)

                def cross1(s):
                    ps = PS[s]
                    yield 1
                    w.next(G("ksq_ready", s), 2)
                    w.link(nc.vector.tensor_reduce(VE[s][0:C, 0:H], KQ[s][:], AX.X, ALU.add))
                    nc.vector.tensor_scalar(VE[s][0:C, 0:H], VE[s][0:C, 0:H], 1.0 / E, 1e-6,
                                            ALU.mult, ALU.add).then_inc(G("var_ready", s), 1)
                    yield 2
                    w.next(G("rstd_ready", s))
                    w.next(G("k_ready", s), 2)
                    for j in range(2):
                        ins = nc.vector.tensor_tensor(
                            KN[s][:, j * 8:(j + 1) * 8, :], ps[0:C, 1 + j, :].rearrange("p (a b) -> p a b", b=E),
                            spread(RS[s][0:C, j * 8:(j + 1) * 8], 2, E), ALU.mult)
                    ins.then_inc(G("kn_ready", s), 1)
                    for j in range(HP):
                        yield 3 + j
                        w.next(G("aq_ready", s))
                        nc.vector.tensor_copy(AQ[s][:, j, :], ps[:, j % 3, :]).then_inc(G("aq_sb", s), 1)
                    yield 12.5
                    w.next(G("ssq_turned", s))
                    nc.vector.tensor_scalar(VE[s][:, 0:NB * H].rearrange("p (h k) -> p k h", k=NB),
                                            ps[:, 3, 0:NB * H].rearrange("p (k h) -> p k h", h=H), 1.0 / E, 1e-6,
                                            ALU.mult, ALU.add).then_inc(G("var_ready", s), 1)

                    def logits(j):
                        raw = ps[:, 0:2, 0:NB * C].rearrange("p a (k c) -> p a k c", c=C)
                        to = SC[s][:, j % GB]
                        w.next(G("s_ready", s))
                        nc.vector.tensor_reduce(MX[s][:], raw, AX.X, ALU.max).then_inc(G("own_done", s), 1)
                        yield 0.1
                        w.next(G("own_done", s))
                        if j >= GB:
                            w.next(G("wT_ready", s), 2)
                        nc.vector.tensor_tensor(to, raw, spread(MX[s], 3, C), ALU.subtract)\
                            .then_inc(G("s_drained", s), 1)
                        yield 0.2
                        w.next(G("s_drained", s))
                        w.next(G("rstd_ready", s))
                        rs = RS[s][:, 2 * j * NB:2 * (j + 1) * NB].rearrange("p (a k) -> p a k", k=NB)
                        nc.vector.tensor_tensor(to, to, spread(rs, 3, C), ALU.mult).then_inc(G("l_ready", s), 1)

                    def probabilities(j):
                        p, rd = SC[s][:, j % GB], RD[s][:, j % GB]
                        w.next(G("p_ready", s))
                        nc.vector.tensor_reduce(rd, p, AX.X, ALU.add).then_inc(G("own_done", s), 1)
                        yield 0.1
                        w.next(G("own_done", s))
                        nc.vector.reciprocal(rd, rd).then_inc(G("own_done", s), 1)
                        yield 0.2
                        w.next(G("own_done", s))
                        nc.vector.tensor_tensor(p, p, spread(rd, 3, C), ALU.mult).then_inc(G("pn_ready", s), 1)

                    def staged(stage, steps):
                        yield stage
                        for n in steps:
                            yield stage + n

                    yield from staged(19, logits(0))
                    for j in range(HP):
                        if j + 1 < HP:
                            yield from staged(20 + 3 * j, logits(j + 1))
                        yield from staged(21 + 3 * j, probabilities(j))
                    yield 50
                    w.next(G("o_ready", s))
                    residual(s, bank(s, 0), a_bo)
                    yield 51
                    new_x(s)

                def experts(s):
                    ps = PS[s]
                    yield 0
                    w.link(nc.vector.tensor_tensor(R2[s][:], X[s][:], X[s][:], ALU.mult))
                    w.link(nc.vector.tensor_reduce(ST[s][:, 2, :], R2[s][:], AX.X, ALU.add))
                    mean_squares(s, ST[s][:, 2, :], D)
                    yield 1
                    w.next(G("rstd_ready", s))
                    for k in range(NB):
                        ins = nc.vector.tensor_scalar(R[s][:, k, :], X[s][:, k, :], RS[s][:, k:k + 1], None, ALU.mult)
                    ins.then_inc(G("xr_ready", s), 1)

                    def best_keys(k):
                        w.next(G("sim_sb", s))
                        sims = SIM[s][:, k, :].rearrange("p (a h n) -> p a h n", a=2, h=PH)
                        for a in range(2):
                            for h in range(PH):
                                ins = nc.vector.max(T8[s][:, a, h, :], sims[:, a, h, :])
                        ins.then_inc(G("own_done", s), 1)

                    def thresholds(k):
                        w.next(G("own_done", s))
                        c = 0
                        for i0, i1, nj in CANDIDATES:
                            n = (i1 - i0) * nj
                            ins = nc.vector.tensor_tensor(
                                SUMS[s][:, :, c:c + n].rearrange("p h (i j) -> p h i j", j=nj),
                                spread(T8[s][:, 0, :, i0:i1], 3, nj), spread(T8[s][:, 1, :, 0:nj], 2, i1 - i0),
                                ALU.add)
                            c += n
                        w.link(ins)
                        for h in range(PH):
                            ins = nc.vector.max(TT[s][:, h, :], SUMS[s][:, h, :])
                        w.link(ins)
                        w.link(nc.vector.tensor_scalar(TH[s][:], TT[s][:, :, TOP - 1], 0.0, None, ALU.max))

                    yield 3
                    best_keys(0)
                    yield 3.5
                    thresholds(0)
                    for k in range(NB):
                        sims = SIM[s][:, k, :].rearrange("p (a h n) -> p a h n", a=2, h=PH)
                        for h in range(PH):
                            yield 10 + 20 * k + h
                            if k or h:
                                w.next(G("wh_ready", s))
                            if h in ACT_HEADS:
                                yield 10.5 + 20 * k + h
                                w.next(G("asum_ready", s))
                                sv = SVA[s][:, (k * len(ACT_HEADS) + ACT_HEADS.index(h)) % 2, :]
                            else:
                                sv = SV[s][:]
                                nc.vector.tensor_tensor(sv.rearrange("p (i j) -> p i j", i=NK),
                                                        spread(sims[:, 0, h, :], 2, NK),
                                                        spread(sims[:, 1, h, :], 1, NK), ALU.add)\
                                    .then_inc(G("own_done", s), 1)
                                yield 10.5 + 20 * k + h
                                w.next(G("own_done", s))
                            if k * PH + h >= WB:
                                w.next(G("wh_used", s))
                            nc.vector.scalar_tensor_tensor(
                                out=WH[s][:, h % WB, :], in0=sv, scalar=TH[s][:, h:h + 1], in1=sv,
                                op0=ALU.is_ge, op1=ALU.mult).then_inc(G("wh_ready", s), 1)
                        if k + 1 < NB:
                            yield 17.9 + 20 * k
                            best_keys(k + 1)
                        yield 18 + 20 * k
                        dve.wait_ge(G("wh_used", s), (k + 1) * PH)
                        w.next(G("g_sb", s))
                        nc.vector.tensor_tensor(HW[s][:], HW[s][:], ps[:, 0:2, :].rearrange("p a b -> p (a b)"),
                                                ALU.mult).then_inc(G("hw_ready", s), 1)
                        if k + 1 < NB:
                            yield 19 + 20 * k
                            thresholds(k + 1)
                    yield 94
                    w.next(G("eo_drained", s), NB)
                    residual(s, OS[s][:], None)
                    yield 95
                    new_x(s)

                in_turn(sublayers([hyena, cross0, bitffn, scan, cross1, experts]))

        def pool_program(block):
            @block.gpsimd
            def _(pool):
                w = Signals(pool)

                def rsqrt(s, rows, n, i=0):
                    if i == 0:
                        w.next(sg["var_ready"][s])
                    nc.gpsimd.tensor_tensor(RS[s][0:rows, i * n:(i + 1) * n], VE[s][0:rows, i * n:(i + 1) * n],
                                            minus_half[0:rows, 0:n], ALU.pow)\
                        .then_inc(sg["rstd_ready"][s], 1)

                def program(s):
                    for stage in (4, 103, 104, 200, 203, 205):
                        yield stage
                        rsqrt(s, P, NB)
                    if s == POOL_LANE:
                        for n in range(NS):
                            yield 304.45 + n
                            w.next(sg["scan_done"][s])
                            w.next(sg["c_sb"][s])
                            if n >= 2:
                                w.next(sg["y_acc"][s])
                            nc.gpsimd.tensor_tensor(HC[s][:, n % 2], (HS, TU)[n % 2][s][:],
                                                    spread(CSB[s][:], 1, DJ), ALU.mult)\
                                .then_inc(sg["hc_done"][s], 1)
                    yield 306 + NS
                    rsqrt(s, P, NB)
                    yield 401
                    rsqrt(s, C, H)
                    for j in range(HP):
                        yield 413 + 0.1 * j
                        rsqrt(s, P, 2 * NB, j)
                    for stage in (450, 500, 594):
                        yield stage
                        rsqrt(s, P, NB)

                in_turn(program)

        with nc.Fori(0, B // LANES) as it:
            body(it)
            for q in lane_sems:
                nc.gpsimd.sem_clear(q)
            nc.all_engine_barrier()


_INS = ['x', 'ctx_1024', 'mask_BxSxS2_ik1', 'L0_attn_w_in', 'L0_attn_b_in', 'L0_attn_w_conv',
        'L0_attn_b_conv', 'L0_attn_w1', 'L0_attn_b1', 'L0_attn_w2', 'L0_attn_b2', 'L0_attn_w3',
        'L0_attn_filt_bias', 'L0_attn_w_out', 'L0_attn_b_out', 'L0_xattn_gamma', 'L0_xattn_beta',
        'L0_ffn_w1', 'L0_ffn_b1', 'L0_ffn_w2', 'L0_ffn_b2', 'L1_attn_W_in', 'L1_attn_W_delta',
        'L1_attn_b_delta', 'L1_attn_W_B', 'L1_attn_W_C', 'L1_attn_A_log', 'L1_attn_D_param',
        'L1_attn_W_out', 'L1_xattn_Wq', 'L1_xattn_Wk', 'L1_xattn_Wv', 'L1_xattn_Wo', 'L1_xattn_bo',
        'L1_xattn_gq', 'L1_xattn_gk', 'L1_ffn_w_q', 'L1_ffn_keys', 'L1_ffn_expert_down',
        'L1_ffn_expert_up', 'L1_ffn_norm_w']


def kernel(**inputs):
    import numpy as _np
    import concourse.bacc as _bacc
    from concourse import mybir as _mybir
    from concourse.bass_utils import run_bass_kernel_spmd as _run

    nc = _bacc.Bacc("TRN2", target_bir_lowering=False, num_devices=1)
    arrays, args = {}, []
    for name in _INS:
        a = _np.ascontiguousarray(inputs[name])
        arrays[f"in_{name}_dram"] = a
        args.append(nc.dram_tensor(f"in_{name}_dram", a.shape, _mybir.dt.from_np(a.dtype), kind="ExternalInput").ap())
    args.append(nc.dram_tensor("out_0_dram", inputs["x"].shape, F32, kind="ExternalOutput").ap())
    decoder(nc, *args)
    r = _run(nc, [arrays], core_ids=[0])
    return r.results[0]["out_0_dram"]
```
